# Optimizing a Trainium2 kernel written in Bass

```python
import numpy as np
import jax
import jax.numpy as jnp

def _softmax(x, axis=-1):
    return jax.nn.softmax(x, axis=axis)

def _gelu(x):
    return jax.nn.gelu(x, approximate=True)

def _silu(x):
    return jax.nn.silu(x)

def _sigmoid(x):
    return jax.nn.sigmoid(x)

def _layernorm(x, axis=-1, eps=1e-05):
    m = jnp.mean(x, axis=axis, keepdims=True)
    v = jnp.var(x, axis=axis, keepdims=True)
    return (x - m) / jnp.sqrt(v + eps)

def _scatter_add(tgt, idx, src, axis=0):
    return tgt.at[idx].add(src)

def _segment_sum(src, seg, n):
    return jax.ops.segment_sum(src, seg, n)
kernel_name = 'mk_adaln_d2_jaxref_r4_964598'

def setup_inputs(seed: int=0):
    np.random.seed(seed)
    _w = jnp.asarray

    def _L0_attn_setup():
        import jax, jax.numpy as jnp
        import numpy as np
        B, T, D = (8, 1024, 256)
        key = jax.random.key(seed)
        ks = jax.random.split(key, 7)
        s1 = 1.0 / np.sqrt(D)
        return {'x': jax.random.normal(ks[0], (B, T, D), dtype=jnp.float32), 'W1': jax.random.normal(ks[1], (D, D), dtype=jnp.float32) * s1, 'b1': jnp.zeros((D,), dtype=jnp.float32), 'w2': jax.random.normal(ks[2], (1, D), dtype=jnp.float32) * s1, 'b2': jnp.zeros((1,), dtype=jnp.float32), 'Wc': jax.random.normal(ks[3], (D, 2 * D), dtype=jnp.float32) * (1.0 / np.sqrt(2 * D)), 'bc': jnp.zeros((D,), dtype=jnp.float32)}
    _L0_attn_in = _L0_attn_setup()

    def _L0_ffn_setup():
        import jax, jax.numpy as jnp
        import numpy as np
        E = 8
        TOPK = 2
        SCALE = 2.0
        key = jax.random.key(seed)
        ks = jax.random.split(key, 12)
        B, S, D, F, R = (2, 128, 256, 1024, 16)
        w = lambda k, shp: jax.random.normal(k, shp, dtype=jnp.float32) * 0.02
        return {'hidden_states': jax.random.normal(ks[0], (B, S, D), dtype=jnp.float32), 'gate_w': w(ks[1], (E, D)), 'w_gate': w(ks[2], (F, D)), 'w_up': w(ks[3], (F, D)), 'w_down': w(ks[4], (D, F)), 'A1': w(ks[5], (E, R, D)), 'B1': w(ks[6], (E, F, R)), 'A3': w(ks[7], (E, R, D)), 'B3': w(ks[8], (E, F, R)), 'A2': w(ks[9], (E, R, F)), 'B2': w(ks[10], (E, D, R))}
    _L0_ffn_in = _L0_ffn_setup()
    _L0_c = _w((lambda *s: np.random.randn(*s).astype(np.float32) * 0.05)(16, 256))
    _L0_wmod = _w((lambda *s: np.random.randn(*s).astype(np.float32) * 0.05)(256, 6 * 256) * 256 ** (-0.5))

    def _L1_attn_setup():
        import jax, jax.numpy as jnp
        import numpy as np
        B, N, C, H = (4, 1024, 256, 16)
        EPS = 1e-06
        key = jax.random.key(seed)
        k1, k2, k3 = jax.random.split(key, 3)
        x = jax.random.normal(k1, (B, N, C), dtype=jnp.float32)
        qkv_w = jax.random.normal(k2, (3 * C, C), dtype=jnp.float32) * 0.02
        qkv_b = jnp.zeros((3 * C,), dtype=jnp.float32)
        proj_w = jax.random.normal(k3, (C, C), dtype=jnp.float32) * 0.02
        proj_b = jnp.zeros((C,), dtype=jnp.float32)
        return {'x': x, 'qkv_w': qkv_w, 'qkv_b': qkv_b, 'proj_w': proj_w, 'proj_b': proj_b}
    _L1_attn_in = _L1_attn_setup()

    def _L1_ffn_setup():
        import jax, jax.numpy as jnp
        import numpy as np
        DIM = 256

        def _reference_tuple_inner(x, W_r, W_k, W_v, mu_r, mu_k):
            B, T, C = x.shape
            x_prev = jnp.concatenate([jnp.zeros((B, 1, C), x.dtype), x[:, :-1, :]], axis=1)
            xr = mu_r * x + (1.0 - mu_r) * x_prev
            xk = mu_k * x + (1.0 - mu_k) * x_prev
            r = jax.nn.sigmoid(jnp.einsum('btc,dc->btd', xr, W_r))
            k = jnp.einsum('btc,dc->btd', xk, W_k)
            k_act = jnp.square(jax.nn.relu(k))
            out = r * jnp.einsum('btc,dc->btd', k_act, W_v)
            new_state = x[:, -1, :]
            return (out, new_state)
        key = jax.random.key(seed)
        ks = jax.random.split(key, 6)
        B, T, C = (8, 512, DIM)
        x = jax.random.normal(ks[0], (B, T, C), dtype=jnp.float32)
        s = 1.0 / np.sqrt(C)
        W_r = jax.random.uniform(ks[1], (C, C), jnp.float32, -s, s)
        W_k = jax.random.uniform(ks[2], (C, C), jnp.float32, -s, s)
        W_v = jax.random.uniform(ks[3], (C, C), jnp.float32, -s, s)
        mu_r = jax.random.uniform(ks[4], (C,), jnp.float32)
        mu_k = jax.random.uniform(ks[5], (C,), jnp.float32)
        return {'x': x, 'W_r': W_r, 'W_k': W_k, 'W_v': W_v, 'mu_r': mu_r, 'mu_k': mu_k}
    _L1_ffn_in = _L1_ffn_setup()
    _L1_c = _w((lambda *s: np.random.randn(*s).astype(np.float32) * 0.05)(16, 256))
    _L1_wmod = _w((lambda *s: np.random.randn(*s).astype(np.float32) * 0.05)(256, 6 * 256) * 256 ** (-0.5))
    _d = {'L0_attn_x': _L0_attn_in['x'], 'L0_attn_W1': _L0_attn_in['W1'], 'L0_attn_b1': _L0_attn_in['b1'], 'L0_attn_w2': _L0_attn_in['w2'], 'L0_attn_b2': _L0_attn_in['b2'], 'L0_attn_Wc': _L0_attn_in['Wc'], 'L0_attn_bc': _L0_attn_in['bc'], 'L0_ffn_gate_w': _L0_ffn_in['gate_w'], 'L0_ffn_w_gate': _L0_ffn_in['w_gate'], 'L0_ffn_w_up': _L0_ffn_in['w_up'], 'L0_ffn_w_down': _L0_ffn_in['w_down'], 'L0_ffn_A1': _L0_ffn_in['A1'], 'L0_ffn_B1': _L0_ffn_in['B1'], 'L0_ffn_A3': _L0_ffn_in['A3'], 'L0_ffn_B3': _L0_ffn_in['B3'], 'L0_ffn_A2': _L0_ffn_in['A2'], 'L0_ffn_B2': _L0_ffn_in['B2'], 'L0_c': _L0_c, 'L0_wmod': _L0_wmod, 'L1_attn_qkv_w': _L1_attn_in['qkv_w'], 'L1_attn_qkv_b': _L1_attn_in['qkv_b'], 'L1_attn_proj_w': _L1_attn_in['proj_w'], 'L1_attn_proj_b': _L1_attn_in['proj_b'], 'L1_ffn_W_r': _L1_ffn_in['W_r'], 'L1_ffn_W_k': _L1_ffn_in['W_k'], 'L1_ffn_W_v': _L1_ffn_in['W_v'], 'L1_ffn_mu_r': _L1_ffn_in['mu_r'], 'L1_ffn_mu_k': _L1_ffn_in['mu_k'], 'L1_c': _L1_c, 'L1_wmod': _L1_wmod}
    _x0 = _d['L0_attn_x']
    _d['L0_attn_x'] = jax.random.normal(jax.random.fold_in(jax.random.key(seed), 1), (16, 512, 256), dtype=_x0.dtype)
    del _x0
    return _d

def reference(L0_attn_x, L0_attn_W1, L0_attn_b1, L0_attn_w2, L0_attn_b2, L0_attn_Wc, L0_attn_bc, L0_ffn_gate_w, L0_ffn_w_gate, L0_ffn_w_up, L0_ffn_w_down, L0_ffn_A1, L0_ffn_B1, L0_ffn_A3, L0_ffn_B3, L0_ffn_A2, L0_ffn_B2, L0_c, L0_wmod, L1_attn_qkv_w, L1_attn_qkv_b, L1_attn_proj_w, L1_attn_proj_b, L1_ffn_W_r, L1_ffn_W_k, L1_ffn_W_v, L1_ffn_mu_r, L1_ffn_mu_k, L1_c, L1_wmod):

    def _L0_attn_ref(x, W1, b1, w2, b2, Wc, bc):
        import jax, jax.numpy as jnp
        import numpy as np
        B, T, D = (8, 1024, 256)
        h = jnp.tanh(jnp.einsum('btd,ed->bte', x, W1) + b1)
        s = (jnp.einsum('btd,od->bto', h, w2) + b2)[..., 0]
        m = jnp.max(s, axis=1, keepdims=True)
        e = jnp.exp(s - m)
        num = jnp.cumsum(e[..., None] * x, axis=1)
        den = jnp.cumsum(e, axis=1)[..., None]
        ctx = num / den
        combined = jnp.concatenate((ctx, x), axis=2)
        out = jnp.tanh(jnp.einsum('btk,dk->btd', combined, Wc) + bc)
        return out

    def _L0_ffn_ref(hidden_states, gate_w, w_gate, w_up, w_down, A1, B1, A3, B3, A2, B2):
        import jax, jax.numpy as jnp
        import numpy as np
        E = 8
        TOPK = 2
        SCALE = 2.0
        B, S, D = hidden_states.shape
        x = hidden_states.reshape(-1, D)
        N = x.shape[0]
        probs = jax.nn.softmax(x @ gate_w.T, axis=-1)
        vals, idx = jax.lax.top_k(probs, TOPK)
        rw = vals / jnp.sum(vals, axis=-1, keepdims=True)
        weight = jnp.zeros((N, E), x.dtype).at[jnp.arange(N)[:, None], idx].add(rw)
        common_w1 = x @ w_gate.T
        common_w3 = x @ w_up.T
        d1 = jnp.einsum('enr,efr->enf', jnp.einsum('nd,erd->enr', x, A1), B1) * SCALE
        d3 = jnp.einsum('enr,efr->enf', jnp.einsum('nd,erd->enr', x, A3), B3) * SCALE
        act = jax.nn.silu(common_w1[None] + d1) * (common_w3[None] + d3)
        out = jnp.einsum('ne,enf->nf', weight, act) @ w_down.T
        z = jnp.einsum('enf,erf->enr', act, A2)
        out = out + jnp.einsum('ne,enr,edr->nd', weight, z, B2) * SCALE
        return out.reshape(B, S, D)

    def _L1_attn_ref(x, qkv_w, qkv_b, proj_w, proj_b):
        import jax, jax.numpy as jnp
        import numpy as np
        B, N, C, H = (4, 1024, 256, 16)
        EPS = 1e-06
        b, n, c = x.shape
        d = c // H
        qkv = x @ qkv_w.T + qkv_b
        qkv = qkv.reshape(b, n, 3, H, d).transpose(2, 0, 3, 1, 4)
        q, k, v = (qkv[0], qkv[1], qkv[2])
        q = jax.nn.sigmoid(q)
        k = jax.nn.sigmoid(k)
        k_sum = k.sum(axis=2)
        sink_incoming = 1.0 / jnp.sum((q + EPS) * (k_sum[:, :, None, :] + EPS), axis=-1)
        q_sum = q.sum(axis=2)
        source_outgoing = 1.0 / jnp.sum((k + EPS) * (q_sum[:, :, None, :] + EPS), axis=-1)
        k_so_sum = (k * source_outgoing[..., None]).sum(axis=2, keepdims=True)
        conserved_sink = jnp.sum((q + EPS) * (k_so_sum + EPS), axis=-1) + EPS
        q_si_sum = (q * sink_incoming[..., None]).sum(axis=2, keepdims=True)
        conserved_source = jnp.sum((k + EPS) * (q_si_sum + EPS), axis=-1) + EPS
        conserved_source = jnp.clip(conserved_source, -1.0, 1.0)
        ratio = float(n) / float(n)
        sink_allocation = jax.nn.sigmoid(conserved_sink * ratio)
        source_competition = jax.nn.softmax(conserved_source, axis=-1) * float(n)
        q_norm = q * sink_incoming[..., None]
        v_comp = v * source_competition[..., None]
        kv = jnp.einsum('bhnd,bhnm->bhdm', k, v_comp)
        out = jnp.einsum('bhnd,bhdm->bhnm', q_norm, kv)
        out = out * sink_allocation[..., None]
        out = out.transpose(0, 2, 1, 3).reshape(b, n, c)
        out = out @ proj_w.T + proj_b
        return out

    def _L1_ffn_ref(x, W_r, W_k, W_v, mu_r, mu_k):
        import jax, jax.numpy as jnp
        import numpy as np
        DIM = 256

        def _reference_tuple_inner(x, W_r, W_k, W_v, mu_r, mu_k):
            B, T, C = x.shape
            x_prev = jnp.concatenate([jnp.zeros((B, 1, C), x.dtype), x[:, :-1, :]], axis=1)
            xr = mu_r * x + (1.0 - mu_r) * x_prev
            xk = mu_k * x + (1.0 - mu_k) * x_prev
            r = jax.nn.sigmoid(jnp.einsum('btc,dc->btd', xr, W_r))
            k = jnp.einsum('btc,dc->btd', xk, W_k)
            k_act = jnp.square(jax.nn.relu(k))
            out = r * jnp.einsum('btc,dc->btd', k_act, W_v)
            new_state = x[:, -1, :]
            return (out, new_state)
        return _reference_tuple_inner(x, W_r, W_k, W_v, mu_r, mu_k)[0]
    x = L0_attn_x
    mod = (_silu(L0_c) @ L0_wmod).reshape(L0_c.shape[0], 6, 1, -1)
    sa, ca, ga, sb, cb, gb = (mod[:, 0], mod[:, 1], mod[:, 2], mod[:, 3], mod[:, 4], mod[:, 5])
    ga = (2 * (ga >= 0) - 1) * jnp.maximum(jnp.abs(ga), 0.25)
    gb = (2 * (gb >= 0) - 1) * jnp.maximum(jnp.abs(gb), 0.25)
    h = _layernorm(x, axis=-1) * (1 + ca) + sa
    x = x + ga * _L0_attn_ref(h, L0_attn_W1, L0_attn_b1, L0_attn_w2, L0_attn_b2, L0_attn_Wc, L0_attn_bc)
    h = _layernorm(x, axis=-1) * (1 + cb) + sb
    x = x + gb * _L0_ffn_ref(h, L0_ffn_gate_w, L0_ffn_w_gate, L0_ffn_w_up, L0_ffn_w_down, L0_ffn_A1, L0_ffn_B1, L0_ffn_A3, L0_ffn_B3, L0_ffn_A2, L0_ffn_B2)
    mod = (_silu(L1_c) @ L1_wmod).reshape(L1_c.shape[0], 6, 1, -1)
    sa, ca, ga, sb, cb, gb = (mod[:, 0], mod[:, 1], mod[:, 2], mod[:, 3], mod[:, 4], mod[:, 5])
    ga = (2 * (ga >= 0) - 1) * jnp.maximum(jnp.abs(ga), 0.25)
    gb = (2 * (gb >= 0) - 1) * jnp.maximum(jnp.abs(gb), 0.25)
    h = _layernorm(x, axis=-1) * (1 + ca) + sa
    x = x + ga * _L1_attn_ref(h, L1_attn_qkv_w, L1_attn_qkv_b, L1_attn_proj_w, L1_attn_proj_b)
    h = _layernorm(x, axis=-1) * (1 + cb) + sb
    x = x + gb * _L1_ffn_ref(h, L1_ffn_W_r, L1_ffn_W_k, L1_ffn_W_v, L1_ffn_mu_r, L1_ffn_mu_k)
    return x

_drawn_inputs = setup_inputs


def setup_inputs(seed=0):
    import zlib

    import numpy as np

    out = dict(_drawn_inputs(seed))
    spreads = {'L0_attn_b1': (0.0, 0.8),
     'L0_attn_bc': (0.0, 0.427),
     'L1_attn_qkv_b': (0.0, 2.0),
     'L1_attn_proj_b': (0.0, 2.0)}
    factors = {'L0_attn_W1': 5.367,
     'L0_attn_w2': 5.351,
     'L0_ffn_gate_w': 8.0,
     'L0_ffn_w_gate': 6.752,
     'L0_ffn_w_up': 6.683,
     'L0_ffn_w_down': 6.679,
     'L0_ffn_A1': 8.0,
     'L0_ffn_B1': 8.0,
     'L0_ffn_A3': 8.0,
     'L0_ffn_B3': 8.0,
     'L0_ffn_A2': 8.0,
     'L0_ffn_B2': 8.0,
     'L1_attn_qkv_w': 64.0,
     'L1_attn_proj_w': 8.0,
     'L1_ffn_W_r': 8.0,
     'L1_ffn_W_k': 3.046,
     'L1_ffn_W_v': 2.79,
     'L1_ffn_mu_r': 8.0,
     'L1_ffn_mu_k': 5.052}
    for name, (base, spread) in spreads.items():
        noise = np.random.default_rng([zlib.crc32(name.encode()), seed]).standard_normal(out[name].shape)
        drawn = base * np.exp(spread * noise) if base else spread * noise
        out[name] = jnp.asarray(drawn.astype(out[name].dtype))
    for name, factor in factors.items():
        out[name] = (out[name] * factor).astype(out[name].dtype)
    return out
```

```python
from contextlib import ExitStack

import numpy as np
import concourse.bass as bass
from concourse import mybir

F32 = mybir.dt.float32
F32R = mybir.dt.float32r
BF16 = mybir.dt.bfloat16
U32 = mybir.dt.uint32
ACT = mybir.ActivationFunctionType
ALU = mybir.AluOpType
AX = mybir.AxisListType

P = 128
NS = 16
T = 512
D = 256
KT = D // P
TT = T // P
E = 8
R = 16
F = 1024
FT = F // P
H = 16
HD = D // H
HG = P // HD
LN_EPS = 1e-5
EPS = 1e-6
SCALE = 2.0
GATE_MIN = 0.25

SA, CA, GA, SB, CB, GB = range(6)


def bc(ap, shape):
    return ap.to_broadcast(shape)


def wait_reuse(engine, sem, n):
    if not isinstance(n, int) or n > 0:
        engine.wait_ge(sem, n)


def mm3(pe, out, w_hi, w_lo, x_hi, x_lo, start, stop):
    pe.matmul(out, w_hi, x_hi, start=start, stop=False)
    pe.matmul(out, w_hi, x_lo, start=False, stop=False)
    return pe.matmul(out, w_lo, x_hi, start=False, stop=stop)


class Norm:

    def __init__(self, sb, sem):
        self.sq = sb("ln_sq", [P, KT, T], F32)
        self.xs = sb("ln_xs", [P, 2, T], F32)
        self.stat = sb("ln_stat", [P, 2, TT], F32)
        self.mm = sb("ln_mm", [P, TT], F32)
        self.var = sb("ln_var", [P, TT], F32)
        self.rstd = sb("ln_rstd", [P, 2, TT], F32)
        self.hx = sb("ln_hx", [P, KT, T], F32)
        self.s_sq = sem("ln_sq_ready")
        self.s_xs = sem("ln_xs_ready")
        self.s_qs = sem("ln_qs_ready")
        self.s_sums = sem("ln_sums_ready")
        self.s_mean = sem("ln_mean_ready")
        self.s_mm = sem("ln_mm_ready")
        self.s_var = sem("ln_var_ready")
        self.s_rstd = sem("ln_rstd_ready")
        self.s_nmr = sem("ln_nmr_ready")
        self.s_bc = sem("ln_spread_ready")
        self.s_mul = sem("ln_mul_ready")
        self.s_add = sem("ln_add_ready")


def norm_square(act, ln, n, x):
    wait_reuse(act, ln.s_qs, n)
    act.activation(ln.sq[:, :, :], x, ACT.Square).then_inc(ln.s_sq, 1)


def norm_presum(pool, ln, n, x):
    wait_reuse(pool, ln.s_sums, n)
    pool.tensor_tensor(ln.xs[:, 0, :], x[:, 0, :], x[:, 1, :], ALU.add).then_inc(ln.s_xs, 1)


def norm_sums(pe, ln, n, bank, ones):
    pe.wait_ge(ln.s_xs, n + 1)
    pe.wait_ge(ln.s_qs, n + 1)
    for j in range(2):
        for t in range(TT):
            c = j * TT + t
            mm = pe.matmul(bank[:, c:c + 1], ln.xs[:, j, t * P:(t + 1) * P], ones[:, 0:1], start=True, stop=True)
    mm.then_inc(ln.s_sums, 1)


def norm_stats_a(dve, ln, n, bank):
    dve.wait_ge(ln.s_sq, n + 1)
    wait_reuse(dve, ln.s_sums, n)
    dve.tensor_tensor(ln.xs[:, 1, :], ln.sq[:, 0, :], ln.sq[:, 1, :], ALU.add).then_inc(ln.s_qs, 1)
    dve.wait_ge(ln.s_sums, n + 1)
    dve.tensor_scalar(ln.stat[:, :, :].rearrange("p a t -> p (a t)"), bank[:, 0:2 * TT], 1.0 / D, None,
                      ALU.mult).then_inc(ln.s_mean, 1)
    dve.wait_ge(ln.s_mean, n + 1)
    dve.tensor_tensor(ln.mm[:, :], ln.stat[:, 0, :], ln.stat[:, 0, :], ALU.mult).then_inc(ln.s_mm, 1)
    dve.wait_ge(ln.s_mm, n + 1)
    dve.scalar_tensor_tensor(out=ln.var[:, :], in0=ln.stat[:, 1, :], scalar=LN_EPS, in1=ln.mm[:, :],
                             op0=ALU.add, op1=ALU.subtract).then_inc(ln.s_var, 1)


def norm_rstd(pool, ln, n, minus_half):
    pool.wait_ge(ln.s_var, n + 1)
    pool.tensor_tensor(ln.rstd[:, 0, :], ln.var[:, :], minus_half, ALU.pow).then_inc(ln.s_rstd, 1)


def norm_stats_b(dve, ln, n):
    dve.wait_ge(ln.s_rstd, n + 1)
    dve.scalar_tensor_tensor(out=ln.rstd[:, 1, :], in0=ln.stat[:, 0, :], scalar=-1.0, in1=ln.rstd[:, 0, :],
                             op0=ALU.mult, op1=ALU.mult).then_inc(ln.s_nmr, 1)


def norm_spread(pe, ln, n, banks, ident):
    pe.wait_ge(ln.s_rstd, n + 1)
    pe.wait_ge(ln.s_nmr, n + 1)
    for j in range(2):
        for t in range(TT):
            mm = pe.transpose(banks[j][:, t * P:(t + 1) * P], bc(ln.rstd[:, j, t:t + 1], [P, P]), ident)
    mm.then_inc(ln.s_bc, 1)


def norm_apply(dve, ln, n, x, banks):
    dve.wait_ge(ln.s_bc, n + 1)
    for k in range(KT):
        mul = dve.tensor_tensor(ln.hx[:, k, :], x[:, k, :], banks[0][:, :], ALU.mult)
    mul.then_inc(ln.s_mul, 1)
    dve.wait_ge(ln.s_mul, n + 1)
    for k in range(KT):
        add = dve.tensor_tensor(ln.hx[:, k, :], ln.hx[:, k, :], banks[1][:, :], ALU.add)
    add.then_inc(ln.s_add, 1)


def first_layer(nc, sems, x_in, mid, w, mod, const):
    ident, ident16, ones, minus_half = const
    with ExitStack() as ctx:
        def sb(name, shape, dt=F32):
            return ctx.enter_context(nc.sbuf_tensor("a_" + name, shape, dt))

        def sem(name):
            sems.append(nc.alloc_semaphore("a_" + name))
            return sems[-1]

        gate_ps, up_ps, out_ps0, out_ps1, z_ps0, z_ps1, fr0, fr1 = [
            ctx.enter_context(nc.psum_tensor(f"a_bank{i}", [P, T], F32)) for i in range(8)]
        out_ps, z_ps, fr = (out_ps0, out_ps1), (z_ps0, z_ps1), (fr0, fr1)

        shapes = {"W1": KT * D, "Wc": 2 * KT * D, "A1": KT * P, "A3": KT * P, "Wg": KT * F, "Wu": KT * F,
                  "B1": F, "B3": F, "A2": FT * P, "Wd": FT * D, "B2": D}
        chunks = [(name, c, min(c + 1024, n)) for name, n in shapes.items() for c in range(0, n, 1024)]
        hi = {name: sb(name + "_hi", [P, n], F32R) for name, n in shapes.items()}
        lo = {name: sb(name + "_lo", [P, n], F32R) for name, n in shapes.items()}

        def wt(name, width, k, m, cols=P):
            a = k * width + m * P
            return hi[name][:, a:a + cols], lo[name][:, a:a + cols]

        gw = sb("gate_w", [P, KT, E])
        b1 = sb("b1", [P, KT])
        bcv = sb("bc", [P, KT])
        w2 = sb("w2", [P, KT])
        b2 = sb("b2", [P, 1])
        b2p = sb("b2_part", [P, 1])
        cur = sb("mod_now", [P, 6 * KT])
        iota = sb("expert_no", [P, TT, E])

        ln = Norm(sb, sem)
        x = sb("x", [P, KT, T])
        h = sb("h", [P, KT, T])
        hh = sb("h_hi", [P, KT, T], F32R)
        hl = sb("h_lo", [P, KT, T], F32R)
        th = sb("tanh", [P, KT, T])
        sp = sb("score_part", [P, T])
        nmx = sb("score_max_neg", [P, 1])
        ex = sb("exp", [P, T])
        den = sb("den", [P, T])
        ch = sb("ctx_hi", [P, KT, T], F32R)
        cl = sb("ctx_lo", [P, KT, T], F32R)
        lg = sb("logits", [P, TT, E])
        top = sb("top_values", [P, TT, E])
        topi = sb("top_index", [P, TT, E], U32)
        topf = sb("top_index_f", [P, TT, 2])
        hot = sb("one_hot", [P, 2, TT, E])
        sel = sb("masks", [P, 3, TT, E * R], BF16)
        dl = sb("logit_gap", [P, TT])
        eg = sb("gap_exp", [P, TT])
        rw = sb("route_w", [P, 2, TT])
        selb = sb("masks_spread", [P, 3, T], BF16)
        rwb = sb("route_w_spread", [P, 2, T])
        um = sb("u_masked", [P, 4, T])
        uh = sb("u_hi", [P, 4, T], F32R)
        ul = sb("u_lo", [P, 4, T], F32R)
        sg = sb("silu", [P, 2, T])
        ah = sb("act_hi", [P, 2, T], F32R)
        al = sb("act_lo", [P, 2, T], F32R)
        cb = sb("act_sum", [P, T])
        cbh = sb("act_sum_hi", [P, T], F32R)
        cbl = sb("act_sum_lo", [P, T], F32R)
        dummy = sb("dummy", [P, 1])
        stage = [um[:, 0:2, :].rearrange("p a t -> p (a t)"), um[:, 2:4, :].rearrange("p a t -> p (a t)"),
                 h[:, :, :].rearrange("p a t -> p (a t)"), th[:, :, :].rearrange("p a t -> p (a t)")]

        names = ("w_loaded w_hi w_lo vec iota b2p x_in cur h_ready hh hl w1 tanh part score smax exp den prod scan "
                 "rden ctx ctxh ctxl wc tanh2 attn logits lgc settle top topi topf hot sel dif gap gapexp "
                 "gap1 rw0 rw1 spread spreadc u umul umh uml gate up silu sw aw awh awl comb combh combl "
                 "down zdone z0m z1m zsum zh zl out y stored").split()
        s = {n: sem(n + "_s") for n in names}
        block = ctx.enter_context(nc.Block())

        @block.sync
        def _(sp_):
            for dst, src in ((gw, w["gate_w"]), (b1, w["b1"]), (bcv, w["bc"]), (w2, w["w2"]), (b2, w["b2"])):
                sp_.dma_start(dst[tuple(slice(None) for _ in dst.shape)], src).then_inc(s["vec"], 16)
            for n, (name, a, b) in enumerate(chunks):
                if n >= len(stage):
                    sp_.wait_ge(s["w_lo"], n - len(stage) + 1)
                sp_.dma_start(stage[n % len(stage)][:, 0:b - a], w[name][:, a:b]).then_inc(s["w_loaded"], 16)
                sp_.wait_ge(s["w_loaded"], 16 * (n + 1))

        @block.scalar
        def _(act):
            for n, (name, a, b) in enumerate(chunks):
                act.wait_ge(s["w_loaded"], 16 * (n + 1))
                act.copy(hi[name][:, a:b], stage[n % len(stage)][:, 0:b - a]).then_inc(s["w_hi"], 1)

            def body(i):
                wait_reuse(act, s["y"], i * KT)
                wait_reuse(act, s["stored"], i * 16)
                act.dma_start(x[:, :, :], x_in[bass.ds(i, 1)].rearrange("a p k t -> p (a k) t")).then_inc(s["x_in"], 16)

                def norm(which, c, sh):
                    n = i * 2 + which
                    if which == 0:
                        act.wait_ge(s["x_in"], i * 16 + 16)
                    else:
                        act.wait_ge(s["attn"], i * KT + KT)
                    norm_square(act, ln, n, x[:, :, :])
                    act.wait_ge(ln.s_add, n + 1)
                    act.wait_ge(s["cur"], i * 2 + 2)
                    if which == 0:
                        wait_reuse(act, s["zdone"], i)
                    for k in range(KT):
                        act.activation(h[:, k, :], ln.hx[:, k, :], ACT.Identity, bias=cur[:, sh * KT + k:sh * KT + k + 1],
                                       scale=cur[:, c * KT + k:c * KT + k + 1]).then_inc(s["h_ready"], 1)
                    for k in range(KT):
                        act.activation(hh[:, k, :], ln.hx[:, k, :], ACT.Identity, bias=cur[:, sh * KT + k:sh * KT + k + 1],
                                       scale=cur[:, c * KT + k:c * KT + k + 1]).then_inc(s["hh"], 1)

                norm(0, CA, SA)
                for m in range(KT):
                    act.wait_ge(s["w1"], i * KT + m + 1)
                    act.activation(th[:, m, :], fr[m][:, :], ACT.Tanh, bias=b1[:, m:m + 1]).then_inc(s["tanh"], 1)
                act.wait_ge(s["smax"], i + 1)
                act.activation(ex[:, :], fr0[:, :], ACT.Exp, bias=nmx[:, 0:1]).then_inc(s["exp"], 1)
                act.wait_ge(s["ctx"], i + 1)
                act.copy(ch[:, :, :], th[:, :, :]).then_inc(s["ctxh"], 1)
                act.wait_ge(s["ctxl"], i + 1)
                for m in range(KT):
                    act.wait_ge(s["wc"], i * KT + m + 1)
                    act.activation(th[:, m, :], fr[m][:, :], ACT.Tanh, bias=bcv[:, m:m + 1]).then_inc(s["tanh2"], 1)
                norm(1, CB, SB)
                act.wait_ge(s["gap"], i + 1)
                act.activation(eg[:, :], dl[:, :], ACT.Exp).then_inc(s["gapexp"], 1)
                for j in range(5):
                    act.wait_ge(s["spread"], i * 5 + j + 1)
                    dst = selb[:, j, :] if j < 3 else rwb[:, j - 3, :]
                    act.copy(dst, fr[j % 2][:, :]).then_inc(s["spreadc"], 1)
                for q in range(4):
                    act.wait_ge(s["umul"], i * 4 + q + 1)
                    act.copy(uh[:, q, :], um[:, q, :]).then_inc(s["umh"], 1)
                for f in range(FT):
                    for j in range(2):
                        n = i * 2 * FT + 2 * f + j
                        act.wait_ge(s["gate"], n + 1)
                        wait_reuse(act, s["awl"], n - 1 if f or j else i * 2 * FT)
                        wait_reuse(act, s["comb"], i * FT + f)
                        act.activation(sg[:, j, :], gate_ps[:, :], ACT.Silu).then_inc(s["silu"], 1)
                    for j in range(2):
                        n = i * 2 * FT + 2 * f + j
                        act.wait_ge(s["aw"], n + 1)
                        wait_reuse(act, s["down"], i * FT + f)
                        act.copy(ah[:, j, :], sg[:, j, :]).then_inc(s["awh"], 1)
                    act.wait_ge(s["comb"], i * FT + f + 1)
                    act.copy(cbh[:, :], cb[:, :]).then_inc(s["combh"], 1)
                act.wait_ge(s["zsum"], i + 1)
                act.wait_ge(s["down"], i * FT + FT)
                act.copy(cbh[:, :], cb[:, :]).then_inc(s["zh"], 1)
                act.wait_ge(s["y"], i * KT + KT)
                act.dma_start(mid[bass.ds(i, 1)].rearrange("a p k t -> p (a k) t"), x[:, :, :]).then_inc(s["stored"], 16)

            body(0)
            with act.Fori(1, NS) as i:
                body(i)
            act.wait_ge(s["stored"], 16 * NS)

        @block.gpsimd
        def _(pool):
            for e in range(E):
                pool.memset(iota[:, :, e:e + 1], float(e)).then_inc(s["iota"], 1)

            def body(i):
                pool.wait_ge(s["x_in"], i * 16 + 16)
                norm_presum(pool, ln, i * 2, x)
                norm_rstd(pool, ln, i * 2, minus_half)
                pool.wait_ge(s["attn"], i * KT + KT)
                norm_presum(pool, ln, i * 2 + 1, x)
                norm_rstd(pool, ln, i * 2 + 1, minus_half)
                for f in range(FT):
                    for j in range(2):
                        n = i * 2 * FT + 2 * f + j
                        pool.wait_ge(s["silu"], n + 1)
                        pool.wait_ge(s["spreadc"], i * 5 + 5)
                        pool.tensor_tensor(sg[:, j, :], sg[:, j, :], rwb[:, j, :], ALU.mult).then_inc(s["sw"], 1)
                    pool.wait_ge(s["aw"], i * 2 * FT + 2 * f + 2)
                    wait_reuse(pool, s["combl"], i * FT + f)
                    wait_reuse(pool, s["zl"], i)
                    pool.tensor_tensor(cb[:, :], sg[:, 0, :], sg[:, 1, :], ALU.add).then_inc(s["comb"], 1)

            body(0)
            with pool.Fori(1, NS) as i:
                body(i)

        @block.vector
        def _(dve):
            for n, (name, a, b) in enumerate(chunks):
                dve.wait_ge(s["w_hi"], n + 1)
                dve.tensor_tensor(lo[name][:, a:b], stage[n % len(stage)][:, 0:b - a], hi[name][:, a:b].bitcast(F32),
                                  ALU.subtract).then_inc(s["w_lo"], 1)
            dve.wait_ge(s["vec"], 16 * 5)
            dve.tensor_scalar(b2p[:, :], b2[:, :], 1.0 / P, None, ALU.mult).then_inc(s["b2p"], 1)
            dve.wait_ge(s["b2p"], 1)
            dve.wait_ge(s["iota"], E)

            def body(i):
                def norm(which):
                    n = i * 2 + which
                    norm_stats_a(dve, ln, n, fr0)
                    norm_stats_b(dve, ln, n)
                    norm_apply(dve, ln, n, x, fr)
                    dve.wait_ge(s["hh"], n * KT + KT)
                    dve.wait_ge(s["h_ready"], n * KT + KT)
                    dve.tensor_tensor(hl[:, :, :], h[:, :, :], hh[:, :, :].bitcast(F32), ALU.subtract).then_inc(s["hl"], 1)

                wait_reuse(dve, s["y"], i * KT)
                dve.tensor_copy(cur[:, :], mod[:, bass.ds(i, 1), :].rearrange("p a c -> p (a c)")).then_inc(s["cur"], 1)
                dve.wait_ge(s["cur"], i * 2 + 1)
                dve.tensor_copy(dummy[:, :], cur[:, 0:1]).then_inc(s["cur"], 1)
                dve.wait_ge(s["x_in"], i * 16 + 16)
                norm(0)
                dve.wait_ge(s["tanh"], i * KT + KT)
                dve.tensor_scalar(sp[:, :], th[:, 0, :], w2[:, 0:1], b2p[:, 0:1], ALU.mult, ALU.add).then_inc(s["part"], 1)
                dve.wait_ge(s["part"], i * 2 + 1)
                dve.scalar_tensor_tensor(out=sp[:, :], in0=th[:, 1, :], scalar=w2[:, 1:2], in1=sp[:, :], op0=ALU.mult,
                                         op1=ALU.add).then_inc(s["part"], 1)
                dve.wait_ge(s["score"], i + 1)
                dve.tensor_reduce(nmx[:, :], fr0[:, :], AX.X, ALU.max, negate=True).then_inc(s["smax"], 1)
                dve.wait_ge(s["exp"], i + 1)
                dve.tensor_tensor_scan(den[:, :], ex[:, :], ex[:, :], 0.0, ALU.add, ALU.bypass).then_inc(s["den"], 1)
                for k in range(KT):
                    prod = dve.tensor_tensor(ln.hx[:, k, :], h[:, k, :], ex[:, :], ALU.mult)
                prod.then_inc(s["prod"], 1)
                dve.wait_ge(s["den"], i + 1)
                dve.reciprocal(den[:, :], den[:, :]).then_inc(s["rden"], 1)
                dve.wait_ge(s["prod"], i + 1)
                for k in range(KT):
                    scan = dve.tensor_tensor_scan(th[:, k, :], ln.hx[:, k, :], ln.hx[:, k, :], 0.0, ALU.add, ALU.bypass)
                scan.then_inc(s["scan"], 1)
                dve.wait_ge(s["rden"], i + 1)
                dve.wait_ge(s["scan"], i + 1)
                for k in range(KT):
                    c = dve.tensor_tensor(th[:, k, :], th[:, k, :], den[:, :], ALU.mult)
                c.then_inc(s["ctx"], 1)
                dve.wait_ge(s["ctx"], i + 1)
                dve.wait_ge(s["ctxh"], i + 1)
                dve.tensor_tensor(cl[:, :, :], th[:, :, :], ch[:, :, :].bitcast(F32), ALU.subtract).then_inc(s["ctxl"], 1)
                for m in range(KT):
                    dve.wait_ge(s["tanh2"], i * KT + m + 1)
                    dve.scalar_tensor_tensor(out=x[:, m, :], in0=th[:, m, :], scalar=cur[:, GA * KT + m:GA * KT + m + 1],
                                             in1=x[:, m, :], op0=ALU.mult, op1=ALU.add).then_inc(s["attn"], 1)
                dve.wait_ge(s["attn"], i * KT + KT)
                norm(1)
                dve.wait_ge(s["logits"], i + 1)
                dve.tensor_copy(lg[:, :, :].rearrange("p t e -> p (t e)"), fr0[:, 0:TT * E]).then_inc(s["lgc"], 1)
                dve.wait_ge(s["lgc"], i + 1)
                dve.tensor_copy(dummy[:, :], lg[:, 0, 0:1]).then_inc(s["settle"], 1)
                for t in range(TT):
                    mx = dve.max(top[:, t, :], lg[:, t, :])
                mx.then_inc(s["top"], 1)
                dve.wait_ge(s["settle"], i * 2 + 1)
                dve.wait_ge(s["top"], i + 1)
                dve.tensor_copy(dummy[:, :], top[:, 0, 0:1]).then_inc(s["settle"], 1)
                for t in range(TT):
                    mx = dve.max_index(topi[:, t, :], top[:, t, :], lg[:, t, :])
                mx.then_inc(s["topi"], 1)
                dve.tensor_tensor(dl[:, :], top[:, :, 1], top[:, :, 0], ALU.subtract).then_inc(s["gap"], 1)
                dve.wait_ge(s["settle"], i * 2 + 2)
                dve.wait_ge(s["topi"], i + 1)
                dve.tensor_copy(topf[:, :, :], topi[:, :, 0:2]).then_inc(s["topf"], 1)
                dve.wait_ge(s["topf"], i + 1)
                for j in range(2):
                    hot_ = dve.tensor_tensor(hot[:, j, :, :], iota[:, :, :], bc(topf[:, :, j:j + 1], [P, TT, E]), ALU.is_equal)
                hot_.then_inc(s["hot"], 1)
                dve.wait_ge(s["hot"], i + 1)
                dve.tensor_scalar(sel[:, 0:2, :, :].rearrange("p a t (e r) -> p (a t e) r", r=R),
                                  bc(hot[:, :, :, :].rearrange("p a t e -> p (a t e)").unsqueeze(2), [P, 2 * TT * E, R]),
                                  SCALE, None, ALU.mult).then_inc(s["sel"], 1)
                dve.wait_ge(s["sel"], i + 1)
                dve.tensor_tensor(sel[:, 2, :, :], sel[:, 1, :, :], sel[:, 0, :, :], ALU.subtract).then_inc(s["dif"], 1)
                dve.wait_ge(s["gapexp"], i + 1)
                dve.tensor_scalar(dl[:, :], eg[:, :], 1.0, None, ALU.add).then_inc(s["gap1"], 1)
                dve.wait_ge(s["gap1"], i + 1)
                dve.reciprocal(rw[:, 0, :], dl[:, :]).then_inc(s["rw0"], 1)
                dve.wait_ge(s["rw0"], i + 1)
                dve.tensor_tensor(rw[:, 1, :], eg[:, :], rw[:, 0, :], ALU.mult).then_inc(s["rw1"], 1)
                for a in range(2):
                    dve.wait_ge(s["u"], i * 2 + a + 1)
                    dve.wait_ge(s["spreadc"], i * 5 + 5)
                    for j in range(2):
                        dve.tensor_tensor(um[:, 2 * a + j, :], fr[1 - a][:, :], selb[:, 2 * j, :], ALU.mult).then_inc(s["umul"], 1)
                for q in range(4):
                    dve.wait_ge(s["umh"], i * 4 + q + 1)
                    dve.tensor_tensor(ul[:, q, :], um[:, q, :], uh[:, q, :].bitcast(F32), ALU.subtract).then_inc(s["uml"], 1)
                for f in range(FT):
                    for j in range(2):
                        n = i * 2 * FT + 2 * f + j
                        dve.wait_ge(s["up"], n + 1)
                        dve.wait_ge(s["sw"], n + 1)
                        dve.tensor_tensor(sg[:, j, :], up_ps[:, :], sg[:, j, :], ALU.mult).then_inc(s["aw"], 1)
                    for j in range(2):
                        n = i * 2 * FT + 2 * f + j
                        dve.wait_ge(s["aw"], n + 1)
                        dve.wait_ge(s["awh"], n + 1)
                        dve.tensor_tensor(al[:, j, :], sg[:, j, :], ah[:, j, :].bitcast(F32), ALU.subtract).then_inc(s["awl"], 1)
                    dve.wait_ge(s["combh"], i * FT + f + 1)
                    dve.tensor_tensor(cbl[:, :], cb[:, :], cbh[:, :].bitcast(F32), ALU.subtract).then_inc(s["combl"], 1)
                dve.wait_ge(s["zdone"], i + 1)
                dve.wait_ge(s["combl"], i * FT + FT)
                dve.tensor_tensor(cb[:, :], z_ps0[:, :], selb[:, 0, :], ALU.mult).then_inc(s["z0m"], 1)
                dve.tensor_tensor(sg[:, 0, :], z_ps1[:, :], selb[:, 1, :], ALU.mult).then_inc(s["z1m"], 1)
                dve.wait_ge(s["z0m"], i + 1)
                dve.wait_ge(s["z1m"], i + 1)
                dve.tensor_tensor(cb[:, :], cb[:, :], sg[:, 0, :], ALU.add).then_inc(s["zsum"], 1)
                dve.wait_ge(s["zsum"], i + 1)
                dve.wait_ge(s["zh"], i + 1)
                dve.tensor_tensor(cbl[:, :], cb[:, :], cbh[:, :].bitcast(F32), ALU.subtract).then_inc(s["zl"], 1)
                dve.wait_ge(s["out"], i + 1)
                for m in range(KT):
                    dve.scalar_tensor_tensor(out=x[:, m, :], in0=out_ps[m][:, :], scalar=cur[:, GB * KT + m:GB * KT + m + 1],
                                             in1=x[:, m, :], op0=ALU.mult, op1=ALU.add).then_inc(s["y"], 1)

            body(0)
            with dve.Fori(1, NS) as i:
                body(i)

        @block.tensor
        def _(pe):
            pe.wait_ge(s["w_lo"], len(chunks))
            pe.wait_ge(s["vec"], 16 * 5)

            def body(i):
                def norm(which):
                    n = i * 2 + which
                    norm_sums(pe, ln, n, fr0, ones)
                    norm_spread(pe, ln, n, fr, ident)

                norm(0)
                pe.wait_ge(s["hl"], i * 2 + 1)
                for m in range(KT):
                    for k in range(KT):
                        mm = mm3(pe, fr[m][:, :], *wt("W1", D, k, m), hh[:, k, :], hl[:, k, :], k == 0, k == KT - 1)
                    mm.then_inc(s["w1"], 1)
                pe.wait_ge(s["part"], i * 2 + 2)
                pe.matmul(fr0[:, :], ones, sp[:, :], start=True, stop=True).then_inc(s["score"], 1)
                pe.wait_ge(s["exp"], i + 1)
                pe.wait_ge(s["ctxl"], i + 1)
                for m in range(KT):
                    for k in range(2 * KT):
                        q = (k + KT) % (2 * KT)
                        xh, xl = (hh, hl) if q >= KT else (ch, cl)
                        mm = mm3(pe, fr[m][:, :], *wt("Wc", D, q, m), xh[:, q % KT, :], xl[:, q % KT, :], k == 0,
                                 k == 2 * KT - 1)
                    mm.then_inc(s["wc"], 1)
                norm(1)
                pe.wait_ge(s["h_ready"], i * 2 * KT + 2 * KT)
                for t in range(TT):
                    for k in range(KT):
                        mm = pe.matmul(fr0[:, t * E:(t + 1) * E], h[:, k, t * P:(t + 1) * P], gw[:, k, :], start=(k == 0),
                                       stop=(k == KT - 1))
                mm.then_inc(s["logits"], 1)
                pe.wait_ge(s["hl"], i * 2 + 2)
                pe.wait_ge(s["lgc"], i + 1)
                pe.wait_ge(s["dif"], i + 1)
                for j in range(3):
                    if j == 2:
                        pe.wait_ge(s["spreadc"], i * 5 + 1)
                    for t in range(TT):
                        mm = pe.matmul(fr[j % 2][:, t * P:(t + 1) * P], sel[:, j, t, :], ident16,
                                       start=True, stop=True)
                    mm.then_inc(s["spread"], 1)
                pe.wait_ge(s["rw1"], i + 1)
                for j in range(2):
                    pe.wait_ge(s["spreadc"], i * 5 + 2 + j)
                    for t in range(TT):
                        mm = pe.transpose(fr[1 - j][:, t * P:(t + 1) * P], bc(rw[:, j, t:t + 1], [P, P]), ident)
                    mm.then_inc(s["spread"], 1)
                for a, name in enumerate(("A1", "A3")):
                    pe.wait_ge(s["spreadc"], i * 5 + 4 + a)
                    for k in range(KT):
                        mm = mm3(pe, fr[1 - a][:, :], *wt(name, P, k, 0), hh[:, k, :], hl[:, k, :], k == 0, k == KT - 1)
                    mm.then_inc(s["u"], 1)

                def common(ps, big, small, q, f, ready):
                    for k in range(KT):
                        mm3(pe, ps[:, :], *wt(big, F, k, f), hh[:, k, :], hl[:, k, :], k == 0, False)
                    mm3(pe, ps[:, :], *wt(small, F, 0, f), uh[:, q, :], ul[:, q, :], False, True).then_inc(s[ready], 1)

                def second(ps, small, q, f, ready):
                    pe.matmul(ps[:, :], wt(small, F, 0, f)[0], uh[:, q, :], start=False, stop=False, skip_group_check=True)
                    pe.matmul(ps[:, :], wt(small, F, 0, f)[0], ul[:, q, :], start=False, stop=False, skip_group_check=True)
                    pe.matmul(ps[:, :], wt(small, F, 0, f)[1], uh[:, q, :], start=False, stop=True,
                              skip_group_check=True).then_inc(s[ready], 1)

                def low_rank_out(f):
                    pe.wait_ge(s["awl"], i * 2 * FT + 2 * f + 2)
                    for j in range(2):
                        mm = mm3(pe, z_ps[j][:, :], *wt("A2", P, f, 0), ah[:, j, :], al[:, j, :], f == 0, f == FT - 1)
                    if f == FT - 1:
                        mm.then_inc(s["zdone"], 1)

                def down(f):
                    pe.wait_ge(s["combl"], i * FT + f + 1)
                    for m in range(KT):
                        mm = mm3(pe, out_ps[m][:, :], *wt("Wd", D, f, m), cbh[:, :], cbl[:, :], f == 0, False)
                    mm.then_inc(s["down"], 1)

                pe.wait_ge(s["uml"], i * 4 + 4)
                for f in range(FT):
                    n = i * 2 * FT + 2 * f
                    wait_reuse(pe, s["silu"], n)
                    common(gate_ps, "Wg", "B1", 0, f, "gate")
                    wait_reuse(pe, s["aw"], n)
                    common(up_ps, "Wu", "B3", 2, f, "up")
                    if f:
                        low_rank_out(f - 1)
                    pe.wait_ge(s["silu"], n + 1)
                    second(gate_ps, "B1", 1, f, "gate")
                    pe.wait_ge(s["aw"], n + 1)
                    second(up_ps, "B3", 3, f, "up")
                    if f:
                        down(f - 1)
                low_rank_out(FT - 1)
                down(FT - 1)
                pe.wait_ge(s["zl"], i + 1)
                for m in range(KT):
                    b = hi["B2"][:, m * P:(m + 1) * P], lo["B2"][:, m * P:(m + 1) * P]
                    mm = mm3(pe, out_ps[m][:, :], *b, cbh[:, :], cbl[:, :], False, True)
                mm.then_inc(s["out"], 1)

            body(0)
            with pe.Fori(1, NS) as i:
                body(i)


def second_layer(nc, sems, mid, x_out, w, mod, const):
    ident, ident16, ones, minus_half = const
    with ExitStack() as ctx:
        def sb(name, shape, dt=F32):
            return ctx.enter_context(nc.sbuf_tensor("b_" + name, shape, dt))

        def sem(name):
            sems.append(nc.alloc_semaphore("b_" + name))
            return sems[-1]

        bank = [ctx.enter_context(nc.psum_tensor(f"b_bank{i}", [P, T], F32)) for i in range(8)]

        shapes = {"qkv": KT * 3 * D, "proj": KT * D, "Wr": KT * D, "Wk": KT * D, "Wv": KT * D}
        chunks = [(name, c, min(c + 1024, n)) for name, n in shapes.items() for c in range(0, n, 1024)]
        hi = {name: sb(name + "_hi", [P, n], F32R) for name, n in shapes.items()}
        lo = {name: sb(name + "_lo", [P, n], F32R) for name, n in shapes.items()}

        def wt(name, width, k, m, cols=P):
            a = k * width + m * P
            return hi[name][:, a:a + cols], lo[name][:, a:a + cols]

        qkb = sb("qk_bias", [P, 2 * KT])
        vb = sb("v_bias", [P, D])
        pb = sb("proj_bias", [P, KT])
        mur = sb("mu_r", [P, KT])
        muk = sb("mu_k", [P, KT])
        cur = sb("mod_now", [P, 6 * KT])
        mask8 = sb("head_mask", [P, HG])
        bd = sb("block_mask", [P, P])

        ln = Norm(sb, sem)
        x = sb("x", [P, KT, T])
        h = sb("h", [P, KT, T + 1])
        hh = sb("h_hi", [P, KT, T], F32R)
        hl = sb("h_lo", [P, KT, T], F32R)
        qk = sb("qk", [P, 2 * KT, T])
        qke = sb("qk_eps", [P, 2 * KT, T])
        qsum = sb("qk_sum", [P, 2 * KT])
        qsume = sb("qk_sum_eps", [P, 2 * KT])
        kd = sb("sum_heads", [P, 2 * KT, HG])
        kd2 = sb("weighted_sum_heads", [P, 2 * KT, HG])
        tqk = sb("qk_tokens", [P, 2 * KT, T])
        v = sb("v_tokens", [P, TT, D])
        si = sb("flow_inverse", [P, 2, TT, H])
        cs = sb("conserved", [P, 2, TT, H])
        ec = sb("conserved_exp", [P, 2, TT, H])
        sa1 = sb("sink_gate_den", [P, TT, H])
        fo = sb("out_factor", [P, TT, H])
        rs = sb("competition_inverse", [P, H])
        sc = sb("competition", [P, TT, H])
        kv = sb("kv", [P, KT, P])
        ot = sb("out_tokens", [P, TT, D])
        oh = sb("out_hi", [P, KT, T], F32R)
        ol = sb("out_lo", [P, KT, T], F32R)
        dx = sb("shift_gap", [P, KT, T])
        xr = sb("mix_r", [P, KT, T])
        xk = sb("mix_k", [P, KT, T])
        rh = sb("mix_r_hi", [P, KT, T], F32R)
        rl = sb("mix_r_lo", [P, KT, T], F32R)
        kh = sb("mix_k_hi", [P, KT, T], F32R)
        kl = sb("mix_k_lo", [P, KT, T], F32R)
        rg = sb("receptance", [P, KT, T])
        stage = [qk[:, 0:2, :].rearrange("p a t -> p (a t)"), qk[:, 2:4, :].rearrange("p a t -> p (a t)"),
                 xr[:, :, :].rearrange("p a t -> p (a t)"), xk[:, :, :].rearrange("p a t -> p (a t)")]

        names = ("w_loaded w_hi w_lo vec mask pad x_in cur hh hl h_ready qk_ps qk qke sume kd tqk_ps tqk v_ps v s1 si s2 kd2 s3 "
                 "cse clip1 clip2 ex sa1 sar fo esum rs sc0 sc vc kv_ps kv o_ps ot oT oh ol proj py attn dx xr xk rh kh rl kl "
                 "r_ps k_ps rg relu k2 k2h k2l v2 vr y stored").split()
        s = {n: sem(n + "_s") for n in names}
        block = ctx.enter_context(nc.Block())

        @block.sync
        def _(sp_):
            for dst, src in ((qkb, w["qk_bias"]), (pb, w["proj_bias"]), (mur, w["mu_r"]), (muk, w["mu_k"])):
                sp_.dma_start(dst[:, :], src).then_inc(s["vec"], 16)
            sp_.dma_start(vb[:, :], bc(w["v_bias"], [P, D])).then_inc(s["vec"], 16)
            for n, (name, a, b) in enumerate(chunks):
                if n >= len(stage):
                    sp_.wait_ge(s["w_lo"], n - len(stage) + 1)
                sp_.dma_start(stage[n % len(stage)][:, 0:b - a], w[name][:, a:b]).then_inc(s["w_loaded"], 16)
                sp_.wait_ge(s["w_loaded"], 16 * (n + 1))

        @block.gpsimd
        def _(pool):
            pool.memset(mask8[:, :], 1.0).then_inc(s["mask"], 1)
            pool.memset(bd[:, :], 1.0).then_inc(s["mask"], 1)
            pool.memset(h[:, :, 0:1], 0.0).then_inc(s["pad"], 1)
            pool.wait_ge(s["mask"], 2)
            pool.affine_select(out=mask8[:, :], in_=mask8[:, :], compare_op=ALU.is_ge, fill=0.0, base=0,
                               pattern=[[-HD, HG]], channel_multiplier=1).then_inc(s["mask"], 1)
            bdv = bd[:, :].rearrange("p (a b) -> p a b", a=HG)
            pool.affine_select(out=bdv, in_=bdv, compare_op=ALU.is_ge, fill=0.0, base=0,
                               pattern=[[-HD, HG], [0, HD]], channel_multiplier=1).then_inc(s["mask"], 1)
            pool.wait_ge(s["mask"], 4)
            pool.affine_select(out=mask8[:, :], in_=mask8[:, :], compare_op=ALU.is_ge, fill=0.0, base=HD - 1,
                               pattern=[[HD, HG]], channel_multiplier=-1).then_inc(s["mask"], 1)
            pool.affine_select(out=bdv, in_=bdv, compare_op=ALU.is_ge, fill=0.0, base=HD - 1,
                               pattern=[[HD, HG], [0, HD]], channel_multiplier=-1).then_inc(s["mask"], 1)

            def body(i):
                pool.wait_ge(s["x_in"], i * 16 + 16)
                norm_presum(pool, ln, i * 2, x)
                norm_rstd(pool, ln, i * 2, minus_half)
                pool.wait_ge(s["attn"], i + 1)
                norm_presum(pool, ln, i * 2 + 1, x)
                norm_rstd(pool, ln, i * 2 + 1, minus_half)

            body(0)
            with pool.Fori(1, NS) as i:
                body(i)

        @block.scalar
        def _(act):
            for n, (name, a, b) in enumerate(chunks):
                act.wait_ge(s["w_loaded"], 16 * (n + 1))
                act.copy(hi[name][:, a:b], stage[n % len(stage)][:, 0:b - a]).then_inc(s["w_hi"], 1)
            act.wait_ge(s["pad"], 1)

            def body(i):
                wait_reuse(act, s["stored"], i * 16)
                act.dma_start(x[:, :, :], mid[bass.ds(i, 1)].rearrange("a p k t -> p (a k) t")).then_inc(s["x_in"], 16)
                act.wait_ge(s["x_in"], i * 16 + 16)
                norm_square(act, ln, i * 2, x[:, :, :])
                act.wait_ge(ln.s_add, i * 2 + 1)
                act.wait_ge(s["cur"], i * 2 + 2)
                wait_reuse(act, s["kl"], i)

                def modulated(dst, c, sh, k):
                    return act.activation(dst, ln.hx[:, k, :], ACT.Identity, bias=cur[:, sh * KT + k:sh * KT + k + 1],
                                          scale=cur[:, c * KT + k:c * KT + k + 1])

                for k in range(KT):
                    modulated(h[:, k, 1:T + 1], CA, SA, k).then_inc(s["h_ready"], 1)
                for k in range(KT):
                    modulated(hh[:, k, :], CA, SA, k).then_inc(s["hh"], 1)
                for c in range(2 * KT):
                    act.wait_ge(s["qk_ps"], i * 4 + c + 1)
                    act.activation(qk[:, c, :], bank[c][:, :], ACT.Sigmoid, bias=qkb[:, c:c + 1],
                                   accum_out=qsum[:, c:c + 1]).then_inc(s["qk"], 1)
                for c in range(2 * KT):
                    act.wait_ge(s["tqk_ps"], i * 4 + c + 1)
                    act.copy(tqk[:, c, :], bank[c][:, :]).then_inc(s["tqk"], 1)
                act.wait_ge(s["clip2"], i + 1)
                act.activation(ec[:, 1, :, :], cs[:, 1, :, :], ACT.Exp).then_inc(s["ex"], 1)
                act.activation(ec[:, 0, :, :], cs[:, 0, :, :], ACT.Exp, scale=-1.0).then_inc(s["ex"], 1)
                for g in range(KT):
                    act.wait_ge(s["oT"], i * KT + g + 1)
                    act.copy(oh[:, g, :], bank[4 + g][:, :]).then_inc(s["oh"], 1)
                act.wait_ge(s["attn"], i + 1)
                norm_square(act, ln, i * 2 + 1, x[:, :, :])
                act.wait_ge(ln.s_add, i * 2 + 2)
                for k in range(KT):
                    modulated(h[:, k, 1:T + 1], CB, SB, k).then_inc(s["h_ready"], 1)
                act.wait_ge(s["xr"], i + 1)
                act.copy(rh[:, :, :], xr[:, :, :]).then_inc(s["rh"], 1)
                act.wait_ge(s["xk"], i + 1)
                act.copy(kh[:, :, :], xk[:, :, :]).then_inc(s["kh"], 1)
                for m in range(KT):
                    act.wait_ge(s["r_ps"], i * KT + m + 1)
                    act.activation(rg[:, m, :], bank[m][:, :], ACT.Sigmoid).then_inc(s["rg"], 1)
                act.wait_ge(s["k2"], i + 1)
                act.copy(kh[:, :, :], xk[:, :, :]).then_inc(s["k2h"], 1)
                act.wait_ge(s["y"], i + 1)
                act.dma_start(x_out[bass.ds(i, 1)].rearrange("a p k t -> p (a k) t"), x[:, :, :]).then_inc(s["stored"], 16)

            body(0)
            with act.Fori(1, NS) as i:
                body(i)
            act.wait_ge(s["stored"], 16 * NS)

        @block.vector
        def _(dve):
            for n, (name, a, b) in enumerate(chunks):
                dve.wait_ge(s["w_hi"], n + 1)
                dve.tensor_tensor(lo[name][:, a:b], stage[n % len(stage)][:, 0:b - a], hi[name][:, a:b].bitcast(F32),
                                  ALU.subtract).then_inc(s["w_lo"], 1)
            dve.wait_ge(s["vec"], 16 * 5)
            dve.wait_ge(s["mask"], 6)

            def body(i):
                wait_reuse(dve, s["y"], i)
                dve.tensor_copy(cur[:, :], mod[:, bass.ds(i, 1), :].rearrange("p a c -> p (a c)")).then_inc(s["cur"], 2)
                dve.wait_ge(s["x_in"], i * 16 + 16)
                norm_stats_a(dve, ln, i * 2, bank[6])
                norm_stats_b(dve, ln, i * 2)
                norm_apply(dve, ln, i * 2, x, bank[6:8])
                dve.wait_ge(s["h_ready"], i * 2 * KT + KT)
                dve.wait_ge(s["hh"], i * KT + KT)
                dve.tensor_tensor(hl[:, :, :], h[:, :, 1:T + 1], hh[:, :, :].bitcast(F32), ALU.subtract).then_inc(s["hl"], 1)
                for j in range(2):
                    dve.wait_ge(s["v_ps"], i * 2 + j + 1)
                    dve.tensor_tensor(v[:, 2 * j:2 * j + 2, :], bank[4 + j][:, :].rearrange("p (a c) -> p a c", a=2),
                                      bc(vb[:, :].unsqueeze(1), [P, 2, D]), ALU.add).then_inc(s["v"], 1)
                dve.wait_ge(s["qk"], i * 4 + 4)
                dve.tensor_scalar(qke[:, :, :], qk[:, :, :], EPS, None, ALU.add).then_inc(s["qke"], 1)
                dve.tensor_scalar(qsume[:, :], qsum[:, :], EPS, None, ALU.add).then_inc(s["sume"], 1)
                dve.wait_ge(s["sume"], i + 1)
                for c in range(2 * KT):
                    last = dve.tensor_scalar(kd[:, c, :], mask8[:, :], qsume[:, c:c + 1], None, ALU.mult)
                last.then_inc(s["kd"], 1)
                dve.wait_ge(s["s1"], i + 1)
                dve.reciprocal(si[:, :, :, :].rearrange("p a t h -> p (a t h)"), bank[6][:, 0:2 * TT * H]).then_inc(s["si"], 1)
                dve.wait_ge(s["s2"], i + 1)
                dve.scalar_tensor_tensor(out=kd2[:, :, :], in0=bank[7][:, 0:2 * KT * HG].rearrange("p (c e) -> p c e", e=HG),
                                         scalar=EPS, in1=bc(mask8[:, :].unsqueeze(1), [P, 2 * KT, HG]), op0=ALU.add,
                                         op1=ALU.mult).then_inc(s["kd2"], 1)
                dve.wait_ge(s["s3"], i + 1)
                dve.tensor_scalar(cs[:, :, :, :].rearrange("p a t h -> p (a t h)"), bank[6][:, 0:2 * TT * H], EPS, None,
                                  ALU.add).then_inc(s["cse"], 1)
                dve.wait_ge(s["cse"], i + 1)
                dve.tensor_scalar(cs[:, 1, :, :], cs[:, 1, :, :], -1.0, 1.0, ALU.max, ALU.min).then_inc(s["clip2"], 1)
                dve.wait_ge(s["esum"], i + 1)
                dve.reciprocal(rs[:, :], bank[7][:, 0:H]).then_inc(s["rs"], 1)
                dve.wait_ge(s["ex"], i * 2 + 2)
                dve.tensor_scalar(sa1[:, :, :], ec[:, 0, :, :], 1.0, None, ALU.add).then_inc(s["sa1"], 1)
                dve.wait_ge(s["rs"], i + 1)
                dve.scalar_tensor_tensor(out=sc[:, :, :], in0=ec[:, 1, :, :], scalar=float(T),
                                         in1=bc(rs[:, :].unsqueeze(1), [P, TT, H]), op0=ALU.mult, op1=ALU.mult).then_inc(s["sc"], 1)
                dve.wait_ge(s["sa1"], i + 1)
                dve.reciprocal(sa1[:, :, :], sa1[:, :, :]).then_inc(s["sar"], 1)
                dve.wait_ge(s["sc"], i + 1)
                dve.wait_ge(s["v"], i * 2 + 2)
                vv = v[:, :, :].rearrange("p t (h d) -> p (t h) d", d=HD)
                dve.tensor_tensor(vv, vv, bc(sc[:, :, :].rearrange("p t h -> p (t h)").unsqueeze(2), [P, TT * H, HD]),
                                  ALU.mult).then_inc(s["vc"], 1)
                dve.wait_ge(s["sar"], i + 1)
                dve.tensor_tensor(fo[:, :, :], sa1[:, :, :], si[:, 0, :, :], ALU.mult).then_inc(s["fo"], 1)
                dve.wait_ge(s["kv_ps"], i + 1)
                dve.tensor_tensor(kv[:, :, :], bank[7][:, 0:D].rearrange("p (g c) -> p g c", g=KT),
                                  bc(bd[:, :].unsqueeze(1), [P, KT, P]), ALU.mult).then_inc(s["kv"], 1)
                dve.wait_ge(s["fo"], i + 1)
                for g in range(KT):
                    dve.wait_ge(s["o_ps"], i * KT + g + 1)
                    dve.tensor_tensor(ot[:, :, g * P:(g + 1) * P].rearrange("p t (h d) -> p t h d", d=HD),
                                      bank[4 + g][:, :].rearrange("p (t h d) -> p t h d", t=TT, d=HD),
                                      bc(fo[:, :, g * HG:(g + 1) * HG].unsqueeze(3), [P, TT, HG, HD]), ALU.mult).then_inc(s["ot"], 1)
                for g in range(KT):
                    dve.wait_ge(s["oh"], i * KT + g + 1)
                    dve.tensor_tensor(ol[:, g, :], bank[4 + g][:, :], oh[:, g, :].bitcast(F32), ALU.subtract).then_inc(s["ol"], 1)
                for m in range(KT):
                    dve.wait_ge(s["proj"], i * KT + m + 1)
                    last = dve.tensor_scalar(dx[:, m, :], bank[m][:, :], pb[:, m:m + 1],
                                             cur[:, GA * KT + m:GA * KT + m + 1], ALU.add, ALU.mult)
                last.then_inc(s["py"], 1)
                dve.wait_ge(s["py"], i + 1)
                dve.tensor_tensor(x[:, :, :], x[:, :, :], dx[:, :, :], ALU.add).then_inc(s["attn"], 1)
                dve.wait_ge(s["attn"], i + 1)
                norm_stats_a(dve, ln, i * 2 + 1, bank[6])
                norm_stats_b(dve, ln, i * 2 + 1)
                norm_apply(dve, ln, i * 2 + 1, x, bank[6:8])
                dve.wait_ge(s["h_ready"], i * 2 * KT + 2 * KT)
                dve.tensor_tensor(dx[:, :, :], h[:, :, 1:T + 1], h[:, :, 0:T], ALU.subtract).then_inc(s["dx"], 1)
                dve.wait_ge(s["dx"], i + 1)
                for dst, mu, done in ((xr, mur, "xr"), (xk, muk, "xk")):
                    for k in range(KT):
                        last = dve.scalar_tensor_tensor(out=dst[:, k, :], in0=dx[:, k, :], scalar=mu[:, k:k + 1],
                                                        in1=h[:, k, 0:T], op0=ALU.mult, op1=ALU.add)
                    last.then_inc(s[done], 1)
                dve.wait_ge(s["rh"], i + 1)
                dve.tensor_tensor(rl[:, :, :], xr[:, :, :], rh[:, :, :].bitcast(F32), ALU.subtract).then_inc(s["rl"], 1)
                dve.wait_ge(s["kh"], i + 1)
                dve.tensor_tensor(kl[:, :, :], xk[:, :, :], kh[:, :, :].bitcast(F32), ALU.subtract).then_inc(s["kl"], 1)
                for m in range(KT):
                    dve.wait_ge(s["k_ps"], i * KT + m + 1)
                    last = dve.tensor_scalar(dx[:, m, :], bank[2 + m][:, :], 0.0, None, ALU.max)
                last.then_inc(s["relu"], 1)
                dve.wait_ge(s["relu"], i + 1)
                dve.tensor_tensor(xk[:, :, :], dx[:, :, :], dx[:, :, :], ALU.mult).then_inc(s["k2"], 1)
                dve.wait_ge(s["k2"], i + 1)
                dve.wait_ge(s["k2h"], i + 1)
                dve.tensor_tensor(kl[:, :, :], xk[:, :, :], kh[:, :, :].bitcast(F32), ALU.subtract).then_inc(s["k2l"], 1)
                dve.wait_ge(s["rg"], i * KT + KT)
                for m in range(KT):
                    dve.wait_ge(s["v2"], i * KT + m + 1)
                    last = dve.tensor_tensor(dx[:, m, :], bank[4 + m][:, :], rg[:, m, :], ALU.mult)
                last.then_inc(s["vr"], 1)
                dve.wait_ge(s["vr"], i + 1)
                for m in range(KT):
                    last = dve.scalar_tensor_tensor(out=x[:, m, :], in0=dx[:, m, :], scalar=cur[:, GB * KT + m:GB * KT + m + 1],
                                                    in1=x[:, m, :], op0=ALU.mult, op1=ALU.add)
                last.then_inc(s["y"], 1)

            body(0)
            with dve.Fori(1, NS) as i:
                body(i)

        @block.tensor
        def _(pe):
            pe.wait_ge(s["w_lo"], len(chunks))

            def body(i):
                norm_sums(pe, ln, i * 2, bank[6], ones)
                norm_spread(pe, ln, i * 2, bank[6:8], ident)
                pe.wait_ge(s["hl"], i + 1)
                wait_reuse(pe, s["vr"], i)
                for c in range(2 * KT):
                    for k in range(KT):
                        mm = mm3(pe, bank[c][:, :], *wt("qkv", 3 * D, k, c), hh[:, k, :], hl[:, k, :], k == 0, k == KT - 1)
                    mm.then_inc(s["qk_ps"], 1)
                for t in range(TT):
                    tok = slice(t * P, (t + 1) * P)
                    vh, vl = [], []
                    for k in range(KT):
                        wh, wl = wt("qkv", 3 * D, k, 2 * KT, D)
                        mm = mm3(pe, bank[4 + t // 2][:, (t % 2) * D:(t % 2 + 1) * D], hh[:, k, tok], hl[:, k, tok], wh, wl,
                                 k == 0, k == KT - 1)
                    if t % 2:
                        mm.then_inc(s["v_ps"], 1)
                for c in range(2 * KT):
                    pe.wait_ge(s["qk"], i * 4 + c + 1)
                    for t in range(TT):
                        mm = pe.transpose(bank[c][:, t * P:(t + 1) * P], qk[:, c, t * P:(t + 1) * P], ident)
                    mm.then_inc(s["tqk_ps"], 1)

                def flows(rhs, ready):
                    for a in range(2):
                        for g in range(KT):
                            for t in range(TT):
                                o = (a * TT + t) * H + g * HG
                                mm = pe.matmul(bank[6][:, o:o + HG], qke[:, 2 * a + g, t * P:(t + 1) * P],
                                               rhs[:, 2 * (1 - a) + g, :], start=True, stop=True)
                    mm.then_inc(s[ready], 1)

                pe.wait_ge(s["qke"], i + 1)
                pe.wait_ge(s["kd"], i + 1)
                flows(kd, "s1")
                pe.wait_ge(s["tqk"], i * 4 + 4)
                pe.wait_ge(s["si"], i + 1)
                for c in range(2 * KT):
                    a, g = c // KT, c % KT
                    for t in range(TT):
                        mm = pe.matmul(bank[7][:, c * HG:(c + 1) * HG], tqk[:, c, t * P:(t + 1) * P],
                                       si[:, a, t, g * HG:(g + 1) * HG], start=(t == 0), stop=(t == TT - 1))
                mm.then_inc(s["s2"], 1)
                pe.wait_ge(s["kd2"], i + 1)
                flows(kd2, "s3")
                pe.wait_ge(s["ex"], i * 2 + 1)
                for t in range(TT):
                    mm = pe.matmul(bank[7][:, 0:H], ones, ec[:, 1, t, :], start=(t == 0), stop=(t == TT - 1))
                mm.then_inc(s["esum"], 1)
                pe.wait_ge(s["vc"], i + 1)
                for g in range(KT):
                    for t in range(TT):
                        mm = pe.matmul(bank[7][:, g * P:(g + 1) * P], tqk[:, KT + g, t * P:(t + 1) * P],
                                       v[:, t, g * P:(g + 1) * P], start=(t == 0), stop=(t == TT - 1))
                mm.then_inc(s["kv_ps"], 1)
                pe.wait_ge(s["kv"], i + 1)
                for g in range(KT):
                    for t in range(TT):
                        mm = pe.matmul(bank[4 + g][:, t * P:(t + 1) * P], qk[:, g, t * P:(t + 1) * P], kv[:, g, :],
                                       start=True, stop=True)
                    mm.then_inc(s["o_ps"], 1)
                for g in range(KT):
                    pe.wait_ge(s["ot"], i * KT + g + 1)
                    for t in range(TT):
                        mm = pe.transpose(bank[4 + g][:, t * P:(t + 1) * P], ot[:, t, g * P:(g + 1) * P], ident)
                    mm.then_inc(s["oT"], 1)
                pe.wait_ge(s["ol"], i * KT + KT)
                for m in range(KT):
                    for k in range(KT):
                        mm = mm3(pe, bank[m][:, :], *wt("proj", D, k, m), oh[:, k, :], ol[:, k, :], k == 0, k == KT - 1)
                    mm.then_inc(s["proj"], 1)
                norm_sums(pe, ln, i * 2 + 1, bank[6], ones)
                norm_spread(pe, ln, i * 2 + 1, bank[6:8], ident)
                pe.wait_ge(s["rl"], i + 1)
                for m in range(KT):
                    for k in range(KT):
                        mm = mm3(pe, bank[m][:, :], *wt("Wr", D, k, m), rh[:, k, :], rl[:, k, :], k == 0, k == KT - 1)
                    mm.then_inc(s["r_ps"], 1)
                pe.wait_ge(s["kl"], i + 1)
                for m in range(KT):
                    for k in range(KT):
                        mm = mm3(pe, bank[2 + m][:, :], *wt("Wk", D, k, m), kh[:, k, :], kl[:, k, :], k == 0, k == KT - 1)
                    mm.then_inc(s["k_ps"], 1)
                pe.wait_ge(s["k2l"], i + 1)
                for m in range(KT):
                    for k in range(KT):
                        mm = mm3(pe, bank[4 + m][:, :], *wt("Wv", D, k, m), kh[:, k, :], kl[:, k, :], k == 0, k == KT - 1)
                    mm.then_inc(s["v2"], 1)

            body(0)
            with pe.Fori(1, NS) as i:
                body(i)


def modulation(nc, sems, conds, wmods, mods, const):
    ident, ident16, ones, minus_half = const
    N = 6 * KT
    with ExitStack() as ctx:
        def sb(name, shape, dt=F32):
            return ctx.enter_context(nc.sbuf_tensor("m_" + name, shape, dt))

        def sem(name):
            sems.append(nc.alloc_semaphore("m_" + name))
            return sems[-1]

        c_sb = [sb(f"c{l}", [P, KT, NS]) for l in range(2)]
        w_sb = [sb(f"w{l}", [P, KT, 6 * D]) for l in range(2)]
        mag = sb("mag", [P, NS, KT])
        sign = sb("sign", [P, NS, KT])
        ps = [ctx.enter_context(nc.psum_tensor(f"m_bank{l}", [P, N * NS], F32)) for l in range(2)]
        loaded, silu, product, chain, const_ready = (sem(n) for n in ("loaded", "silu", "product", "chain", "const"))
        block = ctx.enter_context(nc.Block())

        @block.sync
        def _(sp_):
            for l in range(2):
                sp_.dma_start(c_sb[l][:, :, :], conds[l]).then_inc(loaded, 16)
                sp_.dma_start(w_sb[l][:, :, :], wmods[l]).then_inc(loaded, 16)

        @block.gpsimd
        def _(pool):
            pool.memset(ones[:, :], 1.0).then_inc(const_ready, 1)
            pool.memset(minus_half[:, :], -0.5).then_inc(const_ready, 1)
            pool.memset(ident[:, :], 0.0).then_inc(const_ready, 1)
            pool.memset(ident16[:, :], 0.0).then_inc(const_ready, 1)
            pool.wait_ge(const_ready, 4)
            for m in (ident, ident16):
                pool.affine_select(out=m[:, :], in_=m[:, :], compare_op=ALU.not_equal, fill=1.0, base=0, pattern=[[-1, P]],
                                   channel_multiplier=1).then_inc(const_ready, 1)

        @block.scalar
        def _(act):
            act.wait_ge(loaded, 64)
            for l in range(2):
                act.activation(c_sb[l][:, :, :], c_sb[l][:, :, :], ACT.Silu).then_inc(silu, 1)

        @block.tensor
        def _(pe):
            for l in range(2):
                pe.wait_ge(silu, l + 1)
                for n in range(N):
                    for k in range(KT):
                        mm = pe.matmul(ps[l][:, n * NS:(n + 1) * NS], w_sb[l][:, k, n * P:(n + 1) * P], c_sb[l][:, k, :],
                                       start=(k == 0), stop=(k == KT - 1))
                mm.then_inc(product, 1)

        @block.vector
        def _(dve):
            done = 0
            for l in range(2):
                dve.wait_ge(product, l + 1)
                dve.tensor_copy(mods[l][:, :, :].rearrange("p s n -> p n s"),
                                ps[l][:, :].rearrange("p (n s) -> p n s", s=NS)).then_inc(chain, 1)
                done += 1
                for row in (CA, CB):
                    dve.wait_ge(chain, done)
                    a = mods[l][:, :, row * KT:(row + 1) * KT]
                    dve.tensor_scalar(a, a, 1.0, None, ALU.add).then_inc(chain, 1)
                    done += 1
                for row in (GA, GB):
                    a = mods[l][:, :, row * KT:(row + 1) * KT]
                    dve.wait_ge(chain, done)
                    dve.scalar_tensor_tensor(out=mag[:, :, :], in0=a, scalar=-1.0, in1=a, op0=ALU.mult, op1=ALU.max).then_inc(chain, 1)
                    dve.tensor_scalar(sign[:, :, :], a, 0.0, 2.0, ALU.is_ge, ALU.mult).then_inc(chain, 1)
                    dve.wait_ge(chain, done + 2)
                    dve.tensor_scalar(mag[:, :, :], mag[:, :, :], GATE_MIN, None, ALU.max).then_inc(chain, 1)
                    dve.wait_ge(chain, done + 3)
                    dve.scalar_tensor_tensor(out=a, in0=sign[:, :, :], scalar=-1.0, in1=mag[:, :, :], op0=ALU.add,
                                             op1=ALU.mult).then_inc(chain, 1)
                    done += 4


def clear(nc, sems):
    nc.all_engine_barrier()
    nc.clear_and_free_semaphores(sems)
    nc.all_engine_barrier()
    sems.clear()


def program(nc, a, x_out):
    mid = nc.dram_tensor("mid", (NS, P, KT, T), F32, kind="Internal").ap()
    with ExitStack() as ctx:
        def sb(name, shape, dt=F32):
            return ctx.enter_context(nc.sbuf_tensor(name, shape, dt))

        ident_t, ident16_t, ones_t = sb("ident", [P, P]), sb("ident16", [P, P], BF16), sb("ones", [P, P])
        half_t = sb("minus_half", [P, TT])
        const = (ident_t[:, :], ident16_t[:, :], ones_t[:, :], half_t[:, :])
        mods = [sb(f"mod{l}", [P, NS, 6 * KT]) for l in range(2)]
        sems = []
        modulation(nc, sems, (a["c0"], a["c1"]), (a["wmod0"], a["wmod1"]), mods, const)
        clear(nc, sems)
        first_layer(nc, sems, a["x"], mid, a, mods[0], const)
        clear(nc, sems)
        second_layer(nc, sems, mid, x_out, a, mods[1], const)



def _rows_down(m):
    k, n = m.shape
    return np.ascontiguousarray(m.reshape(k // P, P, n).transpose(1, 0, 2).reshape(P, -1))


def _vec(v):
    return np.ascontiguousarray(np.asarray(v).reshape(-1, P).T)


def kernel(**inputs):
    import concourse.bacc as _bacc
    from concourse.bass_utils import run_bass_kernel_spmd as _run

    g = {k: np.asarray(v) for k, v in inputs.items()}
    experts_in = lambda m: m.reshape(E * R, -1).T
    experts_out = lambda m: m.transpose(0, 2, 1).reshape(E * R, -1)
    x = g["L0_attn_x"].transpose(0, 2, 1).reshape(NS, KT, P, T).transpose(0, 2, 1, 3)
    host = {
        "x": np.ascontiguousarray(x),
        "c0": _rows_down(g["L0_c"].T).reshape(P, KT, NS),
        "c1": _rows_down(g["L1_c"].T).reshape(P, KT, NS),
        "wmod0": _rows_down(g["L0_wmod"]).reshape(P, KT, 6 * D),
        "wmod1": _rows_down(g["L1_wmod"]).reshape(P, KT, 6 * D),
        "W1": _rows_down(g["L0_attn_W1"].T),
        "b1": _vec(g["L0_attn_b1"]),
        "w2": _vec(g["L0_attn_w2"]),
        "b2": np.ascontiguousarray(np.broadcast_to(g["L0_attn_b2"].reshape(1, 1), (P, 1))),
        "Wc": _rows_down(g["L0_attn_Wc"].T),
        "bc": _vec(g["L0_attn_bc"]),
        "gate_w": _rows_down(g["L0_ffn_gate_w"].T).reshape(P, KT, E),
        "Wg": _rows_down(g["L0_ffn_w_gate"].T),
        "Wu": _rows_down(g["L0_ffn_w_up"].T),
        "Wd": _rows_down(g["L0_ffn_w_down"].T),
        "A1": _rows_down(experts_in(g["L0_ffn_A1"])),
        "A3": _rows_down(experts_in(g["L0_ffn_A3"])),
        "A2": _rows_down(experts_in(g["L0_ffn_A2"])),
        "B1": _rows_down(experts_out(g["L0_ffn_B1"])),
        "B3": _rows_down(experts_out(g["L0_ffn_B3"])),
        "B2": _rows_down(experts_out(g["L0_ffn_B2"])),
        "qkv": _rows_down(g["L1_attn_qkv_w"].T),
        "qk_bias": _vec(g["L1_attn_qkv_b"][:2 * D]),
        "v_bias": np.ascontiguousarray(g["L1_attn_qkv_b"][2 * D:].reshape(1, D)),
        "proj": _rows_down(g["L1_attn_proj_w"].T),
        "proj_bias": _vec(g["L1_attn_proj_b"]),
        "Wr": _rows_down(g["L1_ffn_W_r"].T),
        "Wk": _rows_down(g["L1_ffn_W_k"].T),
        "Wv": _rows_down(g["L1_ffn_W_v"].T),
        "mu_r": _vec(g["L1_ffn_mu_r"]),
        "mu_k": _vec(g["L1_ffn_mu_k"]),
    }
    nc = _bacc.Bacc("TRN2", target_bir_lowering=False, num_devices=1)
    args = {n: nc.dram_tensor("in_" + n, a.shape, mybir.dt.from_np(a.dtype), kind="ExternalInput").ap()
            for n, a in host.items()}
    out = nc.dram_tensor("out", (NS, P, KT, T), F32, kind="ExternalOutput").ap()
    program(nc, args, out)
    r = _run(nc, [{"in_" + n: a for n, a in host.items()}], core_ids=[0])
    y = np.asarray(r.results[0]["out"])
    return np.ascontiguousarray(y.transpose(0, 2, 1, 3).reshape(NS, D, T).transpose(0, 2, 1))
```

```python
from contextlib import ExitStack

import numpy as np
import concourse.bass as bass
from concourse import mybir

F32 = mybir.dt.float32
F32R = mybir.dt.float32r
BF16 = mybir.dt.bfloat16
U32 = mybir.dt.uint32
ACT = mybir.ActivationFunctionType
ALU = mybir.AluOpType
AX = mybir.AxisListType

P = 128
NS = 16
T = 512
D = 256
KT = D // P
TT = T // P
E = 8
R = 16
F = 1024
FT = F // P
H = 16
HD = D // H
HG = P // HD
LN_EPS = 1e-5
EPS = 1e-6
SCALE = 2.0
GATE_MIN = 0.25

SA, CA, GA, SB, CB, GB = range(6)


def bc(ap, shape):
    return ap.to_broadcast(shape)


def wait_reuse(engine, sem, n):
    if not isinstance(n, int) or n > 0:
        engine.wait_ge(sem, n)


def mm3(pe, out, w_hi, w_lo, x_hi, x_lo, start, stop):
    pe.matmul(out, w_hi, x_hi, start=start, stop=False)
    pe.matmul(out, w_hi, x_lo, start=False, stop=False)
    return pe.matmul(out, w_lo, x_hi, start=False, stop=stop)


class Norm:

    def __init__(self, sb, sem, sq, hx, tag=""):
        self.sq = sq
        self.hx = hx
        self.xs = sb("ln_xs" + tag, [P, 2, T], F32)
        self.stat = sb("ln_stat" + tag, [P, 2, TT], F32)
        self.mm = sb("ln_mm" + tag, [P, TT], F32)
        self.var = sb("ln_var" + tag, [P, TT], F32)
        self.rstd = sb("ln_rstd" + tag, [P, 2, TT], F32)
        self.s_sq = sem("ln_sq_ready" + tag)
        self.s_xs = sem("ln_xs_ready" + tag)
        self.s_qs = sem("ln_qs_ready" + tag)
        self.s_sums = sem("ln_sums_ready" + tag)
        self.s_mean = sem("ln_mean_ready" + tag)
        self.s_mm = sem("ln_mm_ready" + tag)
        self.s_var = sem("ln_var_ready" + tag)
        self.s_rstd = sem("ln_rstd_ready" + tag)
        self.s_nmr = sem("ln_nmr_ready" + tag)
        self.s_bc = sem("ln_spread_ready" + tag)
        self.s_mul = sem("ln_mul_ready" + tag)
        self.s_add = sem("ln_add_ready" + tag)


def norm_square(act, ln, n, x):
    wait_reuse(act, ln.s_qs, n)
    act.activation(ln.sq[:, :, :], x, ACT.Square).then_inc(ln.s_sq, 1)


def norm_presum(pool, ln, n, x):
    wait_reuse(pool, ln.s_sums, n)
    pool.tensor_tensor(ln.xs[:, 0, :], x[:, 0, :], x[:, 1, :], ALU.add).then_inc(ln.s_xs, 1)


def norm_sums(pe, ln, n, bank, ones):
    pe.wait_ge(ln.s_xs, n + 1)
    pe.wait_ge(ln.s_qs, n + 1)
    for j in range(2):
        for t in range(TT):
            c = j * TT + t
            mm = pe.matmul(bank[:, c:c + 1], ln.xs[:, j, t * P:(t + 1) * P], ones[:, 0:1], start=True, stop=True)
    mm.then_inc(ln.s_sums, 1)


def norm_presum_squares(dve, ln, n):
    dve.wait_ge(ln.s_sq, n + 1)
    wait_reuse(dve, ln.s_sums, n)
    dve.tensor_tensor(ln.xs[:, 1, :], ln.sq[:, 0, :], ln.sq[:, 1, :], ALU.add).then_inc(ln.s_qs, 1)


def norm_stats(dve, ln, n, bank):
    dve.wait_ge(ln.s_sums, n + 1)
    dve.tensor_scalar(ln.stat[:, :, :].rearrange("p a t -> p (a t)"), bank[:, 0:2 * TT], 1.0 / D, None,
                      ALU.mult).then_inc(ln.s_mean, 1)
    dve.wait_ge(ln.s_mean, n + 1)
    dve.tensor_tensor(ln.mm[:, :], ln.stat[:, 0, :], ln.stat[:, 0, :], ALU.mult).then_inc(ln.s_mm, 1)
    dve.wait_ge(ln.s_mm, n + 1)
    dve.scalar_tensor_tensor(out=ln.var[:, :], in0=ln.stat[:, 1, :], scalar=LN_EPS, in1=ln.mm[:, :],
                             op0=ALU.add, op1=ALU.subtract).then_inc(ln.s_var, 1)


def norm_rstd(pool, ln, n, minus_half):
    pool.wait_ge(ln.s_var, n + 1)
    pool.tensor_tensor(ln.rstd[:, 0, :], ln.var[:, :], minus_half, ALU.pow).then_inc(ln.s_rstd, 1)


def norm_minus_mean(dve, ln, n):
    dve.wait_ge(ln.s_rstd, n + 1)
    dve.scalar_tensor_tensor(out=ln.rstd[:, 1, :], in0=ln.stat[:, 0, :], scalar=-1.0, in1=ln.rstd[:, 0, :],
                             op0=ALU.mult, op1=ALU.mult).then_inc(ln.s_nmr, 1)


def norm_spread(pe, ln, n, banks, ident):
    pe.wait_ge(ln.s_rstd, n + 1)
    pe.wait_ge(ln.s_nmr, n + 1)
    for j in range(2):
        for t in range(TT):
            mm = pe.transpose(banks[j][:, t * P:(t + 1) * P], bc(ln.rstd[:, j, t:t + 1], [P, P]), ident)
    mm.then_inc(ln.s_bc, 1)


def norm_apply(dve, ln, n, x, banks):
    dve.wait_ge(ln.s_bc, n + 1)
    for k in range(KT):
        mul = dve.tensor_tensor(ln.hx[:, k, :], x[:, k, :], banks[0][:, :], ALU.mult)
    mul.then_inc(ln.s_mul, 1)
    dve.wait_ge(ln.s_mul, n + 1)
    for k in range(KT):
        add = dve.tensor_tensor(ln.hx[:, k, :], ln.hx[:, k, :], banks[1][:, :], ALU.add)
    add.then_inc(ln.s_add, 1)


def first_layer(nc, sems, x_in, mid, w, mod, const):
    ident, ident16, ones, minus_half = const
    with ExitStack() as ctx:
        def sb(name, shape, dt=F32):
            return ctx.enter_context(nc.sbuf_tensor("a_" + name, shape, dt))

        def sem(name):
            sems.append(nc.alloc_semaphore("a_" + name))
            return sems[-1]

        gate_ps, up_ps, out_ps0, out_ps1, z_ps0, z_ps1, fr0, fr1 = [
            ctx.enter_context(nc.psum_tensor(f"a_bank{i}", [P, T], F32)) for i in range(8)]
        out_ps, z_ps, fr = (out_ps0, out_ps1), (z_ps0, z_ps1), (fr0, fr1)

        shapes = {"W1": KT * D, "Wc": 2 * KT * D, "A1": KT * P, "A3": KT * P, "Wg": KT * F, "Wu": KT * F,
                  "B1": F, "B3": F, "A2": FT * P, "Wd": FT * D, "B2": D}
        chunks = [(name, c, min(c + 1024, n)) for name, n in shapes.items() for c in range(0, n, 1024)]
        hi = {name: sb(name + "_hi", [P, n], F32R) for name, n in shapes.items()}
        lo = {name: sb(name + "_lo", [P, n], F32R) for name, n in shapes.items()}

        def wt(name, width, k, m, cols=P):
            a = k * width + m * P
            return hi[name][:, a:a + cols], lo[name][:, a:a + cols]

        gw = sb("gate_w", [P, KT, E])
        b1 = sb("b1", [P, KT])
        bcv = sb("bc", [P, KT])
        w2 = sb("w2", [P, KT])
        b2 = sb("b2", [P, 1])
        b2p = sb("b2_part", [P, 1])
        curs = sb("mod_now", [P, 2, 6 * KT])
        iota = sb("expert_no", [P, TT, E])

        x = sb("x", [P, KT, T])
        x1 = sb("x1", [P, 2, KT, T])
        h = sb("h", [P, KT, T])
        hhs = sb("h_hi", [P, 2, KT, T], F32R)
        hls = sb("h_lo", [P, 2, KT, T], F32R)
        th = sb("tanh", [P, KT, T])
        hx = sb("normed", [P, KT, T])
        ln = Norm(sb, sem, hx, hx)
        den = sb("den", [P, T])
        sp = den
        nmx = sb("score_max_neg", [P, 1])
        ex = sb("exp", [P, T])
        ch = sb("ctx_hi", [P, KT, T], F32R)
        cl = sb("ctx_lo", [P, KT, T], F32R)
        lg = sb("logits", [P, TT, E])
        top = sb("top_values", [P, TT, E])
        topi = sb("top_index", [P, TT, E], U32)
        topf = sb("top_index_f", [P, TT, 2])
        hot = sb("one_hot", [P, 2, TT, E])
        sel = sb("masks", [P, 3, TT, E * R], BF16)
        dl = sb("logit_gap", [P, TT])
        eg = sb("gap_exp", [P, TT])
        rw = sb("route_w", [P, 2, TT])
        selbs = sb("masks_spread", [P, 2, 3, T], BF16)
        rwbs = sb("route_w_spread", [P, 2, 2, T])
        um = (h[:, 0, :], h[:, 1, :], th[:, 0, :], th[:, 1, :])
        uh = sb("u_hi", [P, 4, T], F32R)
        ul = sb("u_lo", [P, 4, T], F32R)
        zm, z1 = ex, den
        zh, zl = ch[:, 0, :], cl[:, 0, :]
        sg = sb("silu", [P, 2, T])
        ah = sb("act_hi", [P, 2, T], F32R)
        al = sb("act_lo", [P, 2, T], F32R)
        cb = sb("act_sum", [P, T])
        cbh = sb("act_sum_hi", [P, T], F32R)
        cbl = sb("act_sum_lo", [P, T], F32R)
        dummy = sb("dummy", [P, 1])
        stage = [v.rearrange("p a t -> p (a t)") for v in (h[:, :, :], th[:, :, :], x1[:, 0, :, :], x1[:, 1, :, :])]

        names = ("w_hi w_lo vec iota b2p x_in cur h_ready hh hl w1 tanh part score smax exp den prod scan "
                 "rden ctx ctxh ctxl wc tanh2 attn logits lgc settle top topi topf hot sel dif gap gapexp "
                 "gap1 rw0 rw1 spread spreadc u umul umh uml gate up silu sw aw awh awl comb combh combl "
                 "low down z0m z1m zsum zh zl out y stored").split()
        s = {n: sem(n + "_s") for n in names}
        s_stage = [sem(f"stage{n}_s") for n in range(len(stage))]
        block = ctx.enter_context(nc.Block())

        @block.sync
        def _(sp_):
            for dst, src in ((gw, w["gate_w"]), (b1, w["b1"]), (bcv, w["bc"]), (w2, w["w2"]), (b2, w["b2"])):
                sp_.dma_start(dst[tuple(slice(None) for _ in dst.shape)], src).then_inc(s["vec"], 16)
            for n, (name, a, b) in enumerate(chunks):
                if n >= len(stage):
                    sp_.wait_ge(s["w_lo"], n - len(stage) + 1)
                sp_.dma_start(stage[n % len(stage)][:, 0:b - a], w[name][:, a:b]).then_inc(s_stage[n % len(stage)], 16)

        @block.scalar
        def _(act):
            def split_hi(n):
                name, a, b = chunks[n]
                act.wait_ge(s_stage[n % len(stage)], 16 * (n // len(stage) + 1))
                act.copy(hi[name][:, a:b], stage[n % len(stage)][:, 0:b - a]).then_inc(s["w_hi"], 1)

            def load_x(i):
                wait_reuse(act, s["attn"], i * KT)
                act.dma_start(x[:, :, :], x_in[bass.ds(i, 1)].rearrange("a p k t -> p (a k) t")).then_inc(s["x_in"], 16)

            def squares(i, which, p):
                n = i * 2 + which
                if which == 0:
                    act.wait_ge(s["x_in"], i * 16 + 16)
                else:
                    act.wait_ge(s["attn"], i * KT + KT)
                wait_reuse(act, s["hh"], n * KT)
                norm_square(act, ln, n, x[:, :, :] if which == 0 else x1[:, p, :, :])

            def modulate(i, which, p):
                n = i * 2 + which
                c, sh = ((CA, SA), (CB, SB))[which]
                cur = curs[:, p, :]
                act.wait_ge(ln.s_add, n + 1)
                act.wait_ge(s["cur"], i * 2 + 2)
                if which == 0:
                    wait_reuse(act, s["uml"], i * 4)
                    wait_reuse(act, s["up"], (i - 1) * 2 * FT)
                else:
                    act.wait_ge(s["wc"], i * KT + KT)
                for dst, done in ((h[:, :, :], "h_ready"), (hhs[:, p, :, :], "hh")):
                    for k in range(KT):
                        act.activation(dst[:, k, :], hx[:, k, :], ACT.Identity, bias=cur[:, sh * KT + k:sh * KT + k + 1],
                                       scale=cur[:, c * KT + k:c * KT + k + 1]).then_inc(s[done], 1)

            def tanh(i):
                wait_reuse(act, s["uml"], i * 4)
                for m in range(KT):
                    act.wait_ge(s["w1"], i * KT + m + 1)
                    act.activation(th[:, m, :], fr[m][:, :], ACT.Tanh, bias=b1[:, m:m + 1]).then_inc(s["tanh"], 1)

            def exp(i):
                act.wait_ge(s["smax"], i + 1)
                act.activation(ex[:, :], fr0[:, :], ACT.Exp, bias=nmx[:, 0:1]).then_inc(s["exp"], 1)

            def ctx_hi(i):
                act.wait_ge(s["ctx"], i + 1)
                act.copy(ch[:, :, :], th[:, :, :]).then_inc(s["ctxh"], 1)

            def tanh_out(i):
                act.wait_ge(s["ctxl"], i + 1)
                for m in range(KT):
                    act.wait_ge(s["wc"], i * KT + m + 1)
                    act.activation(th[:, m, :], fr[m][:, :], ACT.Tanh, bias=bcv[:, m:m + 1]).then_inc(s["tanh2"], 1)

            def gap_exp(i):
                act.wait_ge(s["gap"], i + 1)
                act.activation(eg[:, :], dl[:, :], ACT.Exp).then_inc(s["gapexp"], 1)

            def spread_out(i, p, j):
                act.wait_ge(s["spread"], i * 5 + j + 1)
                dst = selbs[:, p, j, :] if j < 3 else rwbs[:, p, j - 3, :]
                act.copy(dst, fr[j % 2][:, :]).then_inc(s["spreadc"], 1)

            def front(i, p):
                return {
                    (0, 0): lambda: squares(i, 0, p),
                    (1, 2): lambda: modulate(i, 0, p),
                    (2, 0): lambda: tanh(i),
                    (2, 3): lambda: exp(i),
                    (3, 3): lambda: ctx_hi(i),
                    (4, 1): lambda: tanh_out(i),
                    (4, 3): lambda: squares(i, 1, p),
                    (5, 2): lambda: modulate(i, 1, p),
                    (6, 0): lambda: gap_exp(i),
                    (6, 2): lambda: [spread_out(i, p, j) for j in range(3)],
                    (6, 4): lambda: [spread_out(i, p, j) for j in (3, 4)],
                }

            def u_hi(i):
                wait_reuse(act, s["up"], i * 2 * FT)
                for q in (0, 2, 1, 3):
                    act.wait_ge(s["umul"], i * 4 + q + 1)
                    act.copy(uh[:, q, :], um[q]).then_inc(s["umh"], 1)

            def z_hi(i):
                act.wait_ge(s["zsum"], i + 1)
                act.copy(zh, zm[:, :]).then_inc(s["zh"], 1)

            def store_x(i, p):
                act.wait_ge(s["y"], i * KT + KT)
                act.dma_start(mid[bass.ds(i, 1)].rearrange("a p k t -> p (a k) t"), x1[:, p, :, :]).then_inc(s["stored"], 16)

            def steps(i, p, ahead, before):
                at = front(i + 1, 1 - p) if ahead else {}
                if before:
                    at[(0, 5)] = lambda: z_hi(i - 1)
                    at[(1, 3)] = lambda: store_x(i - 1, 1 - p)

                def slot(f, q):
                    if (f, q) in at:
                        at[(f, q)]()

                for f in range(FT):
                    for j in range(2):
                        n = i * 2 * FT + 2 * f + j
                        act.wait_ge(s["gate"], n + 1)
                        wait_reuse(act, s["awl"], i * 2 * FT + 2 * f)
                        wait_reuse(act, s["comb"], i * FT + f)
                        act.activation(sg[:, j, :], gate_ps[:, :], ACT.Silu).then_inc(s["silu"], 1)
                        slot(f, j)
                    for j in range(2):
                        n = i * 2 * FT + 2 * f + j
                        act.wait_ge(s["aw"], n + 1)
                        wait_reuse(act, s["low"], i * FT + f)
                        act.copy(ah[:, j, :], sg[:, j, :]).then_inc(s["awh"], 1)
                        slot(f, 2 + j)
                    if ahead and f == FT - 1:
                        act.wait_ge(s["up"], (i + 1) * 2 * FT)
                        u_hi(i + 1)
                    act.wait_ge(s["comb"], i * FT + f + 1)
                    wait_reuse(act, s["down"], i * FT + f)
                    act.copy(cbh[:, :], cb[:, :]).then_inc(s["combh"], 1)
                    slot(f, 4)
                    slot(f, 5)

            def whole_front(i, p):
                for f, q in sorted(at := front(i, p)):
                    at[(f, q)]()

            load_x(0)
            for n in range(len(chunks)):
                split_hi(n)
            act.wait_ge(s["w_lo"], len(chunks))
            whole_front(0, 0)
            u_hi(0)
            load_x(1)
            steps(0, 0, True, False)
            with act.Fori(0, NS // 2 - 1) as pair:
                i = pair * 2 + 1
                for d in range(2):
                    load_x(i + d + 1)
                    steps(i + d, 1 - d, True, True)
            steps(NS - 1, 1, False, True)
            z_hi(NS - 1)
            store_x(NS - 1, 1)
            act.wait_ge(s["stored"], 16 * NS)

        @block.gpsimd
        def _(pool):
            for e in range(E):
                pool.memset(iota[:, :, e:e + 1], float(e)).then_inc(s["iota"], 1)

            def presum(i, which, p):
                if which == 0:
                    pool.wait_ge(s["x_in"], i * 16 + 16)
                else:
                    pool.wait_ge(s["attn"], i * KT + KT)
                norm_presum(pool, ln, i * 2 + which, x if which == 0 else x1[:, p, :, :])

            def steps(i, p, ahead):
                j1 = i + 1
                at = {
                    (0, 0): lambda: presum(j1, 0, 1 - p),
                    (0, 2): lambda: norm_rstd(pool, ln, j1 * 2, minus_half),
                    (4, 2): lambda: presum(j1, 1, 1 - p),
                    (5, 0): lambda: norm_rstd(pool, ln, j1 * 2 + 1, minus_half),
                } if ahead else {}
                for f in range(FT):
                    for j in range(2):
                        n = i * 2 * FT + 2 * f + j
                        pool.wait_ge(s["silu"], n + 1)
                        pool.wait_ge(s["spreadc"], i * 5 + 5)
                        pool.tensor_tensor(sg[:, j, :], sg[:, j, :], rwbs[:, p, j, :], ALU.mult).then_inc(s["sw"], 1)
                        if (f, j) in at:
                            at[(f, j)]()
                    pool.wait_ge(s["aw"], i * 2 * FT + 2 * f + 2)
                    wait_reuse(pool, s["combl"], i * FT + f)
                    pool.tensor_tensor(cb[:, :], sg[:, 0, :], sg[:, 1, :], ALU.add).then_inc(s["comb"], 1)
                    if (f, 2) in at:
                        at[(f, 2)]()

            for which in range(2):
                presum(0, which, 0)
                norm_rstd(pool, ln, which, minus_half)
            steps(0, 0, True)
            with pool.Fori(0, NS // 2 - 1) as pair:
                i = pair * 2 + 1
                for d in range(2):
                    steps(i + d, 1 - d, True)
            steps(NS - 1, 1, False)

        @block.vector
        def _(dve):
            for n, (name, a, b) in enumerate(chunks):
                dve.wait_ge(s["w_hi"], n + 1)
                dve.tensor_tensor(lo[name][:, a:b], stage[n % len(stage)][:, 0:b - a], hi[name][:, a:b].bitcast(F32),
                                  ALU.subtract).then_inc(s["w_lo"], 1)
            dve.wait_ge(s["w_lo"], len(chunks))
            dve.wait_ge(s["vec"], 16 * 5)
            dve.tensor_scalar(b2p[:, :], b2[:, :], 1.0 / P, None, ALU.mult).then_inc(s["b2p"], 1)
            dve.wait_ge(s["b2p"], 1)
            dve.wait_ge(s["iota"], E)

            def now(i, p):
                wait_reuse(dve, s["y"], (i - 1) * KT)
                dve.tensor_copy(curs[:, p, :], mod[:, bass.ds(i, 1), :].rearrange("p a c -> p (a c)")).then_inc(s["cur"], 1)
                dve.wait_ge(s["cur"], i * 2 + 1)
                dve.tensor_copy(dummy[:, :], curs[:, p, 0:1]).then_inc(s["cur"], 1)

            def presum(i, which):
                norm_presum_squares(dve, ln, i * 2 + which)

            def stats(i, which):
                norm_stats(dve, ln, i * 2 + which, fr0)

            def minus_mean(i, which):
                norm_minus_mean(dve, ln, i * 2 + which)

            def apply(i, which, p):
                norm_apply(dve, ln, i * 2 + which, x if which == 0 else x1[:, p, :, :], fr)

            def h_lo(i, which, p):
                n = i * 2 + which
                dve.wait_ge(s["h_ready"], n * KT + KT)
                dve.wait_ge(s["hh"], n * KT + KT)
                dve.tensor_tensor(hls[:, p, :, :], h[:, :, :], hhs[:, p, :, :].bitcast(F32), ALU.subtract).then_inc(s["hl"], 1)

            def score_parts(i):
                dve.wait_ge(s["tanh"], i * KT + KT)
                wait_reuse(dve, s["zsum"], i - 1)
                dve.tensor_scalar(sp[:, :], th[:, 0, :], w2[:, 0:1], b2p[:, 0:1], ALU.mult, ALU.add).then_inc(s["part"], 1)
                dve.wait_ge(s["part"], i * 2 + 1)
                dve.scalar_tensor_tensor(out=sp[:, :], in0=th[:, 1, :], scalar=w2[:, 1:2], in1=sp[:, :], op0=ALU.mult,
                                         op1=ALU.add).then_inc(s["part"], 1)

            def score_max(i):
                dve.wait_ge(s["score"], i + 1)
                dve.tensor_reduce(nmx[:, :], fr0[:, :], AX.X, ALU.max, negate=True).then_inc(s["smax"], 1)

            def products(i):
                dve.wait_ge(s["exp"], i + 1)
                dve.tensor_tensor_scan(den[:, :], ex[:, :], ex[:, :], 0.0, ALU.add, ALU.bypass).then_inc(s["den"], 1)
                for k in range(KT):
                    prod = dve.tensor_tensor(hx[:, k, :], h[:, k, :], ex[:, :], ALU.mult)
                prod.then_inc(s["prod"], 1)
                dve.wait_ge(s["den"], i + 1)
                dve.reciprocal(den[:, :], den[:, :]).then_inc(s["rden"], 1)

            def scans(i):
                dve.wait_ge(s["prod"], i + 1)
                for k in range(KT):
                    scan = dve.tensor_tensor_scan(th[:, k, :], hx[:, k, :], hx[:, k, :], 0.0, ALU.add, ALU.bypass)
                scan.then_inc(s["scan"], 1)

            def context(i):
                dve.wait_ge(s["rden"], i + 1)
                dve.wait_ge(s["scan"], i + 1)
                for k in range(KT):
                    c = dve.tensor_tensor(th[:, k, :], th[:, k, :], den[:, :], ALU.mult)
                c.then_inc(s["ctx"], 1)

            def ctx_lo(i):
                dve.wait_ge(s["ctx"], i + 1)
                dve.wait_ge(s["ctxh"], i + 1)
                dve.tensor_tensor(cl[:, :, :], th[:, :, :], ch[:, :, :].bitcast(F32), ALU.subtract).then_inc(s["ctxl"], 1)

            def attention_out(i, p):
                for m in range(KT):
                    dve.wait_ge(s["tanh2"], i * KT + m + 1)
                    wait_reuse(dve, s["stored"], (i - 1) * 16)
                    dve.scalar_tensor_tensor(out=x1[:, p, m, :], in0=th[:, m, :],
                                             scalar=curs[:, p, GA * KT + m:GA * KT + m + 1],
                                             in1=x[:, m, :], op0=ALU.mult, op1=ALU.add).then_inc(s["attn"], 1)

            def route(i):
                dve.wait_ge(s["logits"], i + 1)
                dve.tensor_copy(lg[:, :, :].rearrange("p t e -> p (t e)"), fr0[:, 0:TT * E]).then_inc(s["lgc"], 1)
                dve.wait_ge(s["lgc"], i + 1)
                dve.tensor_copy(dummy[:, :], lg[:, 0, 0:1]).then_inc(s["settle"], 1)
                for t in range(TT):
                    mx = dve.max(top[:, t, :], lg[:, t, :])
                mx.then_inc(s["top"], 1)
                dve.wait_ge(s["settle"], i * 2 + 1)
                dve.wait_ge(s["top"], i + 1)
                dve.tensor_copy(dummy[:, :], top[:, 0, 0:1]).then_inc(s["settle"], 1)
                for t in range(TT):
                    mx = dve.max_index(topi[:, t, :], top[:, t, :], lg[:, t, :])
                mx.then_inc(s["topi"], 1)
                dve.tensor_tensor(dl[:, :], top[:, :, 1], top[:, :, 0], ALU.subtract).then_inc(s["gap"], 1)
                dve.wait_ge(s["settle"], i * 2 + 2)
                dve.wait_ge(s["topi"], i + 1)
                dve.tensor_copy(topf[:, :, :], topi[:, :, 0:2]).then_inc(s["topf"], 1)
                dve.wait_ge(s["topf"], i + 1)
                for j in range(2):
                    hot_ = dve.tensor_tensor(hot[:, j, :, :], iota[:, :, :], bc(topf[:, :, j:j + 1], [P, TT, E]), ALU.is_equal)
                hot_.then_inc(s["hot"], 1)
                dve.wait_ge(s["hot"], i + 1)
                dve.tensor_scalar(sel[:, 0:2, :, :].rearrange("p a t (e r) -> p (a t e) r", r=R),
                                  bc(hot[:, :, :, :].rearrange("p a t e -> p (a t e)").unsqueeze(2), [P, 2 * TT * E, R]),
                                  SCALE, None, ALU.mult).then_inc(s["sel"], 1)
                dve.wait_ge(s["sel"], i + 1)
                dve.tensor_tensor(sel[:, 2, :, :], sel[:, 1, :, :], sel[:, 0, :, :], ALU.subtract).then_inc(s["dif"], 1)

            def route_weights(i):
                dve.wait_ge(s["gapexp"], i + 1)
                dve.tensor_scalar(dl[:, :], eg[:, :], 1.0, None, ALU.add).then_inc(s["gap1"], 1)
                dve.wait_ge(s["gap1"], i + 1)
                dve.reciprocal(rw[:, 0, :], dl[:, :]).then_inc(s["rw0"], 1)
                dve.wait_ge(s["rw0"], i + 1)
                dve.tensor_tensor(rw[:, 1, :], eg[:, :], rw[:, 0, :], ALU.mult).then_inc(s["rw1"], 1)

            def mask_u(i, p):
                for a in range(2):
                    dve.wait_ge(s["u"], i * 2 + a + 1)
                    dve.wait_ge(s["spreadc"], i * 5 + 5)
                    dve.wait_ge(s["hl"], i * 2 + 2)
                    for j in range(2):
                        dve.tensor_tensor(um[2 * a + j], fr[1 - a][:, :], selbs[:, p, 2 * j, :], ALU.mult).then_inc(s["umul"], 1)

            def front(i, p):
                return {
                    (0, 0): lambda: presum(i, 0),
                    (0, 2): lambda: stats(i, 0),
                    (0, 3): lambda: minus_mean(i, 0),
                    (1, 0): lambda: apply(i, 0, p),
                    (1, 2): lambda: now(i, p),
                    (1, 3): lambda: h_lo(i, 0, p),
                    (2, 0): lambda: score_parts(i),
                    (2, 2): lambda: score_max(i),
                    (2, 4): lambda: products(i),
                    (3, 0): lambda: scans(i),
                    (3, 1): lambda: context(i),
                    (3, 4): lambda: ctx_lo(i),
                    (4, 1): lambda: attention_out(i, p),
                    (4, 4): lambda: [presum(i, 1), stats(i, 1), minus_mean(i, 1)],
                    (5, 0): lambda: apply(i, 1, p),
                    (5, 4): lambda: [h_lo(i, 1, p), route(i)],
                    (6, 0): lambda: route_weights(i),
                    (7, 0): lambda: mask_u(i, p),
                }

            def u_lo(i):
                wait_reuse(dve, s["up"], i * 2 * FT)
                for n, q in enumerate((0, 2, 1, 3)):
                    dve.wait_ge(s["umul"], i * 4 + 4)
                    dve.wait_ge(s["umh"], i * 4 + n + 1)
                    dve.tensor_tensor(ul[:, q, :], um[q], uh[:, q, :].bitcast(F32), ALU.subtract).then_inc(s["uml"], 1)

            def z_masked(i, p):
                dve.wait_ge(s["low"], i * FT + FT)
                dve.tensor_tensor(zm[:, :], z_ps0[:, :], selbs[:, p, 0, :], ALU.mult).then_inc(s["z0m"], 1)
                dve.tensor_tensor(z1[:, :], z_ps1[:, :], selbs[:, p, 1, :], ALU.mult).then_inc(s["z1m"], 1)
                dve.wait_ge(s["z0m"], i + 1)
                dve.wait_ge(s["z1m"], i + 1)
                dve.tensor_tensor(zm[:, :], zm[:, :], z1[:, :], ALU.add).then_inc(s["zsum"], 1)

            def z_lo(i):
                dve.wait_ge(s["zsum"], i + 1)
                dve.wait_ge(s["zh"], i + 1)
                dve.tensor_tensor(zl, zm[:, :], zh.bitcast(F32), ALU.subtract).then_inc(s["zl"], 1)

            def layer_out(i, p):
                dve.wait_ge(s["out"], i + 1)
                for m in range(KT):
                    dve.scalar_tensor_tensor(out=x1[:, p, m, :], in0=out_ps[m][:, :],
                                             scalar=curs[:, p, GB * KT + m:GB * KT + m + 1],
                                             in1=x1[:, p, m, :], op0=ALU.mult, op1=ALU.add).then_inc(s["y"], 1)

            def steps(i, p, ahead, before):
                at = front(i + 1, 1 - p) if ahead else {}
                late = {
                    (0, 2): lambda: z_masked(i - 1, 1 - p),
                    (0, 4): lambda: z_lo(i - 1),
                    (1, 1): lambda: layer_out(i - 1, 1 - p),
                } if before else {}

                def slot(f, q):
                    if (f, q) in late:
                        late[(f, q)]()
                    if (f, q) in at:
                        at[(f, q)]()

                for f in range(FT):
                    for j in range(2):
                        n = i * 2 * FT + 2 * f + j
                        dve.wait_ge(s["up"], n + 1)
                        dve.wait_ge(s["sw"], n + 1)
                        dve.tensor_tensor(sg[:, j, :], up_ps[:, :], sg[:, j, :], ALU.mult).then_inc(s["aw"], 1)
                        slot(f, 2 * j)
                        dve.wait_ge(s["aw"], n + 1)
                        dve.wait_ge(s["awh"], n + 1)
                        dve.tensor_tensor(al[:, j, :], sg[:, j, :], ah[:, j, :].bitcast(F32), ALU.subtract).then_inc(s["awl"], 1)
                        slot(f, 2 * j + 1)
                    if ahead and f == FT - 1:
                        u_lo(i + 1)
                    dve.wait_ge(s["combh"], i * FT + f + 1)
                    dve.tensor_tensor(cbl[:, :], cb[:, :], cbh[:, :].bitcast(F32), ALU.subtract).then_inc(s["combl"], 1)
                    slot(f, 4)

            at = front(0, 0)
            for f, q in sorted(at):
                at[(f, q)]()
            u_lo(0)
            steps(0, 0, True, False)
            with dve.Fori(0, NS // 2 - 1) as pair:
                i = pair * 2 + 1
                for d in range(2):
                    steps(i + d, 1 - d, True, True)
            steps(NS - 1, 1, False, True)
            z_masked(NS - 1, 1)
            z_lo(NS - 1)
            layer_out(NS - 1, 1)

        @block.tensor
        def _(pe):
            pe.wait_ge(s["w_lo"], len(chunks))
            pe.wait_ge(s["vec"], 16 * 5)

            def w1(i, p):
                pe.wait_ge(s["hl"], i * 2 + 1)
                for m in range(KT):
                    for k in range(KT):
                        mm = mm3(pe, fr[m][:, :], *wt("W1", D, k, m), hhs[:, p, k, :], hls[:, p, k, :], k == 0, k == KT - 1)
                    mm.then_inc(s["w1"], 1)

            def score(i):
                pe.wait_ge(s["part"], i * 2 + 2)
                pe.matmul(fr0[:, :], ones, sp[:, :], start=True, stop=True).then_inc(s["score"], 1)

            def combine(i, p):
                pe.wait_ge(s["exp"], i + 1)
                pe.wait_ge(s["ctxl"], i + 1)
                for m in range(KT):
                    for k in range(2 * KT):
                        xh, xl = (ch[:, k, :], cl[:, k, :]) if k < KT else (hhs[:, p, k - KT, :], hls[:, p, k - KT, :])
                        mm = mm3(pe, fr[m][:, :], *wt("Wc", D, k, m), xh, xl, k == 0, k == 2 * KT - 1)
                    mm.then_inc(s["wc"], 1)

            def logits(i):
                pe.wait_ge(s["h_ready"], i * 2 * KT + 2 * KT)
                for t in range(TT):
                    for k in range(KT):
                        mm = pe.matmul(fr0[:, t * E:(t + 1) * E], h[:, k, t * P:(t + 1) * P], gw[:, k, :], start=(k == 0),
                                       stop=(k == KT - 1))
                mm.then_inc(s["logits"], 1)

            def spread_masks(i):
                pe.wait_ge(s["hl"], i * 2 + 2)
                pe.wait_ge(s["dif"], i + 1)
                for j in range(3):
                    if j == 2:
                        pe.wait_ge(s["spreadc"], i * 5 + 1)
                    for t in range(TT):
                        mm = pe.matmul(fr[j % 2][:, t * P:(t + 1) * P], sel[:, j, t, :], ident16, start=True, stop=True)
                    mm.then_inc(s["spread"], 1)

            def spread_weights(i):
                pe.wait_ge(s["rw1"], i + 1)
                for j in range(2):
                    pe.wait_ge(s["spreadc"], i * 5 + 2 + j)
                    for t in range(TT):
                        mm = pe.transpose(fr[1 - j][:, t * P:(t + 1) * P], bc(rw[:, j, t:t + 1], [P, P]), ident)
                    mm.then_inc(s["spread"], 1)

            def low_rank_in(i, p):
                for a, name in enumerate(("A1", "A3")):
                    pe.wait_ge(s["spreadc"], i * 5 + 4 + a)
                    for k in range(KT):
                        mm = mm3(pe, fr[1 - a][:, :], *wt(name, P, k, 0), hhs[:, p, k, :], hls[:, p, k, :], k == 0, k == KT - 1)
                    mm.then_inc(s["u"], 1)

            def front(i, p):
                return {
                    (0, 3): lambda: norm_sums(pe, ln, i * 2, fr0, ones),
                    (1, 0): lambda: norm_spread(pe, ln, i * 2, fr, ident),
                    (2, 0): lambda: w1(i, p),
                    (2, 3): lambda: score(i),
                    (4, 0): lambda: combine(i, p),
                    (5, 0): lambda: norm_sums(pe, ln, i * 2 + 1, fr0, ones),
                    (5, 2): lambda: norm_spread(pe, ln, i * 2 + 1, fr, ident),
                    (6, 0): lambda: logits(i),
                    (6, 3): lambda: spread_masks(i),
                    (6, 4): lambda: spread_weights(i),
                    (7, 0): lambda: low_rank_in(i, p),
                }

            def common(ps, big, f, p):
                for k in range(KT):
                    mm3(pe, ps[:, :], *wt(big, F, k, f), hhs[:, p, k, :], hls[:, p, k, :], k == 0, False)

            def slot_0(ps, small, q, f):
                return mm3(pe, ps[:, :], *wt(small, F, 0, f), uh[:, q, :], ul[:, q, :], False, True)

            def slot_1(ps, small, q, f):
                w_hi, w_lo = wt(small, F, 0, f)
                pe.matmul(ps[:, :], w_hi, uh[:, q, :], start=False, stop=False, skip_group_check=True)
                pe.matmul(ps[:, :], w_hi, ul[:, q, :], start=False, stop=False, skip_group_check=True)
                return pe.matmul(ps[:, :], w_lo, uh[:, q, :], start=False, stop=True, skip_group_check=True)

            def low_rank_out(i, f):
                for j in range(2):
                    if f == 0:
                        wait_reuse(pe, s["zsum"], i)
                    pe.wait_ge(s["awl"], i * 2 * FT + 2 * f + 1 + j)
                    mm = mm3(pe, z_ps[j][:, :], *wt("A2", P, f, 0), ah[:, j, :], al[:, j, :], f == 0, f == FT - 1)
                mm.then_inc(s["low"], 1)

            def down(i, f):
                if f == 0:
                    wait_reuse(pe, s["y"], i * KT)
                pe.wait_ge(s["combl"], i * FT + f + 1)
                for m in range(KT):
                    mm = mm3(pe, out_ps[m][:, :], *wt("Wd", D, f, m), cbh[:, :], cbl[:, :], f == 0, False)
                mm.then_inc(s["down"], 1)

            def experts_out(i):
                pe.wait_ge(s["zl"], i + 1)
                for m in range(KT):
                    b = hi["B2"][:, m * P:(m + 1) * P], lo["B2"][:, m * P:(m + 1) * P]
                    mm = mm3(pe, out_ps[m][:, :], *b, zh, zl, False, True)
                mm.then_inc(s["out"], 1)

            def steps(i, p, ahead, before):
                at = front(i + 1, 1 - p) if ahead else {}
                if before:
                    at_end = {(1, 1): lambda: experts_out(i - 1)}
                else:
                    at_end = {}

                def slot(f, q):
                    if (f, q) in at_end:
                        at_end[(f, q)]()
                    if (f, q) in at:
                        at[(f, q)]()

                for f in range(FT):
                    n = i * 2 * FT + 2 * f
                    last = (i, f - 1) if f else (i - 1, FT - 1)
                    wait_reuse(pe, s["silu"], n)
                    common(gate_ps, "Wg", f, p)
                    if f == 0:
                        pe.wait_ge(s["uml"], i * 4 + 1)
                    slot_0(gate_ps, "B1", 0, f).then_inc(s["gate"], 1)
                    slot(f, 0)
                    if f or before:
                        low_rank_out(*last)
                    slot(f, 1)
                    wait_reuse(pe, s["aw"], n)
                    common(up_ps, "Wu", f, p)
                    if f == 0:
                        pe.wait_ge(s["uml"], i * 4 + 2)
                    slot_0(up_ps, "B3", 2, f).then_inc(s["up"], 1)
                    slot(f, 2)
                    pe.wait_ge(s["silu"], n + 1)
                    if f == 0:
                        pe.wait_ge(s["uml"], i * 4 + 4)
                    slot_1(gate_ps, "B1", 1, f).then_inc(s["gate"], 1)
                    if f or before:
                        down(*last)
                    slot(f, 3)
                    pe.wait_ge(s["aw"], n + 1)
                    slot_1(up_ps, "B3", 3, f).then_inc(s["up"], 1)
                    slot(f, 4)

            at = front(0, 0)
            for f, q in sorted(at):
                at[(f, q)]()
            steps(0, 0, True, False)
            with pe.Fori(0, NS // 2 - 1) as pair:
                i = pair * 2 + 1
                for d in range(2):
                    steps(i + d, 1 - d, True, True)
            steps(NS - 1, 1, False, True)
            low_rank_out(NS - 1, FT - 1)
            down(NS - 1, FT - 1)
            experts_out(NS - 1)


def second_layer(nc, sems, mid, x_out, w, mod, const):
    ident, ident16, ones, minus_half = const
    with ExitStack() as ctx:
        def sb(name, shape, dt=F32):
            return ctx.enter_context(nc.sbuf_tensor("b_" + name, shape, dt))

        def sem(name):
            sems.append(nc.alloc_semaphore("b_" + name))
            return sems[-1]

        banks = [ctx.enter_context(nc.psum_tensor(f"b_bank{i}", [P, T], F32)) for i in range(8)]
        qkv_ps, flow_ps, out_ps, mix_ps = banks[0:2], banks[2:4], banks[4:6], banks[6:8]

        shapes = {"qkv": KT * 3 * D, "proj": KT * D, "Wr": KT * D, "Wk": KT * D, "Wv": KT * D}
        chunks = [(name, c, min(c + 1024, n)) for name, n in shapes.items() for c in range(0, n, 1024)]
        hi = {name: sb(name + "_hi", [P, n], F32R) for name, n in shapes.items()}
        lo = {name: sb(name + "_lo", [P, n], F32R) for name, n in shapes.items()}

        def wt(name, width, k, m, cols=P):
            a = k * width + m * P
            return hi[name][:, a:a + cols], lo[name][:, a:a + cols]

        qkb = sb("qk_bias", [P, 2 * KT])
        vb = sb("v_bias", [P, D])
        pb = sb("proj_bias", [P, KT])
        mur = sb("mu_r", [P, KT])
        muk = sb("mu_k", [P, KT])
        curs = sb("mod_now", [P, 3, 6 * KT])
        cur3 = sb("mod_mix", [P, 6 * KT])
        mask8 = sb("head_mask", [P, HG])
        bd = sb("block_mask", [P, P])

        x = sb("x", [P, KT, T])
        hx0 = sb("normed0", [P, KT, T])
        ln0 = Norm(sb, sem, hx0, hx0, "0")
        h0 = sb("h0", [P, KT, T])
        hh = sb("h_hi", [P, KT, T], F32R)
        hl = sb("h_lo", [P, KT, T], F32R)
        qks = sb("qk", [P, 3, 2 * KT, T])
        qsums = sb("qk_sum", [P, 3, 2 * KT])
        vs = sb("v_tokens", [P, 3, TT, D])
        qke = sb("qk_eps", [P, 2 * KT, T])
        qsume = sb("qk_sum_eps", [P, 2 * KT])
        kd = sb("sum_heads", [P, 2 * KT, HG])
        kd2 = sb("weighted_sum_heads", [P, 2 * KT, HG])
        tqks = sb("qk_tokens", [P, 3, 2 * KT, T])
        sis = sb("flow_inverse", [P, 3, 2, TT, H])
        cs = sb("conserved", [P, 2, TT, H])
        ecs = sb("conserved_exp", [P, 3, 2, TT, H])
        sa1 = sb("sink_gate_den", [P, TT, H])
        fo = sb("out_factor", [P, TT, H])
        rs = sb("competition_inverse", [P, H])
        sc = sb("competition", [P, TT, H])
        kv = sb("kv", [P, KT, P])
        ot = sb("out_tokens", [P, TT, D])
        oh = sb("out_hi", [P, KT, T], F32R)
        ol = sb("out_lo", [P, KT, T], F32R)
        xbs = sb("x_back", [P, 3, KT, T])
        hx3 = sb("normed3", [P, KT, T])
        ln3 = Norm(sb, sem, hx3, hx3, "3")
        h3 = sb("h3", [P, KT, T + 1])
        dx = sb("shift_gap", [P, KT, T])
        xr = sb("mix_r", [P, KT, T])
        xk = sb("mix_k", [P, KT, T])
        rh = sb("mix_r_hi", [P, KT, T], F32R)
        rl = sb("mix_r_lo", [P, KT, T], F32R)
        kh = sb("mix_k_hi", [P, KT, T], F32R)
        kl = sb("mix_k_lo", [P, KT, T], F32R)
        rg = sb("receptance", [P, KT, T])
        stage = [qks[:, 0, 0:2, :].rearrange("p a t -> p (a t)"), qks[:, 0, 2:4, :].rearrange("p a t -> p (a t)"),
                 xr[:, :, :].rearrange("p a t -> p (a t)"), xk[:, :, :].rearrange("p a t -> p (a t)")]

        names = ("w_hi w_lo vec mask pad x_in x_back cur cur3 hh hl h0 h3 qk_ps qk qke sume kd tqk_ps tqk v_ps v s1 si s2 kd2 s3 "
                 "cse clip ex sa1 sar fo esum rs sc vc kv_ps kv o_ps ot oT oh ol proj py attn dx xr xk rh kh rl kl "
                 "r_ps k_ps rg relu k2 k2h k2l v2 vr y stored").split()
        s = {n: sem(n + "_s") for n in names}
        s_stage = [sem(f"stage{n}_s") for n in range(len(stage))]
        block = ctx.enter_context(nc.Block())

        def turns(engine, turn):
            rounds = (NS - 4) // 3
            for i in range(4):
                turn(i, i % 3, range(i + 1))
            with engine.Fori(0, rounds) as three:
                for d in range(3):
                    turn(three * 3 + 4 + d, (4 + d) % 3, range(4))
            for i in range(4 + rounds * 3, NS + 3):
                turn(i, i % 3, range(max(0, i - NS + 1), 4))

        @block.sync
        def _(sp_):
            for dst, src in ((qkb, w["qk_bias"]), (pb, w["proj_bias"]), (mur, w["mu_r"]), (muk, w["mu_k"])):
                sp_.dma_start(dst[:, :], src).then_inc(s["vec"], 16)
            sp_.dma_start(vb[:, :], bc(w["v_bias"], [P, D])).then_inc(s["vec"], 16)
            for n, (name, a, b) in enumerate(chunks):
                if n >= len(stage):
                    sp_.wait_ge(s["w_lo"], n - len(stage) + 1)
                sp_.dma_start(stage[n % len(stage)][:, 0:b - a], w[name][:, a:b]).then_inc(s_stage[n % len(stage)], 16)

        @block.gpsimd
        def _(pool):
            pool.memset(mask8[:, :], 1.0).then_inc(s["mask"], 1)
            pool.memset(bd[:, :], 1.0).then_inc(s["mask"], 1)
            pool.memset(h3[:, :, 0:1], 0.0).then_inc(s["pad"], 1)
            pool.wait_ge(s["mask"], 2)
            pool.affine_select(out=mask8[:, :], in_=mask8[:, :], compare_op=ALU.is_ge, fill=0.0, base=0,
                               pattern=[[-HD, HG]], channel_multiplier=1).then_inc(s["mask"], 1)
            bdv = bd[:, :].rearrange("p (a b) -> p a b", a=HG)
            pool.affine_select(out=bdv, in_=bdv, compare_op=ALU.is_ge, fill=0.0, base=0,
                               pattern=[[-HD, HG], [0, HD]], channel_multiplier=1).then_inc(s["mask"], 1)
            pool.wait_ge(s["mask"], 4)
            pool.affine_select(out=mask8[:, :], in_=mask8[:, :], compare_op=ALU.is_ge, fill=0.0, base=HD - 1,
                               pattern=[[HD, HG]], channel_multiplier=-1).then_inc(s["mask"], 1)
            pool.affine_select(out=bdv, in_=bdv, compare_op=ALU.is_ge, fill=0.0, base=HD - 1,
                               pattern=[[HD, HG], [0, HD]], channel_multiplier=-1).then_inc(s["mask"], 1)

            def turn(i, r, live):
                if 3 in live:
                    pool.wait_ge(s["attn"], i - 3 + 1)
                    norm_presum(pool, ln3, i - 3, xbs[:, r, :, :])
                if 0 in live:
                    pool.wait_ge(s["x_in"], i * 16 + 16)
                    norm_presum(pool, ln0, i, x)
                    norm_rstd(pool, ln0, i, minus_half)
                if 3 in live:
                    norm_rstd(pool, ln3, i - 3, minus_half)
                if 2 in live:
                    pool.wait_ge(s["py"], i - 2 + 1)
                    xb = xbs[:, (r + 1) % 3, :, :]
                    pool.wait_ge(s["x_back"], (i - 2) * 16 + 16)
                    pool.tensor_tensor(xb, xb, ot[:, :, :].rearrange("p (k a) d -> p k (a d)", k=KT), ALU.add).then_inc(s["attn"], 1)

            turns(pool, turn)

        @block.scalar
        def _(act):
            for n, (name, a, b) in enumerate(chunks):
                act.wait_ge(s_stage[n % len(stage)], 16 * (n // len(stage) + 1))
                act.copy(hi[name][:, a:b], stage[n % len(stage)][:, 0:b - a]).then_inc(s["w_hi"], 1)
            act.wait_ge(s["pad"], 1)
            act.wait_ge(s["w_lo"], len(chunks))
            act.wait_ge(s["vec"], 16 * 5)

            def load_x(i):
                wait_reuse(act, ln0.s_mul, i)
                act.dma_start(x[:, :, :], mid[bass.ds(i, 1)].rearrange("a p k t -> p (a k) t")).then_inc(s["x_in"], 16)

            def squares(i):
                act.wait_ge(s["x_in"], i * 16 + 16)
                wait_reuse(act, s["hh"], i * KT)
                norm_square(act, ln0, i, x[:, :, :])

            def modulated(cur, dst, src, c, sh, k):
                return act.activation(dst, src[:, k, :], ACT.Identity, bias=cur[:, sh * KT + k:sh * KT + k + 1],
                                      scale=cur[:, c * KT + k:c * KT + k + 1])

            def turn(i, r, live):
                i1, i2, i3 = i - 1, i - 2, i - 3
                r1, r2 = (r + 2) % 3, (r + 1) % 3
                if 0 in live:
                    load_x(i)
                if 3 in live:
                    act.wait_ge(s["attn"], i3 + 1)
                    wait_reuse(act, s["h3"], i3 * KT)
                    norm_square(act, ln3, i3, xbs[:, r, :, :])
                if 1 in live:
                    for c in range(KT):
                        act.wait_ge(s["tqk_ps"], i1 * 4 + c + 1)
                        act.copy(tqks[:, r1, c, :], flow_ps[c][:, :]).then_inc(s["tqk"], 1)
                if 0 in live:
                    squares(i)
                if 0 in live:
                    act.wait_ge(ln0.s_add, i + 1)
                    act.wait_ge(s["cur"], i + 1)
                    wait_reuse(act, s["v_ps"], i * 2)
                    for k in range(KT):
                        modulated(curs[:, r, :], h0[:, k, :], hx0, CA, SA, k).then_inc(s["h0"], 1)
                    for k in range(KT):
                        modulated(curs[:, r, :], hh[:, k, :], hx0, CA, SA, k).then_inc(s["hh"], 1)
                if 1 in live:
                    for c in range(KT, 2 * KT):
                        act.wait_ge(s["tqk_ps"], i1 * 4 + c + 1)
                        act.copy(tqks[:, r1, c, :], flow_ps[c - KT][:, :]).then_inc(s["tqk"], 1)
                if 3 in live:
                    act.wait_ge(ln3.s_add, i3 + 1)
                    wait_reuse(act, s["xk"], i3)
                    for k in range(KT):
                        modulated(cur3[:, :], h3[:, k, 1:T + 1], hx3, CB, SB, k).then_inc(s["h3"], 1)
                if 2 in live:
                    wait_reuse(act, s["attn"], i2)
                    wait_reuse(act, s["stored"], i3 * 16)
                    act.dma_start(xbs[:, r2, :, :], mid[bass.ds(i2, 1)].rearrange("a p k t -> p (a k) t")).then_inc(s["x_back"], 16)
                if 0 in live:
                    for c in range(KT):
                        act.wait_ge(s["qk_ps"], i * 4 + c + 1)
                        act.activation(qks[:, r, c, :], qkv_ps[c][:, :], ACT.Sigmoid, bias=qkb[:, c:c + 1],
                                       accum_out=qsums[:, r, c:c + 1]).then_inc(s["qk"], 1)
                if 3 in live:
                    act.wait_ge(s["xr"], i3 + 1)
                    act.copy(rh[:, :, :], xr[:, :, :]).then_inc(s["rh"], 1)
                    act.wait_ge(s["xk"], i3 + 1)
                    wait_reuse(act, s["v2"], i3 * KT)
                    act.copy(kh[:, :, :], xk[:, :, :]).then_inc(s["kh"], 1)
                    for m in range(KT):
                        act.wait_ge(s["r_ps"], i3 * KT + m + 1)
                        act.activation(rg[:, m, :], mix_ps[m][:, :], ACT.Sigmoid).then_inc(s["rg"], 1)
                if 0 in live:
                    for c in range(KT, 2 * KT):
                        act.wait_ge(s["qk_ps"], i * 4 + c + 1)
                        act.activation(qks[:, r, c, :], qkv_ps[c - KT][:, :], ACT.Sigmoid, bias=qkb[:, c:c + 1],
                                       accum_out=qsums[:, r, c:c + 1]).then_inc(s["qk"], 1)
                if 2 in live:
                    for g in range(KT):
                        act.wait_ge(s["oT"], i2 * KT + g + 1)
                        act.copy(oh[:, g, :], out_ps[g][:, :]).then_inc(s["oh"], 1)
                if 3 in live:
                    act.wait_ge(s["k2"], i3 + 1)
                    act.copy(kh[:, :, :], xk[:, :, :]).then_inc(s["k2h"], 1)
                if 1 in live:
                    act.wait_ge(s["clip"], i1 + 1)
                    for a in range(2):
                        act.activation(ecs[:, r1, a, :, :], cs[:, a, :, :], ACT.Exp, scale=(-1.0, 1.0)[a]).then_inc(s["ex"], 1)
                if 3 in live:
                    act.wait_ge(s["y"], i3 + 1)
                    act.dma_start(x_out[bass.ds(i3, 1)].rearrange("a p k t -> p (a k) t"), xbs[:, r, :, :]).then_inc(s["stored"], 16)

            turns(act, turn)
            act.wait_ge(s["stored"], 16 * NS)

        @block.vector
        def _(dve):
            for n, (name, a, b) in enumerate(chunks):
                dve.wait_ge(s["w_hi"], n + 1)
                dve.tensor_tensor(lo[name][:, a:b], stage[n % len(stage)][:, 0:b - a], hi[name][:, a:b].bitcast(F32),
                                  ALU.subtract).then_inc(s["w_lo"], 1)
            dve.wait_ge(s["w_lo"], len(chunks))
            dve.wait_ge(s["vec"], 16 * 5)
            dve.wait_ge(s["mask"], 6)

            def turn(i, r, live):
                i1, i2, i3 = i - 1, i - 2, i - 3
                r1, r2 = (r + 2) % 3, (r + 1) % 3
                if 3 in live:
                    wait_reuse(dve, s["h3"], i3 * KT)
                    wait_reuse(dve, s["y"], i3)
                    dve.tensor_copy(cur3[:, :], curs[:, r, :]).then_inc(s["cur3"], 1)
                if 0 in live:
                    if 3 in live:
                        dve.wait_ge(s["cur3"], i3 + 1)
                    dve.tensor_copy(curs[:, r, :], mod[:, bass.ds(i, 1), :].rearrange("p a c -> p (a c)")).then_inc(s["cur"], 1)
                if 3 in live:
                    norm_presum_squares(dve, ln3, i3)
                if 1 in live:
                    dve.wait_ge(s["qk"], i1 * 4 + 4)
                    wait_reuse(dve, s["s3"], i1)
                    dve.tensor_scalar(qke[:, :, :], qks[:, r1, :, :], EPS, None, ALU.add).then_inc(s["qke"], 1)
                    dve.tensor_scalar(qsume[:, :], qsums[:, r1, :], EPS, None, ALU.add).then_inc(s["sume"], 1)
                    dve.wait_ge(s["sume"], i1 + 1)
                    for c in range(2 * KT):
                        last = dve.tensor_scalar(kd[:, c, :], mask8[:, :], qsume[:, c:c + 1], None, ALU.mult)
                    last.then_inc(s["kd"], 1)
                if 2 in live:
                    v, ec = vs[:, r2, :, :], ecs[:, r2, :, :, :]
                    dve.wait_ge(s["ex"], i2 * 2 + 2)
                    dve.tensor_scalar(sa1[:, :, :], ec[:, 0, :, :], 1.0, None, ALU.add).then_inc(s["sa1"], 1)
                    dve.wait_ge(s["esum"], i2 + 1)
                    dve.reciprocal(rs[:, :], out_ps[1][:, 0:H]).then_inc(s["rs"], 1)
                    dve.wait_ge(s["rs"], i2 + 1)
                    dve.scalar_tensor_tensor(out=sc[:, :, :], in0=ec[:, 1, :, :], scalar=float(T),
                                             in1=bc(rs[:, :].unsqueeze(1), [P, TT, H]), op0=ALU.mult, op1=ALU.mult).then_inc(s["sc"], 1)
                    dve.wait_ge(s["sa1"], i2 + 1)
                    dve.reciprocal(sa1[:, :, :], sa1[:, :, :]).then_inc(s["sar"], 1)
                    dve.wait_ge(s["sc"], i2 + 1)
                    dve.wait_ge(s["v"], i2 * 2 + 2)
                    vv = v.rearrange("p t (h d) -> p (t h) d", d=HD)
                    dve.tensor_tensor(vv, vv, bc(sc[:, :, :].rearrange("p t h -> p (t h)").unsqueeze(2), [P, TT * H, HD]),
                                      ALU.mult).then_inc(s["vc"], 1)
                    dve.wait_ge(s["sar"], i2 + 1)
                    dve.tensor_tensor(fo[:, :, :], sa1[:, :, :], sis[:, r2, 0, :, :], ALU.mult).then_inc(s["fo"], 1)
                if 0 in live:
                    norm_presum_squares(dve, ln0, i)
                    norm_stats(dve, ln0, i, qkv_ps[0])
                if 3 in live:
                    norm_stats(dve, ln3, i3, mix_ps[0])
                if 0 in live:
                    norm_minus_mean(dve, ln0, i)
                if 3 in live:
                    norm_minus_mean(dve, ln3, i3)
                if 0 in live:
                    norm_apply(dve, ln0, i, x, qkv_ps)
                if 2 in live:
                    dve.wait_ge(s["kv_ps"], i2 + 1)
                    dve.tensor_tensor(kv[:, :, :], out_ps[0][:, 0:D].rearrange("p (g c) -> p g c", g=KT),
                                      bc(bd[:, :].unsqueeze(1), [P, KT, P]), ALU.mult).then_inc(s["kv"], 1)
                if 3 in live:
                    norm_apply(dve, ln3, i3, xbs[:, r, :, :], mix_ps)
                if 0 in live:
                    dve.wait_ge(s["h0"], i * KT + KT)
                    dve.wait_ge(s["hh"], i * KT + KT)
                    dve.tensor_tensor(hl[:, :, :], h0[:, :, :], hh[:, :, :].bitcast(F32), ALU.subtract).then_inc(s["hl"], 1)
                if 3 in live:
                    dve.wait_ge(s["h3"], i3 * KT + KT)
                    dve.tensor_tensor(dx[:, :, :], h3[:, :, 1:T + 1], h3[:, :, 0:T], ALU.subtract).then_inc(s["dx"], 1)
                    dve.wait_ge(s["dx"], i3 + 1)
                    for dst, mu, done in ((xr, mur, "xr"), (xk, muk, "xk")):
                        for k in range(KT):
                            last = dve.scalar_tensor_tensor(out=dst[:, k, :], in0=dx[:, k, :], scalar=mu[:, k:k + 1],
                                                            in1=h3[:, k, 0:T], op0=ALU.mult, op1=ALU.add)
                        last.then_inc(s[done], 1)
                if 1 in live:
                    dve.wait_ge(s["s1"], i1 + 1)
                    dve.reciprocal(sis[:, r1, :, :, :].rearrange("p a t h -> p (a t h)"), flow_ps[0][:, 0:2 * TT * H]).then_inc(s["si"], 1)
                if 2 in live:
                    for g in range(KT):
                        dve.wait_ge(s["o_ps"], i2 * KT + g + 1)
                        dve.wait_ge(s["fo"], i2 + 1)
                        dve.tensor_tensor(ot[:, :, g * P:(g + 1) * P].rearrange("p t (h d) -> p t h d", d=HD),
                                          out_ps[g][:, :].rearrange("p (t h d) -> p t h d", t=TT, d=HD),
                                          bc(fo[:, :, g * HG:(g + 1) * HG].unsqueeze(3), [P, TT, HG, HD]), ALU.mult).then_inc(s["ot"], 1)
                if 3 in live:
                    dve.wait_ge(s["rh"], i3 + 1)
                    dve.tensor_tensor(rl[:, :, :], xr[:, :, :], rh[:, :, :].bitcast(F32), ALU.subtract).then_inc(s["rl"], 1)
                    dve.wait_ge(s["kh"], i3 + 1)
                    dve.tensor_tensor(kl[:, :, :], xk[:, :, :], kh[:, :, :].bitcast(F32), ALU.subtract).then_inc(s["kl"], 1)
                if 1 in live:
                    dve.wait_ge(s["s2"], i1 + 1)
                    dve.scalar_tensor_tensor(out=kd2[:, :, :], in0=flow_ps[1][:, 0:2 * KT * HG].rearrange("p (c e) -> p c e", e=HG),
                                             scalar=EPS, in1=bc(mask8[:, :].unsqueeze(1), [P, 2 * KT, HG]), op0=ALU.add,
                                             op1=ALU.mult).then_inc(s["kd2"], 1)
                if 2 in live:
                    for g in range(KT):
                        dve.wait_ge(s["oh"], i2 * KT + g + 1)
                        dve.tensor_tensor(ol[:, g, :], out_ps[g][:, :], oh[:, g, :].bitcast(F32), ALU.subtract).then_inc(s["ol"], 1)
                if 3 in live:
                    for m in range(KT):
                        dve.wait_ge(s["k_ps"], i3 * KT + m + 1)
                        last = dve.tensor_scalar(dx[:, m, :], mix_ps[m][:, :], 0.0, None, ALU.max)
                    last.then_inc(s["relu"], 1)
                    dve.wait_ge(s["relu"], i3 + 1)
                    dve.tensor_tensor(xk[:, :, :], dx[:, :, :], dx[:, :, :], ALU.mult).then_inc(s["k2"], 1)
                if 0 in live:
                    for j in range(2):
                        dve.wait_ge(s["v_ps"], i * 2 + j + 1)
                        dve.tensor_tensor(vs[:, r, 2 * j:2 * j + 2, :], qkv_ps[j][:, :].rearrange("p (a c) -> p a c", a=2),
                                          bc(vb[:, :].unsqueeze(1), [P, 2, D]), ALU.add).then_inc(s["v"], 1)
                if 1 in live:
                    dve.wait_ge(s["s3"], i1 + 1)
                    dve.tensor_scalar(cs[:, :, :, :].rearrange("p a t h -> p (a t h)"), flow_ps[0][:, 0:2 * TT * H], EPS, None,
                                      ALU.add).then_inc(s["cse"], 1)
                    dve.wait_ge(s["cse"], i1 + 1)
                    dve.tensor_scalar(cs[:, 1, :, :], cs[:, 1, :, :], -1.0, 1.0, ALU.max, ALU.min).then_inc(s["clip"], 1)
                if 3 in live:
                    dve.wait_ge(s["k2h"], i3 + 1)
                    dve.wait_ge(s["k2"], i3 + 1)
                    dve.tensor_tensor(kl[:, :, :], xk[:, :, :], kh[:, :, :].bitcast(F32), ALU.subtract).then_inc(s["k2l"], 1)
                if 2 in live:
                    for m in range(KT):
                        dve.wait_ge(s["proj"], i2 * KT + m + 1)
                        last = dve.tensor_scalar(ot[:, 2 * m:2 * m + 2, :].rearrange("p a d -> p (a d)"), out_ps[m][:, :],
                                                 pb[:, m:m + 1], curs[:, r2, GA * KT + m:GA * KT + m + 1], ALU.add, ALU.mult)
                    last.then_inc(s["py"], 1)
                if 3 in live:
                    dve.wait_ge(s["rg"], i3 * KT + KT)
                    for m in range(KT):
                        dve.wait_ge(s["v2"], i3 * KT + m + 1)
                        last = dve.tensor_tensor(dx[:, m, :], mix_ps[m][:, :], rg[:, m, :], ALU.mult)
                    last.then_inc(s["vr"], 1)
                    dve.wait_ge(s["vr"], i3 + 1)
                    for m in range(KT):
                        last = dve.scalar_tensor_tensor(out=xbs[:, r, m, :], in0=dx[:, m, :],
                                                        scalar=cur3[:, GB * KT + m:GB * KT + m + 1],
                                                        in1=xbs[:, r, m, :], op0=ALU.mult, op1=ALU.add)
                    last.then_inc(s["y"], 1)

            turns(dve, turn)

        @block.tensor
        def _(pe):
            pe.wait_ge(s["w_lo"], len(chunks))

            def qk_products(i, cs_):
                for c in cs_:
                    if c >= KT:
                        pe.wait_ge(s["qk"], i * 4 + c - KT + 1)
                    for k in range(KT):
                        mm = mm3(pe, qkv_ps[c % KT][:, :], *wt("qkv", 3 * D, k, c), hh[:, k, :], hl[:, k, :], k == 0, k == KT - 1)
                    mm.then_inc(s["qk_ps"], 1)

            def v_products(i):
                for t in range(TT):
                    tok = slice(t * P, (t + 1) * P)
                    if t % 2 == 0:
                        pe.wait_ge(s["qk"], i * 4 + KT + t // 2 + 1)
                    for k in range(KT):
                        wh, wl = wt("qkv", 3 * D, k, 2 * KT, D)
                        mm = mm3(pe, qkv_ps[t // 2][:, (t % 2) * D:(t % 2 + 1) * D], hh[:, k, tok], hl[:, k, tok], wh, wl,
                                 k == 0, k == KT - 1)
                    if t % 2:
                        mm.then_inc(s["v_ps"], 1)

            def turn_qk(i, r, cs_):
                for c in cs_:
                    if c >= KT:
                        pe.wait_ge(s["tqk"], i * 4 + c - KT + 1)
                    pe.wait_ge(s["qk"], i * 4 + c + 1)
                    for t in range(TT):
                        mm = pe.transpose(flow_ps[c % KT][:, t * P:(t + 1) * P], qks[:, r, c, t * P:(t + 1) * P], ident)
                    mm.then_inc(s["tqk_ps"], 1)

            def flows(i, rhs, ready):
                for a in range(2):
                    for g in range(KT):
                        for t in range(TT):
                            o = (a * TT + t) * H + g * HG
                            mm = pe.matmul(flow_ps[0][:, o:o + HG], qke[:, 2 * a + g, t * P:(t + 1) * P],
                                           rhs[:, 2 * (1 - a) + g, :], start=True, stop=True)
                mm.then_inc(s[ready], 1)

            def mix(i, name, xh, xl, ready):
                for m in range(KT):
                    for k in range(KT):
                        mm = mm3(pe, mix_ps[m][:, :], *wt(name, D, k, m), xh[:, k, :], xl[:, k, :], k == 0, k == KT - 1)
                    mm.then_inc(s[ready], 1)

            def turn(i, r, live):
                i1, i2, i3 = i - 1, i - 2, i - 3
                r1, r2 = (r + 2) % 3, (r + 1) % 3
                if 1 in live:
                    wait_reuse(pe, s["clip"], i1)
                    turn_qk(i1, r1, range(KT))
                if 2 in live:
                    pe.wait_ge(s["ex"], i2 * 2 + 2)
                    wait_reuse(pe, s["py"], i2)
                    for t in range(TT):
                        mm = pe.matmul(out_ps[1][:, 0:H], ones, ecs[:, r2, 1, t, :], start=(t == 0), stop=(t == TT - 1))
                    mm.then_inc(s["esum"], 1)
                if 0 in live:
                    wait_reuse(pe, s["v"], i * 2)
                    norm_sums(pe, ln0, i, qkv_ps[0], ones)
                if 3 in live:
                    wait_reuse(pe, s["vr"], i3)
                    norm_sums(pe, ln3, i3, mix_ps[0], ones)
                if 1 in live:
                    turn_qk(i1, r1, range(KT, 2 * KT))
                if 0 in live:
                    norm_spread(pe, ln0, i, qkv_ps, ident)
                if 2 in live:
                    pe.wait_ge(s["vc"], i2 + 1)
                    pe.wait_ge(s["tqk"], i2 * 4 + 4)
                    for g in range(KT):
                        for t in range(TT):
                            mm = pe.matmul(out_ps[0][:, g * P:(g + 1) * P], tqks[:, r2, KT + g, t * P:(t + 1) * P],
                                           vs[:, r2, t, g * P:(g + 1) * P], start=(t == 0), stop=(t == TT - 1))
                    mm.then_inc(s["kv_ps"], 1)
                if 3 in live:
                    norm_spread(pe, ln3, i3, mix_ps, ident)
                if 1 in live:
                    pe.wait_ge(s["qke"], i1 + 1)
                    pe.wait_ge(s["kd"], i1 + 1)
                    pe.wait_ge(s["tqk"], i1 * 4 + 4)
                    flows(i1, kd, "s1")
                if 2 in live:
                    pe.wait_ge(s["kv"], i2 + 1)
                    for g in range(KT):
                        for t in range(TT):
                            mm = pe.matmul(out_ps[g][:, t * P:(t + 1) * P], qks[:, r2, g, t * P:(t + 1) * P], kv[:, g, :],
                                           start=True, stop=True)
                        mm.then_inc(s["o_ps"], 1)
                if 0 in live:
                    pe.wait_ge(s["hl"], i + 1)
                    qk_products(i, range(KT))
                if 3 in live:
                    pe.wait_ge(s["rl"], i3 + 1)
                    mix(i3, "Wr", rh, rl, "r_ps")
                if 1 in live:
                    pe.wait_ge(s["si"], i1 + 1)
                    for c in range(2 * KT):
                        a, g = c // KT, c % KT
                        for t in range(TT):
                            mm = pe.matmul(flow_ps[1][:, c * HG:(c + 1) * HG], tqks[:, r1, c, t * P:(t + 1) * P],
                                           sis[:, r1, a, t, g * HG:(g + 1) * HG], start=(t == 0), stop=(t == TT - 1))
                    mm.then_inc(s["s2"], 1)
                if 2 in live:
                    for g in range(KT):
                        pe.wait_ge(s["ot"], i2 * KT + g + 1)
                        for t in range(TT):
                            mm = pe.transpose(out_ps[g][:, t * P:(t + 1) * P], ot[:, t, g * P:(g + 1) * P], ident)
                        mm.then_inc(s["oT"], 1)
                if 0 in live:
                    qk_products(i, range(KT, 2 * KT))
                if 3 in live:
                    pe.wait_ge(s["kl"], i3 + 1)
                    pe.wait_ge(s["rg"], i3 * KT + KT)
                    mix(i3, "Wk", kh, kl, "k_ps")
                if 1 in live:
                    pe.wait_ge(s["kd2"], i1 + 1)
                    flows(i1, kd2, "s3")
                if 2 in live:
                    pe.wait_ge(s["ol"], i2 * KT + KT)
                    for m in range(KT):
                        for k in range(KT):
                            mm = mm3(pe, out_ps[m][:, :], *wt("proj", D, k, m), oh[:, k, :], ol[:, k, :], k == 0, k == KT - 1)
                        mm.then_inc(s["proj"], 1)
                if 0 in live:
                    v_products(i)
                if 3 in live:
                    pe.wait_ge(s["k2l"], i3 + 1)
                    mix(i3, "Wv", kh, kl, "v2")

            turns(pe, turn)


def modulation(nc, sems, conds, wmods, mods, const):
    ident, ident16, ones, minus_half = const
    N = 6 * KT
    with ExitStack() as ctx:
        def sb(name, shape, dt=F32):
            return ctx.enter_context(nc.sbuf_tensor("m_" + name, shape, dt))

        def sem(name):
            sems.append(nc.alloc_semaphore("m_" + name))
            return sems[-1]

        c_sb = [sb(f"c{l}", [P, KT, NS]) for l in range(2)]
        w_sb = [sb(f"w{l}", [P, KT, 6 * D]) for l in range(2)]
        mag = sb("mag", [P, NS, KT])
        sign = sb("sign", [P, NS, KT])
        ps = [ctx.enter_context(nc.psum_tensor(f"m_bank{l}", [P, N * NS], F32)) for l in range(2)]
        loaded, silu, product, chain, const_ready = (sem(n) for n in ("loaded", "silu", "product", "chain", "const"))
        block = ctx.enter_context(nc.Block())

        @block.sync
        def _(sp_):
            for l in range(2):
                sp_.dma_start(c_sb[l][:, :, :], conds[l]).then_inc(loaded, 16)
                sp_.dma_start(w_sb[l][:, :, :], wmods[l]).then_inc(loaded, 16)

        @block.gpsimd
        def _(pool):
            pool.memset(ones[:, :], 1.0).then_inc(const_ready, 1)
            pool.memset(minus_half[:, :], -0.5).then_inc(const_ready, 1)
            pool.memset(ident[:, :], 0.0).then_inc(const_ready, 1)
            pool.memset(ident16[:, :], 0.0).then_inc(const_ready, 1)
            pool.wait_ge(const_ready, 4)
            for m in (ident, ident16):
                pool.affine_select(out=m[:, :], in_=m[:, :], compare_op=ALU.not_equal, fill=1.0, base=0, pattern=[[-1, P]],
                                   channel_multiplier=1).then_inc(const_ready, 1)

        @block.scalar
        def _(act):
            act.wait_ge(loaded, 64)
            for l in range(2):
                act.activation(c_sb[l][:, :, :], c_sb[l][:, :, :], ACT.Silu).then_inc(silu, 1)

        @block.tensor
        def _(pe):
            for l in range(2):
                pe.wait_ge(silu, l + 1)
                for n in range(N):
                    for k in range(KT):
                        mm = pe.matmul(ps[l][:, n * NS:(n + 1) * NS], w_sb[l][:, k, n * P:(n + 1) * P], c_sb[l][:, k, :],
                                       start=(k == 0), stop=(k == KT - 1))
                mm.then_inc(product, 1)

        @block.vector
        def _(dve):
            done = 0
            for l in range(2):
                dve.wait_ge(product, l + 1)
                dve.tensor_copy(mods[l][:, :, :].rearrange("p s n -> p n s"),
                                ps[l][:, :].rearrange("p (n s) -> p n s", s=NS)).then_inc(chain, 1)
                done += 1
                for row in (CA, CB):
                    dve.wait_ge(chain, done)
                    a = mods[l][:, :, row * KT:(row + 1) * KT]
                    dve.tensor_scalar(a, a, 1.0, None, ALU.add).then_inc(chain, 1)
                    done += 1
                for row in (GA, GB):
                    a = mods[l][:, :, row * KT:(row + 1) * KT]
                    dve.wait_ge(chain, done)
                    dve.scalar_tensor_tensor(out=mag[:, :, :], in0=a, scalar=-1.0, in1=a, op0=ALU.mult, op1=ALU.max).then_inc(chain, 1)
                    dve.tensor_scalar(sign[:, :, :], a, 0.0, 2.0, ALU.is_ge, ALU.mult).then_inc(chain, 1)
                    dve.wait_ge(chain, done + 2)
                    dve.tensor_scalar(mag[:, :, :], mag[:, :, :], GATE_MIN, None, ALU.max).then_inc(chain, 1)
                    dve.wait_ge(chain, done + 3)
                    dve.scalar_tensor_tensor(out=a, in0=sign[:, :, :], scalar=-1.0, in1=mag[:, :, :], op0=ALU.add,
                                             op1=ALU.mult).then_inc(chain, 1)
                    done += 4


def clear(nc, sems):
    nc.all_engine_barrier()
    nc.clear_and_free_semaphores(sems)
    nc.all_engine_barrier()
    sems.clear()


def program(nc, a, x_out):
    mid = nc.dram_tensor("mid", (NS, P, KT, T), F32, kind="Internal").ap()
    with ExitStack() as ctx:
        def sb(name, shape, dt=F32):
            return ctx.enter_context(nc.sbuf_tensor(name, shape, dt))

        ident_t, ident16_t, ones_t = sb("ident", [P, P]), sb("ident16", [P, P], BF16), sb("ones", [P, P])
        half_t = sb("minus_half", [P, TT])
        const = (ident_t[:, :], ident16_t[:, :], ones_t[:, :], half_t[:, :])
        mods = [sb(f"mod{l}", [P, NS, 6 * KT]) for l in range(2)]
        sems = []
        modulation(nc, sems, (a["c0"], a["c1"]), (a["wmod0"], a["wmod1"]), mods, const)
        clear(nc, sems)
        first_layer(nc, sems, a["x"], mid, a, mods[0], const)
        clear(nc, sems)
        second_layer(nc, sems, mid, x_out, a, mods[1], const)



def _rows_down(m):
    k, n = m.shape
    return np.ascontiguousarray(m.reshape(k // P, P, n).transpose(1, 0, 2).reshape(P, -1))


def _vec(v):
    return np.ascontiguousarray(np.asarray(v).reshape(-1, P).T)


def kernel(**inputs):
    import concourse.bacc as _bacc
    from concourse.bass_utils import run_bass_kernel_spmd as _run

    g = {k: np.asarray(v) for k, v in inputs.items()}
    experts_in = lambda m: m.reshape(E * R, -1).T
    experts_out = lambda m: m.transpose(0, 2, 1).reshape(E * R, -1)
    x = g["L0_attn_x"].transpose(0, 2, 1).reshape(NS, KT, P, T).transpose(0, 2, 1, 3)
    host = {
        "x": np.ascontiguousarray(x),
        "c0": _rows_down(g["L0_c"].T).reshape(P, KT, NS),
        "c1": _rows_down(g["L1_c"].T).reshape(P, KT, NS),
        "wmod0": _rows_down(g["L0_wmod"]).reshape(P, KT, 6 * D),
        "wmod1": _rows_down(g["L1_wmod"]).reshape(P, KT, 6 * D),
        "W1": _rows_down(g["L0_attn_W1"].T),
        "b1": _vec(g["L0_attn_b1"]),
        "w2": _vec(g["L0_attn_w2"]),
        "b2": np.ascontiguousarray(np.broadcast_to(g["L0_attn_b2"].reshape(1, 1), (P, 1))),
        "Wc": _rows_down(g["L0_attn_Wc"].T),
        "bc": _vec(g["L0_attn_bc"]),
        "gate_w": _rows_down(g["L0_ffn_gate_w"].T).reshape(P, KT, E),
        "Wg": _rows_down(g["L0_ffn_w_gate"].T),
        "Wu": _rows_down(g["L0_ffn_w_up"].T),
        "Wd": _rows_down(g["L0_ffn_w_down"].T),
        "A1": _rows_down(experts_in(g["L0_ffn_A1"])),
        "A3": _rows_down(experts_in(g["L0_ffn_A3"])),
        "A2": _rows_down(experts_in(g["L0_ffn_A2"])),
        "B1": _rows_down(experts_out(g["L0_ffn_B1"])),
        "B3": _rows_down(experts_out(g["L0_ffn_B3"])),
        "B2": _rows_down(experts_out(g["L0_ffn_B2"])),
        "qkv": _rows_down(g["L1_attn_qkv_w"].T),
        "qk_bias": _vec(g["L1_attn_qkv_b"][:2 * D]),
        "v_bias": np.ascontiguousarray(g["L1_attn_qkv_b"][2 * D:].reshape(1, D)),
        "proj": _rows_down(g["L1_attn_proj_w"].T),
        "proj_bias": _vec(g["L1_attn_proj_b"]),
        "Wr": _rows_down(g["L1_ffn_W_r"].T),
        "Wk": _rows_down(g["L1_ffn_W_k"].T),
        "Wv": _rows_down(g["L1_ffn_W_v"].T),
        "mu_r": _vec(g["L1_ffn_mu_r"]),
        "mu_k": _vec(g["L1_ffn_mu_k"]),
    }
    nc = _bacc.Bacc("TRN2", target_bir_lowering=False, num_devices=1)
    args = {n: nc.dram_tensor("in_" + n, a.shape, mybir.dt.from_np(a.dtype), kind="ExternalInput").ap()
            for n, a in host.items()}
    out = nc.dram_tensor("out", (NS, P, KT, T), F32, kind="ExternalOutput").ap()
    program(nc, args, out)
    r = _run(nc, [{"in_" + n: a for n, a in host.items()}], core_ids=[0])
    y = np.asarray(r.results[0]["out"])
    return np.ascontiguousarray(y.transpose(0, 2, 1, 3).reshape(NS, D, T).transpose(0, 2, 1))
```

```python
from contextlib import ExitStack

import numpy as np
import concourse.bass as bass
from concourse import mybir

F32 = mybir.dt.float32
F32R = mybir.dt.float32r
BF16 = mybir.dt.bfloat16
U32 = mybir.dt.uint32
ACT = mybir.ActivationFunctionType
ALU = mybir.AluOpType
AX = mybir.AxisListType

P = 128
NS = 16
T = 512
D = 256
KT = D // P
TT = T // P
E = 8
R = 16
F = 1024
FT = F // P
H = 16
HD = D // H
HG = P // HD
LN_EPS = 1e-5
EPS = 1e-6
SCALE = 2.0
GATE_MIN = 0.25

SA, CA, GA, SB, CB, GB = range(6)


def bc(ap, shape):
    return ap.to_broadcast(shape)


def wait_reuse(engine, sem, n):
    if not isinstance(n, int) or n > 0:
        engine.wait_ge(sem, n)


def mm3(pe, out, w_hi, w_lo, x_hi, x_lo, start, stop):
    pe.matmul(out, w_hi, x_hi, start=start, stop=False)
    pe.matmul(out, w_hi, x_lo, start=False, stop=False)
    return pe.matmul(out, w_lo, x_hi, start=False, stop=stop)


class Norm:

    def __init__(self, sb, sem, sq, hx, tag=""):
        self.sq = sq
        self.hx = hx
        self.xs = sb("ln_xs" + tag, [P, 2, T], F32)
        self.stat = sb("ln_stat" + tag, [P, 2, TT], F32)
        self.mm = sb("ln_mm" + tag, [P, TT], F32)
        self.var = sb("ln_var" + tag, [P, TT], F32)
        self.rstd = sb("ln_rstd" + tag, [P, 2, TT], F32)
        self.s_sq = sem("ln_sq_ready" + tag)
        self.s_xs = sem("ln_xs_ready" + tag)
        self.s_qs = sem("ln_qs_ready" + tag)
        self.s_sums = sem("ln_sums_ready" + tag)
        self.s_mean = sem("ln_mean_ready" + tag)
        self.s_mm = sem("ln_mm_ready" + tag)
        self.s_var = sem("ln_var_ready" + tag)
        self.s_rstd = sem("ln_rstd_ready" + tag)
        self.s_nmr = sem("ln_nmr_ready" + tag)
        self.s_bc = sem("ln_spread_ready" + tag)
        self.s_mul = sem("ln_mul_ready" + tag)
        self.s_add = sem("ln_add_ready" + tag)


def norm_square(act, ln, n, x):
    wait_reuse(act, ln.s_qs, n)
    act.activation(ln.sq[:, :, :], x, ACT.Square).then_inc(ln.s_sq, 1)


def norm_presum(pool, ln, n, x):
    wait_reuse(pool, ln.s_sums, n)
    pool.tensor_tensor(ln.xs[:, 0, :], x[:, 0, :], x[:, 1, :], ALU.add).then_inc(ln.s_xs, 1)


def norm_sums(pe, ln, n, bank, ones):
    pe.wait_ge(ln.s_xs, n + 1)
    pe.wait_ge(ln.s_qs, n + 1)
    for j in range(2):
        for t in range(TT):
            c = j * TT + t
            mm = pe.matmul(bank[:, c:c + 1], ln.xs[:, j, t * P:(t + 1) * P], ones[:, 0:1], start=True, stop=True)
    mm.then_inc(ln.s_sums, 1)


def norm_presum_squares(dve, ln, n):
    dve.wait_ge(ln.s_sq, n + 1)
    wait_reuse(dve, ln.s_sums, n)
    dve.tensor_tensor(ln.xs[:, 1, :], ln.sq[:, 0, :], ln.sq[:, 1, :], ALU.add).then_inc(ln.s_qs, 1)


def norm_stats(dve, ln, n, bank):
    dve.wait_ge(ln.s_sums, n + 1)
    dve.tensor_scalar(ln.stat[:, :, :].rearrange("p a t -> p (a t)"), bank[:, 0:2 * TT], 1.0 / D, None,
                      ALU.mult).then_inc(ln.s_mean, 1)
    dve.wait_ge(ln.s_mean, n + 1)
    dve.tensor_tensor(ln.mm[:, :], ln.stat[:, 0, :], ln.stat[:, 0, :], ALU.mult).then_inc(ln.s_mm, 1)
    dve.wait_ge(ln.s_mm, n + 1)
    dve.scalar_tensor_tensor(out=ln.var[:, :], in0=ln.stat[:, 1, :], scalar=LN_EPS, in1=ln.mm[:, :],
                             op0=ALU.add, op1=ALU.subtract).then_inc(ln.s_var, 1)


def norm_rstd(pool, ln, n, minus_half):
    pool.wait_ge(ln.s_var, n + 1)
    pool.tensor_tensor(ln.rstd[:, 0, :], ln.var[:, :], minus_half, ALU.pow).then_inc(ln.s_rstd, 1)


def norm_minus_mean(dve, ln, n):
    dve.wait_ge(ln.s_rstd, n + 1)
    dve.scalar_tensor_tensor(out=ln.rstd[:, 1, :], in0=ln.stat[:, 0, :], scalar=-1.0, in1=ln.rstd[:, 0, :],
                             op0=ALU.mult, op1=ALU.mult).then_inc(ln.s_nmr, 1)


def norm_spread(pe, ln, n, banks, ident):
    pe.wait_ge(ln.s_rstd, n + 1)
    pe.wait_ge(ln.s_nmr, n + 1)
    for j in range(2):
        for t in range(TT):
            mm = pe.transpose(banks[j][:, t * P:(t + 1) * P], bc(ln.rstd[:, j, t:t + 1], [P, P]), ident)
    mm.then_inc(ln.s_bc, 1)


def norm_scale(dve, ln, n, x, banks):
    dve.wait_ge(ln.s_bc, n + 1)
    for k in range(KT):
        mul = dve.tensor_tensor(ln.hx[:, k, :], x[:, k, :], banks[0][:, :], ALU.mult)
    mul.then_inc(ln.s_mul, 1)


def norm_shift(dve, ln, n, banks):
    dve.wait_ge(ln.s_mul, n + 1)
    for k in range(KT):
        add = dve.tensor_tensor(ln.hx[:, k, :], ln.hx[:, k, :], banks[1][:, :], ALU.add)
    add.then_inc(ln.s_add, 1)


def norm_apply(dve, ln, n, x, banks):
    norm_scale(dve, ln, n, x, banks)
    norm_shift(dve, ln, n, banks)


def first_layer(nc, sems, x_in, mid, w, mod, const):
    ident, ident16, ones, minus_half = const
    with ExitStack() as ctx:
        def sb(name, shape, dt=F32):
            return ctx.enter_context(nc.sbuf_tensor("a_" + name, shape, dt))

        def sem(name):
            sems.append(nc.alloc_semaphore("a_" + name))
            return sems[-1]

        gate_ps, up_ps, out_ps0, out_ps1, z_ps0, z_ps1, fr0, fr1 = [
            ctx.enter_context(nc.psum_tensor(f"a_bank{i}", [P, T], F32)) for i in range(8)]
        out_ps, z_ps, fr = (out_ps0, out_ps1), (z_ps0, z_ps1), (fr0, fr1)

        shapes = {"W1": KT * D, "Wc": 2 * KT * D, "A1": KT * P, "A3": KT * P, "Wg": KT * F, "Wu": KT * F,
                  "B1": F, "B3": F, "A2": FT * P, "Wd": FT * D, "B2": D}
        chunks = [(name, c, min(c + 1024, n)) for name, n in shapes.items() for c in range(0, n, 1024)]
        hi = {name: sb(name + "_hi", [P, n], F32R) for name, n in shapes.items()}
        lo = {name: sb(name + "_lo", [P, n], F32R) for name, n in shapes.items()}

        def wt(name, width, k, m, cols=P):
            a = k * width + m * P
            return hi[name][:, a:a + cols], lo[name][:, a:a + cols]

        gw = sb("gate_w", [P, KT, E])
        b1 = sb("b1", [P, KT])
        bcv = sb("bc", [P, KT])
        w2 = sb("w2", [P, KT])
        b2 = sb("b2", [P, 1])
        b2p = sb("b2_part", [P, 1])
        curs = sb("mod_now", [P, 2, 6 * KT])
        iota = sb("expert_no", [P, TT, E])

        x = sb("x", [P, KT, T])
        x1 = sb("x1", [P, 2, KT, T])
        h = sb("h", [P, KT, T])
        hhs = sb("h_hi", [P, 2, KT, T], F32R)
        hls = sb("h_lo", [P, 2, KT, T], F32R)
        th = sb("tanh", [P, KT, T])
        hx = sb("normed", [P, KT, T])
        ln = Norm(sb, sem, hx, hx)
        den = sb("den", [P, T])
        sp = den
        nmx = sb("score_max_neg", [P, 1])
        ex = sb("exp", [P, T])
        ch = sb("ctx_hi", [P, KT, T], F32R)
        cl = sb("ctx_lo", [P, KT, T], F32R)
        lg = sb("logits", [P, TT, E])
        top = sb("top_values", [P, TT, E])
        topi = sb("top_index", [P, TT, E], U32)
        topf = sb("top_index_f", [P, TT, 2])
        hot = sb("one_hot", [P, 2, TT, E])
        sel = sb("masks", [P, 3, TT, E * R], BF16)
        dl = sb("logit_gap", [P, TT])
        eg = sb("gap_exp", [P, TT])
        rw = sb("route_w", [P, 2, TT])
        selbs = sb("masks_spread", [P, 2, 3, T], BF16)
        rwbs = sb("route_w_spread", [P, 2, 2, T])
        um = (h[:, 0, :], h[:, 1, :], th[:, 0, :], th[:, 1, :])
        uh = sb("u_hi", [P, 4, T], F32R)
        ul = sb("u_lo", [P, 4, T], F32R)
        zm, z1 = ex, den
        zh, zl = ch[:, 0, :], cl[:, 0, :]
        sg = sb("silu", [P, 2, T])
        ah = sb("act_hi", [P, 2, T], F32R)
        al = sb("act_lo", [P, 2, T], F32R)
        cb = sb("act_sum", [P, T])
        cbh = sb("act_sum_hi", [P, T], F32R)
        cbl = sb("act_sum_lo", [P, T], F32R)
        dummy = sb("dummy", [P, 1])
        stage = [v.rearrange("p a t -> p (a t)") for v in (
            sg[:, :, :], x1[:, 1, :, :], rwbs[:, 1, :, :])]

        names = ("w_hi w_lo vec iota b2p x_in cur h_ready hh hl w1 tanh part score smax exp den prod scan "
                 "rden ctx ctxh ctxl wc tanh2 attn logits lgc settle top topi topf hot sel dif gap gapexp "
                 "gap1 rw0 rw1 spread spreadc u umul umh uml gate up silu sw aw awh awl comb combh combl "
                 "low down z0m z1m zsum zh zl out y stored").split()
        s = {n: sem(n + "_s") for n in names}
        s_stage = [sem(f"stage{n}_s") for n in range(len(stage))]
        block = ctx.enter_context(nc.Block())

        def first_front(parts, split):
            share = -(-len(chunks) // (FT - 1))
            for f in range(FT):
                for n in range(f * share, min((f + 1) * share, len(chunks))):
                    split(n)
                for at, part in parts:
                    if at[0] == f:
                        part()

        @block.sync
        def _(sp_):
            for dst, src in ((gw, w["gate_w"]), (b1, w["b1"]), (bcv, w["bc"]), (w2, w["w2"]), (b2, w["b2"])):
                sp_.dma_start(dst[tuple(slice(None) for _ in dst.shape)], src).then_inc(s["vec"], 16)
            for n, (name, a, b) in enumerate(chunks):
                if n >= len(stage):
                    sp_.wait_ge(s["w_lo"], n - len(stage) + 1)
                sp_.dma_start(stage[n % len(stage)][:, 0:b - a], w[name][:, a:b]).then_inc(s_stage[n % len(stage)], 16)

        @block.scalar
        def _(act):
            def split_hi(n):
                name, a, b = chunks[n]
                act.wait_ge(s_stage[n % len(stage)], 16 * (n // len(stage) + 1))
                act.copy(hi[name][:, a:b], stage[n % len(stage)][:, 0:b - a]).then_inc(s["w_hi"], 1)

            def load_x(i):
                wait_reuse(act, s["attn"], i * KT)
                act.dma_start(x[:, :, :], x_in[bass.ds(i, 1)].rearrange("a p k t -> p (a k) t")).then_inc(s["x_in"], 16)

            def squares(i, which, p):
                n = i * 2 + which
                if which == 0:
                    act.wait_ge(s["x_in"], i * 16 + 16)
                else:
                    act.wait_ge(s["attn"], i * KT + KT)
                wait_reuse(act, s["hh"], n * KT)
                norm_square(act, ln, n, x[:, :, :] if which == 0 else x1[:, p, :, :])

            def modulate(i, which, p):
                n = i * 2 + which
                c, sh = ((CA, SA), (CB, SB))[which]
                cur = curs[:, p, :]
                act.wait_ge(ln.s_add, n + 1)
                act.wait_ge(s["cur"], i * 2 + 2)
                if which == 0:
                    wait_reuse(act, s["uml"], i * 4)
                    wait_reuse(act, s["up"], (i - 1) * 2 * FT)
                else:
                    act.wait_ge(s["wc"], i * KT + KT)
                for dst, done in ((h[:, :, :], "h_ready"), (hhs[:, p, :, :], "hh")):
                    for k in range(KT):
                        act.activation(dst[:, k, :], hx[:, k, :], ACT.Identity, bias=cur[:, sh * KT + k:sh * KT + k + 1],
                                       scale=cur[:, c * KT + k:c * KT + k + 1]).then_inc(s[done], 1)

            def tanh(i):
                wait_reuse(act, s["uml"], i * 4)
                for m in range(KT):
                    act.wait_ge(s["w1"], i * KT + m + 1)
                    act.activation(th[:, m, :], fr[m][:, :], ACT.Tanh, bias=b1[:, m:m + 1]).then_inc(s["tanh"], 1)

            def exp(i):
                act.wait_ge(s["smax"], i + 1)
                act.activation(ex[:, :], fr0[:, :], ACT.Exp, bias=nmx[:, 0:1]).then_inc(s["exp"], 1)

            def ctx_hi(i):
                act.wait_ge(s["ctx"], i + 1)
                act.copy(ch[:, :, :], th[:, :, :]).then_inc(s["ctxh"], 1)

            def tanh_out(i):
                act.wait_ge(s["ctxl"], i + 1)
                for m in range(KT):
                    act.wait_ge(s["wc"], i * KT + m + 1)
                    act.activation(th[:, m, :], fr[m][:, :], ACT.Tanh, bias=bcv[:, m:m + 1]).then_inc(s["tanh2"], 1)

            def gap_exp(i):
                act.wait_ge(s["gap"], i + 1)
                act.activation(eg[:, :], dl[:, :], ACT.Exp).then_inc(s["gapexp"], 1)

            def spread_out(i, p, j):
                act.wait_ge(s["spread"], i * 5 + j + 1)
                dst = selbs[:, p, j, :] if j < 3 else rwbs[:, p, j - 3, :]
                act.copy(dst, fr[j % 2][:, :]).then_inc(s["spreadc"], 1)

            def front(i, p):
                return [
                    ((0, 0), lambda: squares(i, 0, p)),
                    ((1, 2), lambda: modulate(i, 0, p)),
                    ((2, 0), lambda: tanh(i)),
                    ((2, 3), lambda: exp(i)),
                    ((3, 3), lambda: ctx_hi(i)),
                    ((4, 1), lambda: tanh_out(i)),
                    ((4, 3), lambda: squares(i, 1, p)),
                    ((5, 2), lambda: modulate(i, 1, p)),
                    ((6, 0), lambda: gap_exp(i)),
                    ((6, 2), lambda: spread_out(i, p, 0)),
                    ((6, 2), lambda: spread_out(i, p, 1)),
                    ((6, 2), lambda: spread_out(i, p, 2)),
                    ((6, 4), lambda: spread_out(i, p, 3)),
                    ((6, 4), lambda: spread_out(i, p, 4)),
                ]

            def u_hi(i):
                wait_reuse(act, s["up"], i * 2 * FT)
                for q in (0, 2, 1, 3):
                    act.wait_ge(s["umul"], i * 4 + q + 1)
                    act.copy(uh[:, q, :], um[q]).then_inc(s["umh"], 1)

            def z_hi(i):
                act.wait_ge(s["zsum"], i + 1)
                act.copy(zh, zm[:, :]).then_inc(s["zh"], 1)

            def store_x(i, p):
                act.wait_ge(s["y"], i * KT + KT)
                act.dma_start(mid[bass.ds(i, 1)].rearrange("a p k t -> p (a k) t"), x1[:, p, :, :]).then_inc(s["stored"], 16)

            def steps(i, p, ahead, before):
                parts = [((0, 3), lambda: z_hi(i - 1)), ((1, 3), lambda: store_x(i - 1, 1 - p))] if before else []
                parts += front(i + 1, 1 - p) if ahead else []

                def slot(f, q):
                    for at, part in parts:
                        if at == (f, q):
                            part()

                for f in range(FT):
                    for j in range(2):
                        n = i * 2 * FT + 2 * f + j
                        act.wait_ge(s["gate"], n + 1)
                        wait_reuse(act, s["awl"], i * 2 * FT + 2 * f)
                        wait_reuse(act, s["comb"], i * FT + f)
                        act.activation(sg[:, j, :], gate_ps[:, :], ACT.Silu).then_inc(s["silu"], 1)
                        slot(f, j)
                    for j in range(2):
                        n = i * 2 * FT + 2 * f + j
                        act.wait_ge(s["aw"], n + 1)
                        wait_reuse(act, s["low"], i * FT + f)
                        act.copy(ah[:, j, :], sg[:, j, :]).then_inc(s["awh"], 1)
                        slot(f, 2 + j)
                    if ahead and f == FT - 1:
                        act.wait_ge(s["up"], (i + 1) * 2 * FT)
                        u_hi(i + 1)
                    act.wait_ge(s["comb"], i * FT + f + 1)
                    wait_reuse(act, s["down"], i * FT + f)
                    act.copy(cbh[:, :], cb[:, :]).then_inc(s["combh"], 1)
                    slot(f, 4)
                    slot(f, 5)

            load_x(0)
            first_front(front(0, 0), split_hi)
            act.wait_ge(s["w_lo"], len(chunks))
            u_hi(0)
            load_x(1)
            steps(0, 0, True, False)
            with act.Fori(0, NS // 2 - 1) as pair:
                i = pair * 2 + 1
                for d in range(2):
                    load_x(i + d + 1)
                    steps(i + d, 1 - d, True, True)
            steps(NS - 1, 1, False, True)
            z_hi(NS - 1)
            store_x(NS - 1, 1)
            act.wait_ge(s["stored"], 16 * NS)

        @block.gpsimd
        def _(pool):
            for e in range(E):
                pool.memset(iota[:, :, e:e + 1], float(e)).then_inc(s["iota"], 1)

            def presum(i, which, p):
                if which == 0:
                    pool.wait_ge(s["x_in"], i * 16 + 16)
                else:
                    pool.wait_ge(s["attn"], i * KT + KT)
                norm_presum(pool, ln, i * 2 + which, x if which == 0 else x1[:, p, :, :])

            def front(i, p):
                return [
                    ((0, 0), lambda: presum(i, 0, p)),
                    ((0, 2), lambda: norm_rstd(pool, ln, i * 2, minus_half)),
                    ((4, 1), lambda: presum(i, 1, p)),
                    ((4, 2), lambda: norm_rstd(pool, ln, i * 2 + 1, minus_half)),
                ]

            def steps(i, p, ahead):
                parts = front(i + 1, 1 - p) if ahead else []

                def slot(f, q):
                    for at, part in parts:
                        if at == (f, q):
                            part()

                for f in range(FT):
                    for j in range(2):
                        n = i * 2 * FT + 2 * f + j
                        pool.wait_ge(s["silu"], n + 1)
                        pool.wait_ge(s["spreadc"], i * 5 + 5)
                        pool.tensor_tensor(sg[:, j, :], sg[:, j, :], rwbs[:, p, j, :], ALU.mult).then_inc(s["sw"], 1)
                        slot(f, j)
                    pool.wait_ge(s["aw"], i * 2 * FT + 2 * f + 2)
                    wait_reuse(pool, s["combl"], i * FT + f)
                    pool.tensor_tensor(cb[:, :], sg[:, 0, :], sg[:, 1, :], ALU.add).then_inc(s["comb"], 1)
                    slot(f, 2)

            for _, part in front(0, 0):
                part()
            steps(0, 0, True)
            with pool.Fori(0, NS // 2 - 1) as pair:
                i = pair * 2 + 1
                for d in range(2):
                    steps(i + d, 1 - d, True)
            steps(NS - 1, 1, False)

        @block.vector
        def _(dve):
            def split_lo(n):
                name, a, b = chunks[n]
                dve.wait_ge(s["w_hi"], n + 1)
                dve.tensor_tensor(lo[name][:, a:b], stage[n % len(stage)][:, 0:b - a], hi[name][:, a:b].bitcast(F32),
                                  ALU.subtract).then_inc(s["w_lo"], 1)

            dve.wait_ge(s["vec"], 16 * 5)
            dve.tensor_scalar(b2p[:, :], b2[:, :], 1.0 / P, None, ALU.mult).then_inc(s["b2p"], 1)
            dve.wait_ge(s["b2p"], 1)
            dve.wait_ge(s["iota"], E)

            def now(i, p):
                wait_reuse(dve, s["y"], (i - 1) * KT)
                dve.tensor_copy(curs[:, p, :], mod[:, bass.ds(i, 1), :].rearrange("p a c -> p (a c)")).then_inc(s["cur"], 1)
                dve.wait_ge(s["cur"], i * 2 + 1)
                dve.tensor_copy(dummy[:, :], curs[:, p, 0:1]).then_inc(s["cur"], 1)

            def presum(i, which):
                norm_presum_squares(dve, ln, i * 2 + which)

            def stats(i, which):
                norm_stats(dve, ln, i * 2 + which, fr0)

            def minus_mean(i, which):
                norm_minus_mean(dve, ln, i * 2 + which)

            def scale(i, which, p):
                norm_scale(dve, ln, i * 2 + which, x if which == 0 else x1[:, p, :, :], fr)

            def shift(i, which):
                norm_shift(dve, ln, i * 2 + which, fr)

            def h_lo(i, which, p):
                n = i * 2 + which
                dve.wait_ge(s["h_ready"], n * KT + KT)
                dve.wait_ge(s["hh"], n * KT + KT)
                dve.tensor_tensor(hls[:, p, :, :], h[:, :, :], hhs[:, p, :, :].bitcast(F32), ALU.subtract).then_inc(s["hl"], 1)

            def score_parts(i):
                dve.wait_ge(s["tanh"], i * KT + KT)
                wait_reuse(dve, s["zsum"], i - 1)
                dve.tensor_scalar(sp[:, :], th[:, 0, :], w2[:, 0:1], b2p[:, 0:1], ALU.mult, ALU.add).then_inc(s["part"], 1)
                dve.wait_ge(s["part"], i * 2 + 1)
                dve.scalar_tensor_tensor(out=sp[:, :], in0=th[:, 1, :], scalar=w2[:, 1:2], in1=sp[:, :], op0=ALU.mult,
                                         op1=ALU.add).then_inc(s["part"], 1)

            def score_max(i):
                dve.wait_ge(s["score"], i + 1)
                dve.tensor_reduce(nmx[:, :], fr0[:, :], AX.X, ALU.max, negate=True).then_inc(s["smax"], 1)

            def products(i):
                dve.wait_ge(s["exp"], i + 1)
                dve.tensor_tensor_scan(den[:, :], ex[:, :], ex[:, :], 0.0, ALU.add, ALU.bypass).then_inc(s["den"], 1)
                for k in range(KT):
                    prod = dve.tensor_tensor(hx[:, k, :], h[:, k, :], ex[:, :], ALU.mult)
                prod.then_inc(s["prod"], 1)

            def inverse(i, t):
                tok = slice(t * P, (t + 1) * P)
                dve.wait_ge(s["den"], i + 1)
                dve.reciprocal(den[:, tok], den[:, tok]).then_inc(s["rden"], 1)

            def scans(i):
                dve.wait_ge(s["prod"], i + 1)
                for k in range(KT):
                    scan = dve.tensor_tensor_scan(th[:, k, :], hx[:, k, :], hx[:, k, :], 0.0, ALU.add, ALU.bypass)
                scan.then_inc(s["scan"], 1)

            def context(i):
                dve.wait_ge(s["rden"], i * TT + TT)
                dve.wait_ge(s["scan"], i + 1)
                for k in range(KT):
                    c = dve.tensor_tensor(th[:, k, :], th[:, k, :], den[:, :], ALU.mult)
                c.then_inc(s["ctx"], 1)

            def ctx_lo(i):
                dve.wait_ge(s["ctx"], i + 1)
                dve.wait_ge(s["ctxh"], i + 1)
                dve.tensor_tensor(cl[:, :, :], th[:, :, :], ch[:, :, :].bitcast(F32), ALU.subtract).then_inc(s["ctxl"], 1)

            def attention_out(i, p):
                for m in range(KT):
                    dve.wait_ge(s["tanh2"], i * KT + m + 1)
                    wait_reuse(dve, s["stored"], (i - 1) * 16)
                    dve.scalar_tensor_tensor(out=x1[:, p, m, :], in0=th[:, m, :],
                                             scalar=curs[:, p, GA * KT + m:GA * KT + m + 1],
                                             in1=x[:, m, :], op0=ALU.mult, op1=ALU.add).then_inc(s["attn"], 1)

            def route(i):
                dve.wait_ge(s["logits"], i + 1)
                dve.tensor_copy(lg[:, :, :].rearrange("p t e -> p (t e)"), fr0[:, 0:TT * E]).then_inc(s["lgc"], 1)
                dve.wait_ge(s["lgc"], i + 1)
                dve.tensor_copy(dummy[:, :], lg[:, 0, 0:1]).then_inc(s["settle"], 1)
                for t in range(TT):
                    mx = dve.max(top[:, t, :], lg[:, t, :])
                mx.then_inc(s["top"], 1)
                dve.wait_ge(s["settle"], i * 2 + 1)
                dve.wait_ge(s["top"], i + 1)
                dve.tensor_copy(dummy[:, :], top[:, 0, 0:1]).then_inc(s["settle"], 1)
                for t in range(TT):
                    mx = dve.max_index(topi[:, t, :], top[:, t, :], lg[:, t, :])
                mx.then_inc(s["topi"], 1)
                dve.tensor_tensor(dl[:, :], top[:, :, 1], top[:, :, 0], ALU.subtract).then_inc(s["gap"], 1)

            def route_masks(i):
                dve.wait_ge(s["settle"], i * 2 + 2)
                dve.wait_ge(s["topi"], i + 1)
                dve.tensor_copy(topf[:, :, :], topi[:, :, 0:2]).then_inc(s["topf"], 1)
                dve.wait_ge(s["topf"], i + 1)
                for j in range(2):
                    hot_ = dve.tensor_tensor(hot[:, j, :, :], iota[:, :, :], bc(topf[:, :, j:j + 1], [P, TT, E]), ALU.is_equal)
                hot_.then_inc(s["hot"], 1)
                dve.wait_ge(s["hot"], i + 1)
                dve.tensor_scalar(sel[:, 0:2, :, :].rearrange("p a t (e r) -> p (a t e) r", r=R),
                                  bc(hot[:, :, :, :].rearrange("p a t e -> p (a t e)").unsqueeze(2), [P, 2 * TT * E, R]),
                                  SCALE, None, ALU.mult).then_inc(s["sel"], 1)
                dve.wait_ge(s["sel"], i + 1)
                dve.tensor_tensor(sel[:, 2, :, :], sel[:, 1, :, :], sel[:, 0, :, :], ALU.subtract).then_inc(s["dif"], 1)

            def route_weights(i):
                dve.wait_ge(s["gapexp"], i + 1)
                dve.tensor_scalar(dl[:, :], eg[:, :], 1.0, None, ALU.add).then_inc(s["gap1"], 1)
                dve.wait_ge(s["gap1"], i + 1)
                dve.reciprocal(rw[:, 0, :], dl[:, :]).then_inc(s["rw0"], 1)
                dve.wait_ge(s["rw0"], i + 1)
                dve.tensor_tensor(rw[:, 1, :], eg[:, :], rw[:, 0, :], ALU.mult).then_inc(s["rw1"], 1)

            def mask_u(i, p, a):
                dve.wait_ge(s["u"], i * 2 + a + 1)
                dve.wait_ge(s["spreadc"], i * 5 + 5)
                dve.wait_ge(s["hl"], i * 2 + 2)
                for j in range(2):
                    dve.tensor_tensor(um[2 * a + j], fr[1 - a][:, :], selbs[:, p, 2 * j, :], ALU.mult).then_inc(s["umul"], 1)

            def front(i, p):
                return [
                    ((0, 0), lambda: presum(i, 0)),
                    ((0, 2), lambda: stats(i, 0)),
                    ((0, 3), lambda: minus_mean(i, 0)),
                    ((0, 4), lambda: scale(i, 0, p)),
                    ((0, 4), lambda: shift(i, 0)),
                    ((1, 0), lambda: now(i, p)),
                    ((1, 3), lambda: h_lo(i, 0, p)),
                    ((1, 4), lambda: score_parts(i)),
                    ((2, 2), lambda: score_max(i)),
                    ((2, 3), lambda: products(i)),
                    ((2, 3), lambda: scans(i)),
                    ((2, 4), lambda: inverse(i, 0)),
                    ((2, 4), lambda: inverse(i, 1)),
                    ((3, 0), lambda: inverse(i, 2)),
                    ((3, 1), lambda: inverse(i, 3)),
                    ((3, 2), lambda: context(i)),
                    ((3, 3), lambda: ctx_lo(i)),
                    ((4, 0), lambda: attention_out(i, p)),
                    ((4, 3), lambda: presum(i, 1)),
                    ((4, 4), lambda: stats(i, 1)),
                    ((4, 4), lambda: minus_mean(i, 1)),
                    ((5, 0), lambda: scale(i, 1, p)),
                    ((5, 0), lambda: shift(i, 1)),
                    ((5, 4), lambda: h_lo(i, 1, p)),
                    ((5, 4), lambda: route(i)),
                    ((5, 4), lambda: route_masks(i)),
                    ((6, 0), lambda: route_weights(i)),
                    ((7, 0), lambda: mask_u(i, p, 0)),
                    ((7, 0), lambda: mask_u(i, p, 1)),
                ]

            def u_lo(i):
                wait_reuse(dve, s["up"], i * 2 * FT)
                for n, q in enumerate((0, 2, 1, 3)):
                    dve.wait_ge(s["umul"], i * 4 + 4)
                    dve.wait_ge(s["umh"], i * 4 + n + 1)
                    dve.tensor_tensor(ul[:, q, :], um[q], uh[:, q, :].bitcast(F32), ALU.subtract).then_inc(s["uml"], 1)

            def z_masked(i, p):
                dve.wait_ge(s["low"], i * FT + FT)
                dve.tensor_tensor(zm[:, :], z_ps0[:, :], selbs[:, p, 0, :], ALU.mult).then_inc(s["z0m"], 1)
                dve.tensor_tensor(z1[:, :], z_ps1[:, :], selbs[:, p, 1, :], ALU.mult).then_inc(s["z1m"], 1)
                dve.wait_ge(s["z0m"], i + 1)
                dve.wait_ge(s["z1m"], i + 1)
                dve.tensor_tensor(zm[:, :], zm[:, :], z1[:, :], ALU.add).then_inc(s["zsum"], 1)

            def z_lo(i):
                dve.wait_ge(s["zsum"], i + 1)
                dve.wait_ge(s["zh"], i + 1)
                dve.tensor_tensor(zl, zm[:, :], zh.bitcast(F32), ALU.subtract).then_inc(s["zl"], 1)

            def layer_out(i, p):
                dve.wait_ge(s["out"], i + 1)
                for m in range(KT):
                    dve.scalar_tensor_tensor(out=x1[:, p, m, :], in0=out_ps[m][:, :],
                                             scalar=curs[:, p, GB * KT + m:GB * KT + m + 1],
                                             in1=x1[:, p, m, :], op0=ALU.mult, op1=ALU.add).then_inc(s["y"], 1)

            def steps(i, p, ahead, before):
                parts = [
                    ((0, 2), lambda: z_masked(i - 1, 1 - p)),
                    ((0, 3), lambda: z_lo(i - 1)),
                    ((0, 4), lambda: layer_out(i - 1, 1 - p)),
                ] if before else []
                parts += front(i + 1, 1 - p) if ahead else []

                def slot(f, q):
                    for at, part in parts:
                        if at == (f, q):
                            part()

                for f in range(FT):
                    for j in range(2):
                        n = i * 2 * FT + 2 * f + j
                        dve.wait_ge(s["up"], n + 1)
                        dve.wait_ge(s["sw"], n + 1)
                        dve.tensor_tensor(sg[:, j, :], up_ps[:, :], sg[:, j, :], ALU.mult).then_inc(s["aw"], 1)
                        slot(f, 2 * j)
                        dve.wait_ge(s["aw"], n + 1)
                        dve.wait_ge(s["awh"], n + 1)
                        dve.tensor_tensor(al[:, j, :], sg[:, j, :], ah[:, j, :].bitcast(F32), ALU.subtract).then_inc(s["awl"], 1)
                        slot(f, 2 * j + 1)
                    if ahead and f == FT - 1:
                        u_lo(i + 1)
                    dve.wait_ge(s["combh"], i * FT + f + 1)
                    dve.tensor_tensor(cbl[:, :], cb[:, :], cbh[:, :].bitcast(F32), ALU.subtract).then_inc(s["combl"], 1)
                    slot(f, 4)

            first_front(front(0, 0), split_lo)
            dve.wait_ge(s["w_lo"], len(chunks))
            u_lo(0)
            steps(0, 0, True, False)
            with dve.Fori(0, NS // 2 - 1) as pair:
                i = pair * 2 + 1
                for d in range(2):
                    steps(i + d, 1 - d, True, True)
            steps(NS - 1, 1, False, True)
            z_masked(NS - 1, 1)
            z_lo(NS - 1)
            layer_out(NS - 1, 1)

        @block.tensor
        def _(pe):
            pe.wait_ge(s["vec"], 16 * 5)

            def w1(i, p):
                pe.wait_ge(s["hl"], i * 2 + 1)
                for m in range(KT):
                    for k in range(KT):
                        mm = mm3(pe, fr[m][:, :], *wt("W1", D, k, m), hhs[:, p, k, :], hls[:, p, k, :], k == 0, k == KT - 1)
                    mm.then_inc(s["w1"], 1)

            def score(i):
                pe.wait_ge(s["part"], i * 2 + 2)
                pe.matmul(fr0[:, :], ones, sp[:, :], start=True, stop=True).then_inc(s["score"], 1)

            def combine(i, p):
                pe.wait_ge(s["exp"], i + 1)
                pe.wait_ge(s["ctxl"], i + 1)
                for m in range(KT):
                    for k in range(2 * KT):
                        xh, xl = (ch[:, k, :], cl[:, k, :]) if k < KT else (hhs[:, p, k - KT, :], hls[:, p, k - KT, :])
                        mm = mm3(pe, fr[m][:, :], *wt("Wc", D, k, m), xh, xl, k == 0, k == 2 * KT - 1)
                    mm.then_inc(s["wc"], 1)

            def logits(i):
                pe.wait_ge(s["h_ready"], i * 2 * KT + 2 * KT)
                for t in range(TT):
                    for k in range(KT):
                        mm = pe.matmul(fr0[:, t * E:(t + 1) * E], h[:, k, t * P:(t + 1) * P], gw[:, k, :], start=(k == 0),
                                       stop=(k == KT - 1))
                mm.then_inc(s["logits"], 1)

            def spread_masks(i):
                pe.wait_ge(s["hl"], i * 2 + 2)
                pe.wait_ge(s["dif"], i + 1)
                for j in range(3):
                    if j == 2:
                        pe.wait_ge(s["spreadc"], i * 5 + 1)
                    for t in range(TT):
                        mm = pe.matmul(fr[j % 2][:, t * P:(t + 1) * P], sel[:, j, t, :], ident16, start=True, stop=True)
                    mm.then_inc(s["spread"], 1)

            def spread_weights(i):
                pe.wait_ge(s["rw1"], i + 1)
                for j in range(2):
                    pe.wait_ge(s["spreadc"], i * 5 + 2 + j)
                    for t in range(TT):
                        mm = pe.transpose(fr[1 - j][:, t * P:(t + 1) * P], bc(rw[:, j, t:t + 1], [P, P]), ident)
                    mm.then_inc(s["spread"], 1)

            def low_rank_in(i, p):
                for a, name in enumerate(("A1", "A3")):
                    pe.wait_ge(s["spreadc"], i * 5 + 4 + a)
                    for k in range(KT):
                        mm = mm3(pe, fr[1 - a][:, :], *wt(name, P, k, 0), hhs[:, p, k, :], hls[:, p, k, :], k == 0, k == KT - 1)
                    mm.then_inc(s["u"], 1)

            def front(i, p):
                return [
                    ((0, 4), lambda: norm_sums(pe, ln, i * 2, fr0, ones)),
                    ((1, 1), lambda: norm_spread(pe, ln, i * 2, fr, ident)),
                    ((2, 1), lambda: w1(i, p)),
                    ((2, 4), lambda: score(i)),
                    ((4, 3), lambda: combine(i, p)),
                    ((5, 1), lambda: norm_sums(pe, ln, i * 2 + 1, fr0, ones)),
                    ((5, 3), lambda: norm_spread(pe, ln, i * 2 + 1, fr, ident)),
                    ((6, 0), lambda: logits(i)),
                    ((6, 3), lambda: spread_masks(i)),
                    ((6, 3), lambda: spread_weights(i)),
                    ((7, 2), lambda: low_rank_in(i, p)),
                ]

            def common(ps, big, f, p):
                for k in range(KT):
                    mm3(pe, ps[:, :], *wt(big, F, k, f), hhs[:, p, k, :], hls[:, p, k, :], k == 0, False)

            def slot_0(ps, small, q, f):
                return mm3(pe, ps[:, :], *wt(small, F, 0, f), uh[:, q, :], ul[:, q, :], False, True)

            def slot_1(ps, small, q, f):
                w_hi, w_lo = wt(small, F, 0, f)
                pe.matmul(ps[:, :], w_hi, uh[:, q, :], start=False, stop=False, skip_group_check=True)
                pe.matmul(ps[:, :], w_hi, ul[:, q, :], start=False, stop=False, skip_group_check=True)
                return pe.matmul(ps[:, :], w_lo, uh[:, q, :], start=False, stop=True, skip_group_check=True)

            def low_rank_out(i, f):
                for j in range(2):
                    if f == 0:
                        wait_reuse(pe, s["zsum"], i)
                    pe.wait_ge(s["awl"], i * 2 * FT + 2 * f + 1 + j)
                    mm = mm3(pe, z_ps[j][:, :], *wt("A2", P, f, 0), ah[:, j, :], al[:, j, :], f == 0, f == FT - 1)
                mm.then_inc(s["low"], 1)

            def down(i, f):
                if f == 0:
                    wait_reuse(pe, s["y"], i * KT)
                pe.wait_ge(s["combl"], i * FT + f + 1)
                for m in range(KT):
                    mm = mm3(pe, out_ps[m][:, :], *wt("Wd", D, f, m), cbh[:, :], cbl[:, :], f == 0, False)
                mm.then_inc(s["down"], 1)

            def experts_out(i):
                pe.wait_ge(s["zl"], i + 1)
                for m in range(KT):
                    b = hi["B2"][:, m * P:(m + 1) * P], lo["B2"][:, m * P:(m + 1) * P]
                    mm = mm3(pe, out_ps[m][:, :], *b, zh, zl, False, True)
                mm.then_inc(s["out"], 1)

            def steps(i, p, ahead, before):
                parts = [((1, 1), lambda: experts_out(i - 1))] if before else []
                parts += front(i + 1, 1 - p) if ahead else []

                def slot(f, q):
                    for at, part in parts:
                        if at == (f, q):
                            part()

                for f in range(FT):
                    n = i * 2 * FT + 2 * f
                    last = (i, f - 1) if f else (i - 1, FT - 1)
                    wait_reuse(pe, s["silu"], n)
                    common(gate_ps, "Wg", f, p)
                    if f:
                        slot_0(gate_ps, "B1", 0, f).then_inc(s["gate"], 1)
                    slot(f, 0)
                    wait_reuse(pe, s["aw"], n)
                    common(up_ps, "Wu", f, p)
                    if f == 0:
                        pe.wait_ge(s["uml"], i * 4 + 1)
                        slot_0(gate_ps, "B1", 0, f).then_inc(s["gate"], 1)
                        pe.wait_ge(s["uml"], i * 4 + 2)
                    slot_0(up_ps, "B3", 2, f).then_inc(s["up"], 1)
                    if f or before:
                        low_rank_out(*last)
                    slot(f, 1)
                    slot(f, 2)
                    pe.wait_ge(s["silu"], n + 1)
                    if f == 0:
                        pe.wait_ge(s["uml"], i * 4 + 4)
                    slot_1(gate_ps, "B1", 1, f).then_inc(s["gate"], 1)
                    if f or before:
                        down(*last)
                    slot(f, 3)
                    pe.wait_ge(s["aw"], n + 1)
                    slot_1(up_ps, "B3", 3, f).then_inc(s["up"], 1)
                    slot(f, 4)

            first_front(front(0, 0), lambda n: wait_reuse(pe, s["w_lo"], n - 1))
            pe.wait_ge(s["w_lo"], len(chunks))
            steps(0, 0, True, False)
            with pe.Fori(0, NS // 2 - 1) as pair:
                i = pair * 2 + 1
                for d in range(2):
                    steps(i + d, 1 - d, True, True)
            steps(NS - 1, 1, False, True)
            low_rank_out(NS - 1, FT - 1)
            down(NS - 1, FT - 1)
            experts_out(NS - 1)


def second_layer(nc, sems, mid, x_out, w, mod, const):
    ident, ident16, ones, minus_half = const
    with ExitStack() as ctx:
        def sb(name, shape, dt=F32):
            return ctx.enter_context(nc.sbuf_tensor("b_" + name, shape, dt))

        def sem(name):
            sems.append(nc.alloc_semaphore("b_" + name))
            return sems[-1]

        banks = [ctx.enter_context(nc.psum_tensor(f"b_bank{i}", [P, T], F32)) for i in range(8)]
        qkv_ps, flow_ps, out_ps, mix_ps = banks[0:2], banks[2:4], banks[4:6], banks[6:8]

        shapes = {"qkv": KT * 3 * D, "proj": KT * D, "Wr": KT * D, "Wk": KT * D, "Wv": KT * D}
        chunks = [(name, c, min(c + 1024, n)) for name, n in shapes.items() for c in range(0, n, 1024)]
        hi = {name: sb(name + "_hi", [P, n], F32R) for name, n in shapes.items()}
        lo = {name: sb(name + "_lo", [P, n], F32R) for name, n in shapes.items()}

        def wt(name, width, k, m, cols=P):
            a = k * width + m * P
            return hi[name][:, a:a + cols], lo[name][:, a:a + cols]

        qkb = sb("qk_bias", [P, 2 * KT])
        vb = sb("v_bias", [P, D])
        pb = sb("proj_bias", [P, KT])
        mur = sb("mu_r", [P, KT])
        muk = sb("mu_k", [P, KT])
        curs = sb("mod_now", [P, 3, 6 * KT])
        cur3 = sb("mod_mix", [P, 6 * KT])
        gb4 = sb("mod_last", [P, KT])
        mask8 = sb("head_mask", [P, HG])
        bd = sb("block_mask", [P, P])

        x = sb("x", [P, KT, T])
        hx0 = sb("normed0", [P, KT, T])
        ln0 = Norm(sb, sem, hx0, hx0, "0")
        h0 = sb("h0", [P, KT, T])
        hh = sb("h_hi", [P, KT, T], F32R)
        hl = sb("h_lo", [P, KT, T], F32R)
        qks = sb("qk", [P, 3, 2 * KT, T])
        qsums = sb("qk_sum", [P, 3, 2 * KT])
        vs = sb("v_tokens", [P, 3, TT, D])
        qke = sb("qk_eps", [P, 2 * KT, T])
        qsume = sb("qk_sum_eps", [P, 2 * KT])
        eps = sb("eps", [P, 1])
        kd = sb("sum_heads", [P, 2 * KT, HG])
        kd2 = sb("weighted_sum_heads", [P, 2 * KT, HG])
        tqks = sb("qk_tokens", [P, 3, 2 * KT, T])
        sis = sb("flow_inverse", [P, 3, 2, TT, H])
        cs = sb("conserved", [P, 2, TT, H])
        ecs = sb("conserved_exp", [P, 3, 2, TT, H])
        sa1 = sb("sink_gate_den", [P, TT, H])
        fo = sb("out_factor", [P, TT, H])
        rs = sb("competition_inverse", [P, H])
        sc = sb("competition", [P, TT, H])
        kv = sb("kv", [P, KT, P])
        ot = sb("out_tokens", [P, TT, D])
        oh = sb("out_hi", [P, KT, T], F32R)
        ol = sb("out_lo", [P, KT, T], F32R)
        xbs = sb("x_back", [P, 3, KT, T])
        hx3 = sb("normed3", [P, KT, T])
        ln3 = Norm(sb, sem, hx3, hx3, "3")
        h3 = sb("h3", [P, KT, T + 1])
        dx = sb("shift_gap", [P, KT, T])
        xr = sb("mix_r", [P, KT, T])
        xk = sb("mix_k", [P, KT, T])
        rh = sb("mix_r_hi", [P, KT, T], F32R)
        rl = sb("mix_r_lo", [P, KT, T], F32R)
        kh = sb("mix_k_hi", [P, KT, T], F32R)
        kl = sb("mix_k_lo", [P, KT, T], F32R)
        rg = sb("receptance", [P, KT, T])
        stage = [v.rearrange("p a t -> p (a t)") for v in (
            xr[:, :, :], xk[:, :, :], dx[:, :, :], rg[:, :, :], ot[:, :, :])]

        names = ("w_hi w_lo vec mask pad x_in x_back cur cur3 gb4 hh hl h0 h3 qk_ps qk qke sume kd tqk_ps tqk v_ps v s1 si s2 kd2 s3 "
                 "cse clip ex sa1 sar fo esum rs sc vc kv_ps kv o_ps ot oT oh ol proj py attn dx xr xk rh kh rl kl "
                 "r_ps k_ps rg relu k2 k2h k2l v2 vr y stored").split()
        s = {n: sem(n + "_s") for n in names}
        s_stage = [sem(f"stage{n}_s") for n in range(len(stage))]
        block = ctx.enter_context(nc.Block())

        sums0_ps, sums3_ps = flow_ps[1][:, P:P + 2 * TT], out_ps[1][:, P:P + 2 * TT]

        def turns(engine, turn, split):
            first, rounds = 5, (NS - 1 - 5) // 3
            live = lambda i: [lag for lag in range(-1, 5) if 0 <= i - lag < NS]
            qkv_chunks = sum(name == "qkv" for name, _, _ in chunks)
            for i in range(-1, first):
                for n in {0: range(qkv_chunks), 1: range(qkv_chunks, len(chunks))}.get(i, ()):
                    split(n)
                turn(i, i % 3, live(i))
            with engine.Fori(0, rounds) as three:
                for d in range(3):
                    turn(three * 3 + first + d, (first + d) % 3, range(-1, 5))
            for i in range(first + rounds * 3, NS + 4):
                turn(i, i % 3, live(i))

        @block.sync
        def _(sp_):
            for dst, src in ((qkb, w["qk_bias"]), (pb, w["proj_bias"]), (mur, w["mu_r"]), (muk, w["mu_k"])):
                sp_.dma_start(dst[:, :], src).then_inc(s["vec"], 16)
            sp_.dma_start(vb[:, :], bc(w["v_bias"], [P, D])).then_inc(s["vec"], 16)
            for n, (name, a, b) in enumerate(chunks):
                if n >= len(stage):
                    sp_.wait_ge(s["w_lo"], n - len(stage) + 1)
                sp_.dma_start(stage[n % len(stage)][:, 0:b - a], w[name][:, a:b]).then_inc(s_stage[n % len(stage)], 16)

        @block.gpsimd
        def _(pool):
            pool.memset(mask8[:, :], 1.0).then_inc(s["mask"], 1)
            pool.memset(bd[:, :], 1.0).then_inc(s["mask"], 1)
            pool.memset(h3[:, :, 0:1], 0.0).then_inc(s["pad"], 1)
            pool.memset(eps[:, :], EPS).then_inc(s["pad"], 1)
            pool.wait_ge(s["mask"], 2)
            pool.affine_select(out=mask8[:, :], in_=mask8[:, :], compare_op=ALU.is_ge, fill=0.0, base=0,
                               pattern=[[-HD, HG]], channel_multiplier=1).then_inc(s["mask"], 1)
            bdv = bd[:, :].rearrange("p (a b) -> p a b", a=HG)
            pool.affine_select(out=bdv, in_=bdv, compare_op=ALU.is_ge, fill=0.0, base=0,
                               pattern=[[-HD, HG], [0, HD]], channel_multiplier=1).then_inc(s["mask"], 1)
            pool.wait_ge(s["mask"], 4)
            pool.affine_select(out=mask8[:, :], in_=mask8[:, :], compare_op=ALU.is_ge, fill=0.0, base=HD - 1,
                               pattern=[[HD, HG]], channel_multiplier=-1).then_inc(s["mask"], 1)
            pool.affine_select(out=bdv, in_=bdv, compare_op=ALU.is_ge, fill=0.0, base=HD - 1,
                               pattern=[[HD, HG], [0, HD]], channel_multiplier=-1).then_inc(s["mask"], 1)

            def turn(i, r, live):
                ja, i1, i2, i3 = i + 1, i - 1, i - 2, i - 3
                r1 = (r + 2) % 3
                if 3 in live:
                    pool.wait_ge(s["py"], i3 + 1)
                    pool.wait_ge(s["x_back"], i3 * 16 + 16)
                    xb = xbs[:, r, :, :]
                    pool.tensor_tensor(xb, xb, ot[:, :, :].rearrange("p (k a) d -> p k (a d)", k=KT), ALU.add).then_inc(s["attn"], 1)
                    pool.wait_ge(s["attn"], i3 + 1)
                if 3 in live:
                    norm_presum(pool, ln3, i3, xbs[:, r, :, :])
                if -1 in live:
                    pool.wait_ge(s["x_in"], ja * 16 + 16)
                    norm_presum(pool, ln0, ja, x)
                if 3 in live:
                    norm_rstd(pool, ln3, i3, minus_half)
                if 3 in live:
                    pool.wait_ge(s["kh"], i3 + 1)
                    pool.wait_ge(s["xk"], i3 + 1)
                    pool.tensor_tensor(kl[:, :, :], xk[:, :, :], kh[:, :, :].bitcast(F32), ALU.subtract).then_inc(s["kl"], 1)
                if -1 in live:
                    norm_rstd(pool, ln0, ja, minus_half)

            turns(pool, turn, lambda n: None)

        @block.scalar
        def _(act):
            def split_hi(n):
                name, a, b = chunks[n]
                act.wait_ge(s_stage[n % len(stage)], 16 * (n // len(stage) + 1))
                act.copy(hi[name][:, a:b], stage[n % len(stage)][:, 0:b - a]).then_inc(s["w_hi"], 1)

            act.wait_ge(s["pad"], 2)
            act.wait_ge(s["vec"], 16 * 5)

            def load_x(i):
                wait_reuse(act, ln0.s_mul, i)
                act.dma_start(x[:, :, :], mid[bass.ds(i, 1)].rearrange("a p k t -> p (a k) t")).then_inc(s["x_in"], 16)

            def squares(i):
                act.wait_ge(s["x_in"], i * 16 + 16)
                wait_reuse(act, s["hh"], i * KT)
                norm_square(act, ln0, i, x[:, :, :])

            def modulated(cur, dst, src, c, sh, k):
                return act.activation(dst, src[:, k, :], ACT.Identity, bias=cur[:, sh * KT + k:sh * KT + k + 1],
                                      scale=cur[:, c * KT + k:c * KT + k + 1])

            def qk_sigmoid(i, r, cs_):
                for c in cs_:
                    act.wait_ge(s["qk_ps"], i * 4 + c + 1)
                    act.activation(qks[:, r, c, :], qkv_ps[c % KT][:, :], ACT.Sigmoid, bias=qkb[:, c:c + 1],
                                   accum_out=qsums[:, r, c:c + 1]).then_inc(s["qk"], 1)

            def tokens_down(i, r, cs_):
                for c in cs_:
                    act.wait_ge(s["tqk_ps"], i * 4 + c + 1)
                    act.copy(tqks[:, r, c, :], flow_ps[c % KT][:, :]).then_inc(s["tqk"], 1)

            def turn(i, r, live):
                ja, i1, i2, i3, i4 = i + 1, i - 1, i - 2, i - 3, i - 4
                r1, r2, r4 = (r + 2) % 3, (r + 1) % 3, (r + 2) % 3
                if 2 in live:
                    act.wait_ge(s["clip"], i2 + 1)
                    for a in range(2):
                        act.activation(ecs[:, r2, a, :, :], cs[:, a, :, :], ACT.Exp, scale=(-1.0, 1.0)[a]).then_inc(s["ex"], 1)
                if 1 in live:
                    tokens_down(i1, r1, range(KT))
                if 1 in live:
                    tokens_down(i1, r1, range(KT, 2 * KT))
                if -1 in live:
                    load_x(ja)
                if 0 in live:
                    act.wait_ge(ln0.s_add, i + 1)
                    act.wait_ge(s["cur"], i + 1)
                    wait_reuse(act, s["v_ps"], i * 2)
                    for k in range(KT):
                        modulated(curs[:, r, :], h0[:, k, :], hx0, CA, SA, k).then_inc(s["h0"], 1)
                    for k in range(KT):
                        modulated(curs[:, r, :], hh[:, k, :], hx0, CA, SA, k).then_inc(s["hh"], 1)
                if -1 in live:
                    squares(ja)
                if 2 in live:
                    wait_reuse(act, s["attn"], i2)
                    wait_reuse(act, s["stored"], i4 * 16)
                    act.dma_start(xbs[:, r2, :, :], mid[bass.ds(i2, 1)].rearrange("a p k t -> p (a k) t")).then_inc(s["x_back"], 16)
                if 3 in live:
                    act.wait_ge(s["attn"], i3 + 1)
                    wait_reuse(act, s["h3"], i3 * KT)
                    norm_square(act, ln3, i3, xbs[:, r, :, :])
                if 0 in live:
                    qk_sigmoid(i, r, range(KT))
                if 4 in live:
                    act.wait_ge(s["y"], i4 + 1)
                    act.dma_start(x_out[bass.ds(i4, 1)].rearrange("a p k t -> p (a k) t"), xbs[:, r4, :, :]).then_inc(s["stored"], 16)
                if 0 in live:
                    qk_sigmoid(i, r, range(KT, 2 * KT))
                if 3 in live:
                    act.wait_ge(ln3.s_add, i3 + 1)
                    wait_reuse(act, s["xk"], i3)
                    for k in range(KT):
                        modulated(cur3[:, :], h3[:, k, 1:T + 1], hx3, CB, SB, k).then_inc(s["h3"], 1)
                if 2 in live:
                    for g in range(KT):
                        act.wait_ge(s["oT"], i2 * KT + g + 1)
                        act.copy(oh[:, g, :], out_ps[g][:, :]).then_inc(s["oh"], 1)
                if 3 in live:
                    act.wait_ge(s["xr"], i3 + 1)
                    act.copy(rh[:, :, :], xr[:, :, :]).then_inc(s["rh"], 1)
                    act.wait_ge(s["xk"], i3 + 1)
                    wait_reuse(act, s["v2"], i3 * KT)
                    act.copy(kh[:, :, :], xk[:, :, :]).then_inc(s["kh"], 1)
                    for m in range(KT):
                        act.wait_ge(s["r_ps"], i3 * KT + m + 1)
                        act.activation(rg[:, m, :], mix_ps[m][:, :], ACT.Sigmoid).then_inc(s["rg"], 1)
                if 0 in live:
                    act.wait_ge(s["qk"], i * 4 + 2 * KT)
                    wait_reuse(act, s["s3"], i)
                    act.activation(qke[:, :, :], qks[:, r, :, :], ACT.Identity, bias=eps[:, 0:1]).then_inc(s["qke"], 1)
                if 3 in live:
                    act.wait_ge(s["k2"], i3 + 1)
                    act.copy(kh[:, :, :], xk[:, :, :]).then_inc(s["k2h"], 1)

            turns(act, turn, split_hi)
            act.wait_ge(s["stored"], 16 * NS)

        @block.vector
        def _(dve):
            def split_lo(n):
                name, a, b = chunks[n]
                dve.wait_ge(s["w_hi"], n + 1)
                dve.tensor_tensor(lo[name][:, a:b], stage[n % len(stage)][:, 0:b - a], hi[name][:, a:b].bitcast(F32),
                                  ALU.subtract).then_inc(s["w_lo"], 1)

            dve.wait_ge(s["vec"], 16 * 5)
            dve.wait_ge(s["mask"], 6)

            def turn(i, r, live):
                ja, i1, i2, i3, i4 = i + 1, i - 1, i - 2, i - 3, i - 4
                r1, r2, r4 = (r + 2) % 3, (r + 1) % 3, (r + 2) % 3
                if 4 in live:
                    dve.wait_ge(s["cur3"], i4 + 1)
                    wait_reuse(dve, s["y"], i4)
                    dve.tensor_copy(gb4[:, :], cur3[:, GB * KT:(GB + 1) * KT]).then_inc(s["gb4"], 1)
                if 3 in live:
                    wait_reuse(dve, s["h3"], i3 * KT)
                    wait_reuse(dve, s["gb4"], i3)
                    dve.tensor_copy(cur3[:, :], curs[:, r, :]).then_inc(s["cur3"], 1)
                if 0 in live:
                    if 3 in live:
                        dve.wait_ge(s["cur3"], i3 + 1)
                    dve.tensor_copy(curs[:, r, :], mod[:, bass.ds(i, 1), :].rearrange("p a c -> p (a c)")).then_inc(s["cur"], 1)
                if 4 in live:
                    dve.wait_ge(s["k2h"], i4 + 1)
                    dve.wait_ge(s["k2"], i4 + 1)
                    dve.tensor_tensor(kl[:, :, :], xk[:, :, :], kh[:, :, :].bitcast(F32), ALU.subtract).then_inc(s["k2l"], 1)
                if 0 in live:
                    norm_apply(dve, ln0, i, x, qkv_ps)
                if 2 in live:
                    v, ec = vs[:, r2, :, :], ecs[:, r2, :, :, :]
                    dve.wait_ge(s["ex"], i2 * 2 + 2)
                    dve.tensor_scalar(sa1[:, :, :], ec[:, 0, :, :], 1.0, None, ALU.add).then_inc(s["sa1"], 1)
                    dve.wait_ge(s["esum"], i2 + 1)
                    dve.reciprocal(rs[:, :], out_ps[1][:, 0:H]).then_inc(s["rs"], 1)
                    dve.wait_ge(s["rs"], i2 + 1)
                    dve.scalar_tensor_tensor(out=sc[:, :, :], in0=ec[:, 1, :, :], scalar=float(T),
                                             in1=bc(rs[:, :].unsqueeze(1), [P, TT, H]), op0=ALU.mult, op1=ALU.mult).then_inc(s["sc"], 1)
                    dve.wait_ge(s["sa1"], i2 + 1)
                    dve.reciprocal(sa1[:, :, :], sa1[:, :, :]).then_inc(s["sar"], 1)
                    dve.wait_ge(s["sc"], i2 + 1)
                    dve.wait_ge(s["v"], i2 * 2 + 2)
                    vv = v.rearrange("p t (h d) -> p (t h) d", d=HD)
                    dve.tensor_tensor(vv, vv, bc(sc[:, :, :].rearrange("p t h -> p (t h)").unsqueeze(2), [P, TT * H, HD]),
                                      ALU.mult).then_inc(s["vc"], 1)
                if 0 in live:
                    dve.wait_ge(s["h0"], i * KT + KT)
                    dve.wait_ge(s["hh"], i * KT + KT)
                    dve.tensor_tensor(hl[:, :, :], h0[:, :, :], hh[:, :, :].bitcast(F32), ALU.subtract).then_inc(s["hl"], 1)
                if 3 in live:
                    norm_presum_squares(dve, ln3, i3)
                if 2 in live:
                    dve.wait_ge(s["sar"], i2 + 1)
                    dve.tensor_tensor(fo[:, :, :], sa1[:, :, :], sis[:, r2, 0, :, :], ALU.mult).then_inc(s["fo"], 1)
                if 3 in live:
                    norm_stats(dve, ln3, i3, sums3_ps)
                if 2 in live:
                    dve.wait_ge(s["kv_ps"], i2 + 1)
                    dve.tensor_tensor(kv[:, :, :], out_ps[0][:, 0:D].rearrange("p (g c) -> p g c", g=KT),
                                      bc(bd[:, :].unsqueeze(1), [P, KT, P]), ALU.mult).then_inc(s["kv"], 1)
                if 3 in live:
                    norm_minus_mean(dve, ln3, i3)
                if 1 in live:
                    dve.wait_ge(s["s1"], i1 + 1)
                    dve.reciprocal(sis[:, r1, :, :, :].rearrange("p a t h -> p (a t h)"), flow_ps[0][:, 0:2 * TT * H]).then_inc(s["si"], 1)
                if 4 in live:
                    dve.wait_ge(s["rg"], i4 * KT + KT)
                    for m in range(KT):
                        dve.wait_ge(s["v2"], i4 * KT + m + 1)
                        last = dve.tensor_tensor(dx[:, m, :], mix_ps[m][:, :], rg[:, m, :], ALU.mult)
                    last.then_inc(s["vr"], 1)
                    dve.wait_ge(s["vr"], i4 + 1)
                    dve.wait_ge(s["gb4"], i4 + 1)
                    for m in range(KT):
                        last = dve.scalar_tensor_tensor(out=xbs[:, r4, m, :], in0=dx[:, m, :], scalar=gb4[:, m:m + 1],
                                                        in1=xbs[:, r4, m, :], op0=ALU.mult, op1=ALU.add)
                    last.then_inc(s["y"], 1)
                if 3 in live:
                    norm_apply(dve, ln3, i3, xbs[:, r, :, :], mix_ps)
                if 2 in live:
                    wait_reuse(dve, s["attn"], i2)
                    for g in range(KT):
                        dve.wait_ge(s["o_ps"], i2 * KT + g + 1)
                        dve.wait_ge(s["fo"], i2 + 1)
                        dve.tensor_tensor(ot[:, :, g * P:(g + 1) * P].rearrange("p t (h d) -> p t h d", d=HD),
                                          out_ps[g][:, :].rearrange("p (t h d) -> p t h d", t=TT, d=HD),
                                          bc(fo[:, :, g * HG:(g + 1) * HG].unsqueeze(3), [P, TT, HG, HD]), ALU.mult).then_inc(s["ot"], 1)
                if 3 in live:
                    dve.wait_ge(s["h3"], i3 * KT + KT)
                    dve.tensor_tensor(dx[:, :, :], h3[:, :, 1:T + 1], h3[:, :, 0:T], ALU.subtract).then_inc(s["dx"], 1)
                    dve.wait_ge(s["dx"], i3 + 1)
                    for dst, mu, done in ((xr, mur, "xr"), (xk, muk, "xk")):
                        for k in range(KT):
                            last = dve.scalar_tensor_tensor(out=dst[:, k, :], in0=dx[:, k, :], scalar=mu[:, k:k + 1],
                                                            in1=h3[:, k, 0:T], op0=ALU.mult, op1=ALU.add)
                        last.then_inc(s[done], 1)
                if 1 in live:
                    dve.wait_ge(s["s2"], i1 + 1)
                    dve.scalar_tensor_tensor(out=kd2[:, :, :], in0=flow_ps[1][:, 0:2 * KT * HG].rearrange("p (c e) -> p c e", e=HG),
                                             scalar=EPS, in1=bc(mask8[:, :].unsqueeze(1), [P, 2 * KT, HG]), op0=ALU.add,
                                             op1=ALU.mult).then_inc(s["kd2"], 1)
                if 3 in live:
                    dve.wait_ge(s["rh"], i3 + 1)
                    dve.tensor_tensor(rl[:, :, :], xr[:, :, :], rh[:, :, :].bitcast(F32), ALU.subtract).then_inc(s["rl"], 1)
                if -1 in live:
                    norm_presum_squares(dve, ln0, ja)
                if 0 in live:
                    for j in range(2):
                        dve.wait_ge(s["v_ps"], i * 2 + j + 1)
                        dve.tensor_tensor(vs[:, r, 2 * j:2 * j + 2, :], qkv_ps[j][:, :].rearrange("p (a c) -> p a c", a=2),
                                          bc(vb[:, :].unsqueeze(1), [P, 2, D]), ALU.add).then_inc(s["v"], 1)
                if 2 in live:
                    for g in range(KT):
                        dve.wait_ge(s["oh"], i2 * KT + g + 1)
                        dve.tensor_tensor(ol[:, g, :], out_ps[g][:, :], oh[:, g, :].bitcast(F32), ALU.subtract).then_inc(s["ol"], 1)
                if -1 in live:
                    norm_stats(dve, ln0, ja, sums0_ps)
                if 1 in live:
                    dve.wait_ge(s["s3"], i1 + 1)
                    dve.tensor_scalar(cs[:, :, :, :].rearrange("p a t h -> p (a t h)"), flow_ps[0][:, 0:2 * TT * H], EPS, None,
                                      ALU.add).then_inc(s["cse"], 1)
                    dve.wait_ge(s["cse"], i1 + 1)
                    dve.tensor_scalar(cs[:, 1, :, :], cs[:, 1, :, :], -1.0, 1.0, ALU.max, ALU.min).then_inc(s["clip"], 1)
                if -1 in live:
                    norm_minus_mean(dve, ln0, ja)
                if 3 in live:
                    for m in range(KT):
                        dve.wait_ge(s["k_ps"], i3 * KT + m + 1)
                        last = dve.tensor_scalar(dx[:, m, :], mix_ps[m][:, :], 0.0, None, ALU.max)
                    last.then_inc(s["relu"], 1)
                    dve.wait_ge(s["relu"], i3 + 1)
                    dve.wait_ge(s["kl"], i3 + 1)
                    dve.tensor_tensor(xk[:, :, :], dx[:, :, :], dx[:, :, :], ALU.mult).then_inc(s["k2"], 1)
                if 0 in live:
                    dve.wait_ge(s["qk"], i * 4 + 4)
                    dve.tensor_scalar(qsume[:, :], qsums[:, r, :], EPS, None, ALU.add).then_inc(s["sume"], 1)
                    dve.wait_ge(s["sume"], i + 1)
                    for c in range(2 * KT):
                        last = dve.tensor_scalar(kd[:, c, :], mask8[:, :], qsume[:, c:c + 1], None, ALU.mult)
                    last.then_inc(s["kd"], 1)
                if 2 in live:
                    for m in range(KT):
                        dve.wait_ge(s["proj"], i2 * KT + m + 1)
                        last = dve.tensor_scalar(ot[:, 2 * m:2 * m + 2, :].rearrange("p a d -> p (a d)"), out_ps[m][:, :],
                                                 pb[:, m:m + 1], curs[:, r2, GA * KT + m:GA * KT + m + 1], ALU.add, ALU.mult)
                    last.then_inc(s["py"], 1)

            turns(dve, turn, split_lo)

        @block.tensor
        def _(pe):
            def qk_products(i, cs_):
                for c in cs_:
                    if c >= KT:
                        pe.wait_ge(s["qk"], i * 4 + c - KT + 1)
                    for k in range(KT):
                        mm = mm3(pe, qkv_ps[c % KT][:, :], *wt("qkv", 3 * D, k, c), hh[:, k, :], hl[:, k, :], k == 0, k == KT - 1)
                    mm.then_inc(s["qk_ps"], 1)

            def v_products(i):
                for t in range(TT):
                    tok = slice(t * P, (t + 1) * P)
                    if t % 2 == 0:
                        pe.wait_ge(s["qk"], i * 4 + KT + t // 2 + 1)
                    for k in range(KT):
                        wh, wl = wt("qkv", 3 * D, k, 2 * KT, D)
                        mm = mm3(pe, qkv_ps[t // 2][:, (t % 2) * D:(t % 2 + 1) * D], hh[:, k, tok], hl[:, k, tok], wh, wl,
                                 k == 0, k == KT - 1)
                    if t % 2:
                        mm.then_inc(s["v_ps"], 1)

            def turn_qk(i, r, cs_):
                for c in cs_:
                    if c >= KT:
                        pe.wait_ge(s["tqk"], i * 4 + c - KT + 1)
                    pe.wait_ge(s["qk"], i * 4 + c + 1)
                    for t in range(TT):
                        mm = pe.transpose(flow_ps[c % KT][:, t * P:(t + 1) * P], qks[:, r, c, t * P:(t + 1) * P], ident)
                    mm.then_inc(s["tqk_ps"], 1)

            def flows(i, rhs, ready):
                for a in range(2):
                    for g in range(KT):
                        for t in range(TT):
                            o = (a * TT + t) * H + g * HG
                            mm = pe.matmul(flow_ps[0][:, o:o + HG], qke[:, 2 * a + g, t * P:(t + 1) * P],
                                           rhs[:, 2 * (1 - a) + g, :], start=True, stop=True)
                mm.then_inc(s[ready], 1)

            def mix(i, name, xh, xl, ready):
                for m in range(KT):
                    for k in range(KT):
                        mm = mm3(pe, mix_ps[m][:, :], *wt(name, D, k, m), xh[:, k, :], xl[:, k, :], k == 0, k == KT - 1)
                    mm.then_inc(s[ready], 1)

            def turn(i, r, live):
                ja, i1, i2, i3, i4 = i + 1, i - 1, i - 2, i - 3, i - 4
                r1, r2 = (r + 2) % 3, (r + 1) % 3
                if 1 in live:
                    wait_reuse(pe, s["clip"], i1)
                    if 0 in live:
                        pe.wait_ge(ln0.s_mean, i + 1)
                    turn_qk(i1, r1, range(KT))
                if 0 in live:
                    wait_reuse(pe, s["v"], i * 2)
                    norm_spread(pe, ln0, i, qkv_ps, ident)
                if 2 in live:
                    pe.wait_ge(s["ex"], i2 * 2 + 2)
                    wait_reuse(pe, s["py"], i2)
                    for t in range(TT):
                        mm = pe.matmul(out_ps[1][:, 0:H], ones, ecs[:, r2, 1, t, :], start=(t == 0), stop=(t == TT - 1))
                    mm.then_inc(s["esum"], 1)
                if 1 in live:
                    turn_qk(i1, r1, range(KT, 2 * KT))
                if 4 in live:
                    pe.wait_ge(s["k2l"], i4 + 1)
                    mix(i4, "Wv", kh, kl, "v2")
                if 1 in live:
                    pe.wait_ge(s["qke"], i1 + 1)
                    pe.wait_ge(s["kd"], i1 + 1)
                    pe.wait_ge(s["tqk"], i1 * 4 + KT + 1)
                    flows(i1, kd, "s1")
                if 2 in live:
                    pe.wait_ge(s["vc"], i2 + 1)
                    pe.wait_ge(s["tqk"], i2 * 4 + 4)
                    for g in range(KT):
                        for t in range(TT):
                            mm = pe.matmul(out_ps[0][:, g * P:(g + 1) * P], tqks[:, r2, KT + g, t * P:(t + 1) * P],
                                           vs[:, r2, t, g * P:(g + 1) * P], start=(t == 0), stop=(t == TT - 1))
                    mm.then_inc(s["kv_ps"], 1)
                if 3 in live:
                    norm_sums(pe, ln3, i3, sums3_ps, ones)
                if 0 in live:
                    pe.wait_ge(s["hl"], i + 1)
                    qk_products(i, range(KT))
                if 2 in live:
                    pe.wait_ge(s["kv"], i2 + 1)
                    if 3 in live:
                        pe.wait_ge(ln3.s_mean, i3 + 1)
                    for g in range(KT):
                        for t in range(TT):
                            mm = pe.matmul(out_ps[g][:, t * P:(t + 1) * P], qks[:, r2, g, t * P:(t + 1) * P], kv[:, g, :],
                                           start=True, stop=True)
                        mm.then_inc(s["o_ps"], 1)
                if 3 in live:
                    wait_reuse(pe, s["vr"], i3)
                    norm_spread(pe, ln3, i3, mix_ps, ident)
                if 0 in live:
                    qk_products(i, range(KT, 2 * KT))
                if 1 in live:
                    pe.wait_ge(s["si"], i1 + 1)
                    for c in range(2 * KT):
                        a, g = c // KT, c % KT
                        for t in range(TT):
                            mm = pe.matmul(flow_ps[1][:, c * HG:(c + 1) * HG], tqks[:, r1, c, t * P:(t + 1) * P],
                                           sis[:, r1, a, t, g * HG:(g + 1) * HG], start=(t == 0), stop=(t == TT - 1))
                    mm.then_inc(s["s2"], 1)
                if 2 in live:
                    for g in range(KT):
                        pe.wait_ge(s["ot"], i2 * KT + g + 1)
                        for t in range(TT):
                            mm = pe.transpose(out_ps[g][:, t * P:(t + 1) * P], ot[:, t, g * P:(g + 1) * P], ident)
                        mm.then_inc(s["oT"], 1)
                if 0 in live:
                    v_products(i)
                if 1 in live:
                    pe.wait_ge(s["kd2"], i1 + 1)
                    flows(i1, kd2, "s3")
                if 3 in live:
                    pe.wait_ge(s["rl"], i3 + 1)
                    mix(i3, "Wr", rh, rl, "r_ps")
                if -1 in live:
                    norm_sums(pe, ln0, ja, sums0_ps, ones)
                if 3 in live:
                    pe.wait_ge(s["kl"], i3 + 1)
                    pe.wait_ge(s["rg"], i3 * KT + KT)
                    mix(i3, "Wk", kh, kl, "k_ps")
                if 2 in live:
                    pe.wait_ge(s["ol"], i2 * KT + KT)
                    for m in range(KT):
                        for k in range(KT):
                            mm = mm3(pe, out_ps[m][:, :], *wt("proj", D, k, m), oh[:, k, :], ol[:, k, :], k == 0, k == KT - 1)
                        mm.then_inc(s["proj"], 1)

            turns(pe, turn, lambda n: pe.wait_ge(s["w_lo"], n + 1))


def modulation(nc, sems, conds, wmods, mods, const):
    ident, ident16, ones, minus_half = const
    N = 6 * KT
    with ExitStack() as ctx:
        def sb(name, shape, dt=F32):
            return ctx.enter_context(nc.sbuf_tensor("m_" + name, shape, dt))

        def sem(name):
            sems.append(nc.alloc_semaphore("m_" + name))
            return sems[-1]

        c_sb = [sb(f"c{l}", [P, KT, NS]) for l in range(2)]
        w_sb = [sb(f"w{l}", [P, KT, 6 * D]) for l in range(2)]
        mag = sb("mag", [P, NS, KT])
        sign = sb("sign", [P, NS, KT])
        ps = [ctx.enter_context(nc.psum_tensor(f"m_bank{l}", [P, N * NS], F32)) for l in range(2)]
        loaded, silu, product, chain, const_ready = (sem(n) for n in ("loaded", "silu", "product", "chain", "const"))
        block = ctx.enter_context(nc.Block())

        @block.sync
        def _(sp_):
            for l in range(2):
                sp_.dma_start(c_sb[l][:, :, :], conds[l]).then_inc(loaded, 16)
                sp_.dma_start(w_sb[l][:, :, :], wmods[l]).then_inc(loaded, 16)

        @block.gpsimd
        def _(pool):
            pool.memset(ones[:, :], 1.0).then_inc(const_ready, 1)
            pool.memset(minus_half[:, :], -0.5).then_inc(const_ready, 1)
            pool.memset(ident[:, :], 0.0).then_inc(const_ready, 1)
            pool.memset(ident16[:, :], 0.0).then_inc(const_ready, 1)
            pool.wait_ge(const_ready, 4)
            for m in (ident, ident16):
                pool.affine_select(out=m[:, :], in_=m[:, :], compare_op=ALU.not_equal, fill=1.0, base=0, pattern=[[-1, P]],
                                   channel_multiplier=1).then_inc(const_ready, 1)

        @block.scalar
        def _(act):
            act.wait_ge(loaded, 64)
            for l in range(2):
                act.activation(c_sb[l][:, :, :], c_sb[l][:, :, :], ACT.Silu).then_inc(silu, 1)

        @block.tensor
        def _(pe):
            for l in range(2):
                pe.wait_ge(silu, l + 1)
                for n in range(N):
                    for k in range(KT):
                        mm = pe.matmul(ps[l][:, n * NS:(n + 1) * NS], w_sb[l][:, k, n * P:(n + 1) * P], c_sb[l][:, k, :],
                                       start=(k == 0), stop=(k == KT - 1))
                mm.then_inc(product, 1)

        @block.vector
        def _(dve):
            done = 0
            for l in range(2):
                dve.wait_ge(product, l + 1)
                dve.tensor_copy(mods[l][:, :, :].rearrange("p s n -> p n s"),
                                ps[l][:, :].rearrange("p (n s) -> p n s", s=NS)).then_inc(chain, 1)
                done += 1
                for row in (CA, CB):
                    dve.wait_ge(chain, done)
                    a = mods[l][:, :, row * KT:(row + 1) * KT]
                    dve.tensor_scalar(a, a, 1.0, None, ALU.add).then_inc(chain, 1)
                    done += 1
                for row in (GA, GB):
                    a = mods[l][:, :, row * KT:(row + 1) * KT]
                    dve.wait_ge(chain, done)
                    dve.scalar_tensor_tensor(out=mag[:, :, :], in0=a, scalar=-1.0, in1=a, op0=ALU.mult, op1=ALU.max).then_inc(chain, 1)
                    dve.tensor_scalar(sign[:, :, :], a, 0.0, 2.0, ALU.is_ge, ALU.mult).then_inc(chain, 1)
                    dve.wait_ge(chain, done + 2)
                    dve.tensor_scalar(mag[:, :, :], mag[:, :, :], GATE_MIN, None, ALU.max).then_inc(chain, 1)
                    dve.wait_ge(chain, done + 3)
                    dve.scalar_tensor_tensor(out=a, in0=sign[:, :, :], scalar=-1.0, in1=mag[:, :, :], op0=ALU.add,
                                             op1=ALU.mult).then_inc(chain, 1)
                    done += 4


def clear(nc, sems):
    nc.all_engine_barrier()
    nc.clear_and_free_semaphores(sems)
    nc.all_engine_barrier()
    sems.clear()


def program(nc, a, x_out):
    mid = nc.dram_tensor("mid", (NS, P, KT, T), F32, kind="Internal").ap()
    with ExitStack() as ctx:
        def sb(name, shape, dt=F32):
            return ctx.enter_context(nc.sbuf_tensor(name, shape, dt))

        ident_t, ident16_t, ones_t = sb("ident", [P, P]), sb("ident16", [P, P], BF16), sb("ones", [P, P])
        half_t = sb("minus_half", [P, TT])
        const = (ident_t[:, :], ident16_t[:, :], ones_t[:, :], half_t[:, :])
        mods = [sb(f"mod{l}", [P, NS, 6 * KT]) for l in range(2)]
        sems = []
        modulation(nc, sems, (a["c0"], a["c1"]), (a["wmod0"], a["wmod1"]), mods, const)
        clear(nc, sems)
        first_layer(nc, sems, a["x"], mid, a, mods[0], const)
        clear(nc, sems)
        second_layer(nc, sems, mid, x_out, a, mods[1], const)



def _rows_down(m):
    k, n = m.shape
    return np.ascontiguousarray(m.reshape(k // P, P, n).transpose(1, 0, 2).reshape(P, -1))


def _vec(v):
    return np.ascontiguousarray(np.asarray(v).reshape(-1, P).T)


def kernel(**inputs):
    import concourse.bacc as _bacc
    from concourse.bass_utils import run_bass_kernel_spmd as _run

    g = {k: np.asarray(v) for k, v in inputs.items()}
    experts_in = lambda m: m.reshape(E * R, -1).T
    experts_out = lambda m: m.transpose(0, 2, 1).reshape(E * R, -1)
    x = g["L0_attn_x"].transpose(0, 2, 1).reshape(NS, KT, P, T).transpose(0, 2, 1, 3)
    host = {
        "x": np.ascontiguousarray(x),
        "c0": _rows_down(g["L0_c"].T).reshape(P, KT, NS),
        "c1": _rows_down(g["L1_c"].T).reshape(P, KT, NS),
        "wmod0": _rows_down(g["L0_wmod"]).reshape(P, KT, 6 * D),
        "wmod1": _rows_down(g["L1_wmod"]).reshape(P, KT, 6 * D),
        "W1": _rows_down(g["L0_attn_W1"].T),
        "b1": _vec(g["L0_attn_b1"]),
        "w2": _vec(g["L0_attn_w2"]),
        "b2": np.ascontiguousarray(np.broadcast_to(g["L0_attn_b2"].reshape(1, 1), (P, 1))),
        "Wc": _rows_down(g["L0_attn_Wc"].T),
        "bc": _vec(g["L0_attn_bc"]),
        "gate_w": _rows_down(g["L0_ffn_gate_w"].T).reshape(P, KT, E),
        "Wg": _rows_down(g["L0_ffn_w_gate"].T),
        "Wu": _rows_down(g["L0_ffn_w_up"].T),
        "Wd": _rows_down(g["L0_ffn_w_down"].T),
        "A1": _rows_down(experts_in(g["L0_ffn_A1"])),
        "A3": _rows_down(experts_in(g["L0_ffn_A3"])),
        "A2": _rows_down(experts_in(g["L0_ffn_A2"])),
        "B1": _rows_down(experts_out(g["L0_ffn_B1"])),
        "B3": _rows_down(experts_out(g["L0_ffn_B3"])),
        "B2": _rows_down(experts_out(g["L0_ffn_B2"])),
        "qkv": _rows_down(g["L1_attn_qkv_w"].T),
        "qk_bias": _vec(g["L1_attn_qkv_b"][:2 * D]),
        "v_bias": np.ascontiguousarray(g["L1_attn_qkv_b"][2 * D:].reshape(1, D)),
        "proj": _rows_down(g["L1_attn_proj_w"].T),
        "proj_bias": _vec(g["L1_attn_proj_b"]),
        "Wr": _rows_down(g["L1_ffn_W_r"].T),
        "Wk": _rows_down(g["L1_ffn_W_k"].T),
        "Wv": _rows_down(g["L1_ffn_W_v"].T),
        "mu_r": _vec(g["L1_ffn_mu_r"]),
        "mu_k": _vec(g["L1_ffn_mu_k"]),
    }
    nc = _bacc.Bacc("TRN2", target_bir_lowering=False, num_devices=1)
    args = {n: nc.dram_tensor("in_" + n, a.shape, mybir.dt.from_np(a.dtype), kind="ExternalInput").ap()
            for n, a in host.items()}
    out = nc.dram_tensor("out", (NS, P, KT, T), F32, kind="ExternalOutput").ap()
    program(nc, args, out)
    r = _run(nc, [{"in_" + n: a for n, a in host.items()}], core_ids=[0])
    y = np.asarray(r.results[0]["out"])
    return np.ascontiguousarray(y.transpose(0, 2, 1, 3).reshape(NS, D, T).transpose(0, 2, 1))
```
